# Optimizing a Trainium2 kernel written in Bass

```python
import numpy as np
import jax
import jax.numpy as jnp

def _softmax(x, axis=-1):
    return jax.nn.softmax(x, axis=axis)

def _gelu(x):
    return jax.nn.gelu(x, approximate=True)

def _silu(x):
    return jax.nn.silu(x)

def _sigmoid(x):
    return jax.nn.sigmoid(x)

def _layernorm(x, axis=-1, eps=1e-05):
    m = jnp.mean(x, axis=axis, keepdims=True)
    v = jnp.var(x, axis=axis, keepdims=True)
    return (x - m) / jnp.sqrt(v + eps)

def _scatter_add(tgt, idx, src, axis=0):
    return tgt.at[idx].add(src)

def _segment_sum(src, seg, n):
    return jax.ops.segment_sum(src, seg, n)
kernel_name = 'mk_recurrent_d2_jaxref_r4_faf24f'

def setup_inputs(seed: int=0):
    np.random.seed(seed)
    _w = jnp.asarray

    def _L0_attn_setup():
        import jax, jax.numpy as jnp
        import numpy as np
        DIM = 256
        HEADS = 16
        HEAD_DIM = DIM // HEADS
        ROPE_BASE = 500000.0
        SCALE = HEAD_DIM ** (-0.5)

        def _rope_cos_sin(T, dtype=jnp.float32):
            inv_freq = 1.0 / ROPE_BASE ** (jnp.arange(0, HEAD_DIM, 2, dtype=jnp.float32) / HEAD_DIM)
            t = jnp.arange(T, dtype=jnp.float32)
            freqs = t[:, None] * inv_freq[None, :]
            emb = jnp.concatenate([freqs, freqs], axis=-1)
            return (jnp.cos(emb).astype(dtype), jnp.sin(emb).astype(dtype))

        def _rotate_half(x):
            x1, x2 = jnp.split(x, 2, axis=-1)
            return jnp.concatenate([-x2, x1], axis=-1)

        def _apply_rope(x, cos, sin):
            return x * cos + _rotate_half(x) * sin
        key = jax.random.key(seed)
        k1, k2, k3 = jax.random.split(key, 3)
        B, T = (4, 1024)
        x = jax.random.normal(k1, (B, T, DIM), dtype=jnp.float32)
        W_qkv = jax.random.normal(k2, (DIM, 3 * DIM), dtype=jnp.float32) * DIM ** (-0.5)
        W_out = jax.random.normal(k3, (DIM, DIM), dtype=jnp.float32) * DIM ** (-0.5)
        return {'x': x, 'W_qkv': W_qkv, 'W_out': W_out}
    _L0_attn_in = _L0_attn_setup()

    def _L0_ffn_setup():
        import jax, jax.numpy as jnp
        import numpy as np
        import math
        B, T, D, H, E, TOPK, CAPF = (4, 512, 256, 16, 8, 2, 2.0)
        HD = D // H

        def layernorm(x, g, b, eps=1e-05):
            m = jnp.mean(x, -1, keepdims=True)
            v = jnp.mean(jnp.square(x - m), -1, keepdims=True)
            return (x - m) * jax.lax.rsqrt(v + eps) * g + b

        def block_forward(x, ln1_g, ln1_b, Wqkv, Wproj, ln2_g, ln2_b, Wgate, W1, b1, W2, b2):
            Bb, Tt, d = x.shape
            hd = HD
            half = hd // 2
            h = layernorm(x, ln1_g, ln1_b)
            qkv = (h @ Wqkv).reshape(Bb, Tt, H, 3 * hd)
            q, k, v = (qkv[..., :hd], qkv[..., hd:2 * hd], qkv[..., 2 * hd:])
            inv_freq = 1.0 / 10000.0 ** (jnp.arange(0, hd, 2, dtype=jnp.float32) / hd)
            ang = jnp.arange(Tt, dtype=jnp.float32)[:, None] * inv_freq
            sin = jnp.sin(ang)[None, :, None, :].astype(x.dtype)
            cos = jnp.cos(ang)[None, :, None, :].astype(x.dtype)

            def rope(t):
                t1, t2 = (t[..., :half], t[..., half:])
                return jnp.concatenate([t1 * cos - t2 * sin, t1 * sin + t2 * cos], -1)
            q, k = (rope(q), rope(k))
            scores = jnp.einsum('bqhd,bkhd->bhqk', q, k) / math.sqrt(hd)
            causal = jnp.tril(jnp.ones((Tt, Tt), dtype=bool))
            scores = jnp.where(causal, scores, jnp.asarray(-1000000000.0, scores.dtype))
            probs = jax.nn.softmax(scores, axis=-1)
            attn = jnp.einsum('bhqk,bkhd->bqhd', probs, v).reshape(Bb, Tt, d) @ Wproj
            x = x + attn
            h2 = layernorm(x, ln2_g, ln2_b)
            flat = h2.reshape(-1, d)
            N = flat.shape[0]
            capacity = int(math.ceil(CAPF * N / E))
            gates = jax.nn.softmax((flat @ Wgate).astype(jnp.float32), -1).astype(flat.dtype)
            _, top_inds = jax.lax.top_k(gates, TOPK)
            mask = jnp.zeros((N, E), dtype=bool).at[jnp.arange(N)[:, None], top_inds].set(True)
            pos = jnp.cumsum(mask.astype(jnp.int32), axis=0) * mask - 1
            keep = (pos < capacity) & mask
            t_flat = jnp.repeat(jnp.arange(N), TOPK)
            e_flat = top_inds.reshape(-1)
            p = pos[t_flat, e_flat]
            kp = keep[t_flat, e_flat]
            p_eff = jnp.where(kp, p, capacity)
            exp_in = jnp.zeros((E, capacity, d), flat.dtype).at[e_flat, p_eff].set(flat[t_flat], mode='drop')
            hmid = jax.nn.gelu(jnp.einsum('ecd,edf->ecf', exp_in, W1) + b1[:, None, :], approximate=False)
            exp_out = jnp.einsum('ecf,efd->ecd', hmid, W2) + b2[:, None, :]
            gate = gates[t_flat, e_flat] * kp.astype(flat.dtype)
            p_g = jnp.minimum(p_eff, capacity - 1)
            moe = jnp.zeros((N, d), flat.dtype).at[t_flat].add(exp_out[e_flat, p_g] * gate[:, None])
            return x + moe.reshape(Bb, Tt, d)
        key = jax.random.key(seed)
        ks = jax.random.split(key, 8)
        s = 0.02
        return {'x': jax.random.normal(ks[0], (B, T, D), jnp.float32), 'ln1_g': jnp.ones((D,), jnp.float32), 'ln1_b': jnp.zeros((D,), jnp.float32), 'Wqkv': jax.random.normal(ks[1], (D, 3 * D), jnp.float32) * s, 'Wproj': jax.random.normal(ks[2], (D, D), jnp.float32) * s, 'ln2_g': jnp.ones((D,), jnp.float32), 'ln2_b': jnp.zeros((D,), jnp.float32), 'Wgate': jax.random.normal(ks[3], (D, E), jnp.float32) * s, 'W1': jax.random.normal(ks[4], (E, D, 4 * D), jnp.float32) * s, 'b1': jnp.zeros((E, 4 * D), jnp.float32), 'W2': jax.random.normal(ks[5], (E, 4 * D, D), jnp.float32) * s, 'b2': jnp.zeros((E, D), jnp.float32)}
    _L0_ffn_in = _L0_ffn_setup()

    def _L1_attn_setup():
        import jax, jax.numpy as jnp
        import numpy as np
        NUM_HEADS = 16
        key = jax.random.key(seed)
        ks = jax.random.split(key, 5)
        B, N, C = (2, 512, 256)
        x = jax.random.normal(ks[0], (B, N, C), dtype=jnp.float32)
        s_in = 1.0 / np.sqrt(C)
        Wq = jax.random.normal(ks[1], (C, 2 * C), dtype=jnp.float32) * s_in
        Wk = jax.random.normal(ks[2], (C, 2 * C), dtype=jnp.float32) * s_in
        Wv = jax.random.normal(ks[3], (C, 2 * C), dtype=jnp.float32) * s_in
        Wo = jax.random.normal(ks[4], (2 * C, C), dtype=jnp.float32) * (1.0 / np.sqrt(2 * C))
        return {'x': x, 'Wq': Wq, 'Wk': Wk, 'Wv': Wv, 'Wo': Wo}
    _L1_attn_in = _L1_attn_setup()

    def _L1_ffn_setup():
        import jax, jax.numpy as jnp
        import numpy as np
        INT4_QMAX = 7.0

        def simulate_quantize_int4(w):
            scale = jnp.max(jnp.abs(w)) / INT4_QMAX
            q = jnp.clip(jnp.round(w / scale), -8.0, 7.0)
            return q * scale
        key = jax.random.key(seed)
        k_x, k_w, k_bias, k_a, k_b = jax.random.split(key, 5)
        d_in, features, rank = (256, 256, 16)
        x = jax.random.normal(k_x, (4, 2048, d_in), dtype=jnp.float32)
        kernel = jax.random.normal(k_w, (d_in, features), dtype=jnp.float32)
        bias = jax.random.normal(k_bias, (features,), dtype=jnp.float32)
        a = jax.random.normal(k_a, (d_in, rank), dtype=jnp.float32) * (1.0 / np.sqrt(d_in))
        b = jax.random.normal(k_b, (rank, features), dtype=jnp.float32) * 0.01
        return {'x': x, 'kernel': kernel, 'bias': bias, 'a': a, 'b': b}
    _L1_ffn_in = _L1_ffn_setup()
    _d = {'L0_attn_x': _L0_attn_in['x'], 'L0_attn_W_qkv': _L0_attn_in['W_qkv'], 'L0_attn_W_out': _L0_attn_in['W_out'], 'L0_ffn_ln1_g': _L0_ffn_in['ln1_g'], 'L0_ffn_ln1_b': _L0_ffn_in['ln1_b'], 'L0_ffn_Wqkv': _L0_ffn_in['Wqkv'], 'L0_ffn_Wproj': _L0_ffn_in['Wproj'], 'L0_ffn_ln2_g': _L0_ffn_in['ln2_g'], 'L0_ffn_ln2_b': _L0_ffn_in['ln2_b'], 'L0_ffn_Wgate': _L0_ffn_in['Wgate'], 'L0_ffn_W1': _L0_ffn_in['W1'], 'L0_ffn_b1': _L0_ffn_in['b1'], 'L0_ffn_W2': _L0_ffn_in['W2'], 'L0_ffn_b2': _L0_ffn_in['b2'], 'L1_attn_Wq': _L1_attn_in['Wq'], 'L1_attn_Wk': _L1_attn_in['Wk'], 'L1_attn_Wv': _L1_attn_in['Wv'], 'L1_attn_Wo': _L1_attn_in['Wo'], 'L1_ffn_kernel': _L1_ffn_in['kernel'], 'L1_ffn_bias': _L1_ffn_in['bias'], 'L1_ffn_a': _L1_ffn_in['a'], 'L1_ffn_b': _L1_ffn_in['b']}
    _x0 = _d['L0_attn_x']
    _d['L0_attn_x'] = jax.random.normal(jax.random.fold_in(jax.random.key(seed), 1), (2, 2048, 256), dtype=_x0.dtype)
    del _x0
    return _d

def reference(L0_attn_x, L0_attn_W_qkv, L0_attn_W_out, L0_ffn_ln1_g, L0_ffn_ln1_b, L0_ffn_Wqkv, L0_ffn_Wproj, L0_ffn_ln2_g, L0_ffn_ln2_b, L0_ffn_Wgate, L0_ffn_W1, L0_ffn_b1, L0_ffn_W2, L0_ffn_b2, L1_attn_Wq, L1_attn_Wk, L1_attn_Wv, L1_attn_Wo, L1_ffn_kernel, L1_ffn_bias, L1_ffn_a, L1_ffn_b):

    def _L0_attn_ref(x, W_qkv, W_out):
        import jax, jax.numpy as jnp
        import numpy as np
        DIM = 256
        HEADS = 16
        HEAD_DIM = DIM // HEADS
        ROPE_BASE = 500000.0
        SCALE = HEAD_DIM ** (-0.5)

        def _rope_cos_sin(T, dtype=jnp.float32):
            inv_freq = 1.0 / ROPE_BASE ** (jnp.arange(0, HEAD_DIM, 2, dtype=jnp.float32) / HEAD_DIM)
            t = jnp.arange(T, dtype=jnp.float32)
            freqs = t[:, None] * inv_freq[None, :]
            emb = jnp.concatenate([freqs, freqs], axis=-1)
            return (jnp.cos(emb).astype(dtype), jnp.sin(emb).astype(dtype))

        def _rotate_half(x):
            x1, x2 = jnp.split(x, 2, axis=-1)
            return jnp.concatenate([-x2, x1], axis=-1)

        def _apply_rope(x, cos, sin):
            return x * cos + _rotate_half(x) * sin
        B, T, D = x.shape
        H, hd = (HEADS, HEAD_DIM)
        qkv = (x @ W_qkv).reshape(B, T, 3, H, hd).transpose(2, 0, 3, 1, 4)
        q, k, v = (qkv[0], qkv[1], qkv[2])
        cos, sin = _rope_cos_sin(T, q.dtype)
        q = _apply_rope(q, cos, sin)
        k = _apply_rope(k, cos, sin)
        q_feat = jax.nn.elu(q * SCALE) + 1.0
        k_feat = jax.nn.elu(k) + 1.0
        kv = jnp.einsum('bhtd,bhtv->bhdv', k_feat, v)
        k_sum = k_feat.sum(axis=2)
        denom = jnp.maximum(jnp.einsum('bhtd,bhd->bht', q_feat, k_sum), 1e-06)
        out = jnp.einsum('bhtd,bhdv->bhtv', q_feat, kv) / denom[..., None]
        out = out.transpose(0, 2, 1, 3).reshape(B, T, D)
        return out @ W_out

    def _L0_ffn_ref(x, ln1_g, ln1_b, Wqkv, Wproj, ln2_g, ln2_b, Wgate, W1, b1, W2, b2):
        import jax, jax.numpy as jnp
        import numpy as np
        import math
        B, T, D, H, E, TOPK, CAPF = (4, 512, 256, 16, 8, 2, 2.0)
        HD = D // H

        def layernorm(x, g, b, eps=1e-05):
            m = jnp.mean(x, -1, keepdims=True)
            v = jnp.mean(jnp.square(x - m), -1, keepdims=True)
            return (x - m) * jax.lax.rsqrt(v + eps) * g + b

        def block_forward(x, ln1_g, ln1_b, Wqkv, Wproj, ln2_g, ln2_b, Wgate, W1, b1, W2, b2):
            Bb, Tt, d = x.shape
            hd = HD
            half = hd // 2
            h = layernorm(x, ln1_g, ln1_b)
            qkv = (h @ Wqkv).reshape(Bb, Tt, H, 3 * hd)
            q, k, v = (qkv[..., :hd], qkv[..., hd:2 * hd], qkv[..., 2 * hd:])
            inv_freq = 1.0 / 10000.0 ** (jnp.arange(0, hd, 2, dtype=jnp.float32) / hd)
            ang = jnp.arange(Tt, dtype=jnp.float32)[:, None] * inv_freq
            sin = jnp.sin(ang)[None, :, None, :].astype(x.dtype)
            cos = jnp.cos(ang)[None, :, None, :].astype(x.dtype)

            def rope(t):
                t1, t2 = (t[..., :half], t[..., half:])
                return jnp.concatenate([t1 * cos - t2 * sin, t1 * sin + t2 * cos], -1)
            q, k = (rope(q), rope(k))
            scores = jnp.einsum('bqhd,bkhd->bhqk', q, k) / math.sqrt(hd)
            causal = jnp.tril(jnp.ones((Tt, Tt), dtype=bool))
            scores = jnp.where(causal, scores, jnp.asarray(-1000000000.0, scores.dtype))
            probs = jax.nn.softmax(scores, axis=-1)
            attn = jnp.einsum('bhqk,bkhd->bqhd', probs, v).reshape(Bb, Tt, d) @ Wproj
            x = x + attn
            h2 = layernorm(x, ln2_g, ln2_b)
            flat = h2.reshape(-1, d)
            N = flat.shape[0]
            capacity = int(math.ceil(CAPF * N / E))
            gates = jax.nn.softmax((flat @ Wgate).astype(jnp.float32), -1).astype(flat.dtype)
            _, top_inds = jax.lax.top_k(gates, TOPK)
            mask = jnp.zeros((N, E), dtype=bool).at[jnp.arange(N)[:, None], top_inds].set(True)
            pos = jnp.cumsum(mask.astype(jnp.int32), axis=0) * mask - 1
            keep = (pos < capacity) & mask
            t_flat = jnp.repeat(jnp.arange(N), TOPK)
            e_flat = top_inds.reshape(-1)
            p = pos[t_flat, e_flat]
            kp = keep[t_flat, e_flat]
            p_eff = jnp.where(kp, p, capacity)
            exp_in = jnp.zeros((E, capacity, d), flat.dtype).at[e_flat, p_eff].set(flat[t_flat], mode='drop')
            hmid = jax.nn.gelu(jnp.einsum('ecd,edf->ecf', exp_in, W1) + b1[:, None, :], approximate=False)
            exp_out = jnp.einsum('ecf,efd->ecd', hmid, W2) + b2[:, None, :]
            gate = gates[t_flat, e_flat] * kp.astype(flat.dtype)
            p_g = jnp.minimum(p_eff, capacity - 1)
            moe = jnp.zeros((N, d), flat.dtype).at[t_flat].add(exp_out[e_flat, p_g] * gate[:, None])
            return x + moe.reshape(Bb, Tt, d)
        return block_forward(x, ln1_g, ln1_b, Wqkv, Wproj, ln2_g, ln2_b, Wgate, W1, b1, W2, b2)

    def _L1_attn_ref(x, Wq, Wk, Wv, Wo):
        import jax, jax.numpy as jnp
        import numpy as np
        NUM_HEADS = 16
        B, N, C = x.shape
        H = NUM_HEADS
        hd = C // H

        def proj(W):
            return (x @ W).reshape(B, N, H, 2 * hd).transpose(0, 2, 1, 3)
        q = proj(Wq)
        k = proj(Wk)
        v = proj(Wv)
        q_r, q_i = (q[..., :hd], q[..., hd:])
        k_r, k_i = (k[..., :hd], k[..., hd:])
        v_r, v_i = (v[..., :hd], v[..., hd:])
        scores = (jnp.einsum('bhnd,bhmd->bhnm', q_r, k_r) + jnp.einsum('bhnd,bhmd->bhnm', q_i, k_i)) / jnp.sqrt(jnp.float32(hd))
        causal = jnp.tril(jnp.ones((N, N), dtype=bool))
        scores = jnp.where(causal[None, None], scores, -jnp.inf)
        probs = jax.nn.softmax(scores, axis=-1)
        out_r = jnp.einsum('bhnm,bhmd->bhnd', probs, v_r)
        out_i = jnp.einsum('bhnm,bhmd->bhnd', probs, v_i)
        out = jnp.concatenate([out_r, out_i], axis=-1)
        out = out.transpose(0, 2, 1, 3).reshape(B, N, 2 * C)
        return out @ Wo

    def _L1_ffn_ref(x, kernel, bias, a, b):
        import jax, jax.numpy as jnp
        import numpy as np
        INT4_QMAX = 7.0

        def simulate_quantize_int4(w):
            scale = jnp.max(jnp.abs(w)) / INT4_QMAX
            q = jnp.clip(jnp.round(w / scale), -8.0, 7.0)
            return q * scale
        w = simulate_quantize_int4(kernel)
        y = jnp.einsum('bsd,df->bsf', x, w) + bias
        lora = jnp.einsum('bsr,rf->bsf', jnp.einsum('bsd,dr->bsr', x, a), b)
        return y + lora
    x = L0_attn_x
    xn = _layernorm(x, axis=-1)
    s = _L0_attn_ref(xn, L0_attn_W_qkv, L0_attn_W_out)
    g = _silu(_L0_ffn_ref(xn, L0_ffn_ln1_g, L0_ffn_ln1_b, L0_ffn_Wqkv, L0_ffn_Wproj, L0_ffn_ln2_g, L0_ffn_ln2_b, L0_ffn_Wgate, L0_ffn_W1, L0_ffn_b1, L0_ffn_W2, L0_ffn_b2))
    x = x + s * g
    xn = _layernorm(x, axis=-1)
    s = _L1_attn_ref(xn, L1_attn_Wq, L1_attn_Wk, L1_attn_Wv, L1_attn_Wo)
    g = _silu(_L1_ffn_ref(xn, L1_ffn_kernel, L1_ffn_bias, L1_ffn_a, L1_ffn_b))
    x = x + s * g
    return x

_drawn_inputs = setup_inputs


def setup_inputs(seed=0):
    import zlib

    import numpy as np

    out = dict(_drawn_inputs(seed))
    spreads = {'L0_ffn_ln1_g': (1.0, 0.6),
     'L0_ffn_ln1_b': (0.0, 0.8),
     'L0_ffn_ln2_g': (1.0, 0.6),
     'L0_ffn_ln2_b': (0.0, 0.8),
     'L0_ffn_b1': (0.0, 0.8),
     'L0_ffn_b2': (0.0, 2.0)}
    factors = {'L0_ffn_Wqkv': 8.0,
     'L0_ffn_Wproj': 8.0,
     'L0_ffn_Wgate': 8.0,
     'L0_ffn_W1': 8.0,
     'L0_ffn_W2': 8.0,
     'L1_ffn_a': 8.0,
     'L1_ffn_b': 8.0}
    for name, (base, spread) in spreads.items():
        noise = np.random.default_rng([zlib.crc32(name.encode()), seed]).standard_normal(out[name].shape)
        drawn = base * np.exp(spread * noise) if base else spread * noise
        out[name] = jnp.asarray(drawn.astype(out[name].dtype))
    for name, factor in factors.items():
        out[name] = (out[name] * factor).astype(out[name].dtype)
    return out
```

```python
import concourse.bass as bass
from concourse import mybir
from contextlib import ExitStack

F32 = mybir.dt.float32
F16 = mybir.dt.float16
BF16 = mybir.dt.bfloat16
U32 = mybir.dt.uint32
I32 = mybir.dt.int32
ALU = mybir.AluOpType
ACT = mybir.ActivationFunctionType
AX = mybir.AxisListType

P = 128
B, T, D, H = 2, 2048, 256, 16
GROUPS = 8
HG = 4
QB = 512
NQB = T // QB
NKC = T // P
MROW = 96
NROW = MROW + 2 * HG
MSHIFT = 2.0 ** 15


class Ctx:

    def __init__(self, nc, tag):
        self.nc, self.tag, self.stack = nc, tag, ExitStack()

    def __enter__(self):
        self.stack.__enter__()
        return self

    def __exit__(self, *a):
        return self.stack.__exit__(*a)

    def sb(self, name, shape, dt):
        return self.stack.enter_context(self.nc.sbuf_tensor(f"{self.tag}_{name}", shape, dt))

    def ps(self, name, shape, dt=F32):
        return self.stack.enter_context(self.nc.psum_tensor(f"{self.tag}_{name}", shape, dt))

    def sem(self, name):
        return self.stack.enter_context(self.nc.semaphore(f"{self.tag}_{name}"))

    def block(self):
        return self.stack.enter_context(self.nc.Block())


def attention_schedule(sums_apart, ahead_share=0.02, behind_share=0.0, s_slots=2):
    order = [3, 2, 1, 0]

    def pass1(g, u):
        items = []
        for qt in range(4):
            for h in range(HG):
                for j in range(u + 1):
                    width = QB if j < u else (qt + 1) * P
                    items.append(("S", (g, u), qt, h, j, width))
        return items

    def stream(units):
        out, late = [], None
        for g, u in units:
            for n, it in enumerate(pass1(g, u)):
                out.append(it)
                if late and n == 3:
                    out.append(("T", late))
                    late = None
            out.append(("M", (g, u)))
            late = (g, u)
        out.append(("T", late))
        return out

    prologue = stream([(0, order[0])])
    ahead = stream([(0, u) for u in order[1:]] + [(1, u) for u in order] + [(2, order[0])])
    steps = [((g, u), kc) for g in range(2) for u in order for kc in range(4 * u + 4)]
    width2 = lambda s: QB - max(0, s[1] - 4 * s[0][1]) * P
    pairs = [(s, pair) for s in steps for pair in range(2)]

    LATENCY, COLUMN = 180, 0.417
    pe_time = {"S": lambda ev: ev[5] * COLUMN + (50 if ev[4] == ev[1][1] else 0),
               "T": lambda ev: 100}
    dve_time = {"S": lambda ev: ev[5] * 1.04 + 65, "T": lambda ev: 1250, "M": lambda ev: 400}
    cost1 = lambda ev: dve_time[ev[0]](ev)
    total1, total2 = sum(map(cost1, ahead)), sum(map(width2, steps)) * 2
    done1 = done2 = 0
    pe = dve = act = 0.0
    slot_free = [0.0] * s_slots
    st_free = [0.0, 0.0]
    exp_end, pv_end, ended, row_at = [], [], {}, {(0, order[0]): 0.0}
    at = n_slot = n_pair = n_quad = 0
    made = 0.0
    body = []
    ring = 3
    while at < len(ahead) or n_pair < len(pairs) or n_quad < len(steps):
        choice = []
        if at < len(ahead):
            ready = slot_free[n_slot % s_slots] + LATENCY
            if ahead[at][0] == "T":
                ready = max(ready, made + LATENCY)
            if n_pair == len(pairs) or done1 / total1 <= done2 / total2 + ahead_share:
                patience = 600 if done1 / total1 < done2 / total2 + behind_share else 0
                choice.append((max(pe, ready) - patience, 0, "S", max(pe, ready)))
        if n_pair < len(pairs):
            s, pair = pairs[n_pair]
            if s[0] in row_at:
                quad = n_pair // 2
                ready = max(st_free[n_pair % 2], row_at[s[0]]) + LATENCY
                if quad - n_quad < 2:
                    choice.append((max(pe, ready), 1, "ST", max(pe, ready)))
            elif not any(c[2] == "S" for c in choice):
                ready = max(pe, slot_free[n_slot % s_slots] + LATENCY)
                choice.append((ready, 0, "S", ready))
        if n_quad < len(steps) and 2 * n_quad + 1 < n_pair:
            ready = exp_end[2 * n_quad + 1] + LATENCY
            choice.append((max(pe, ready), 2, "PV", max(pe, ready)))
        _, _, kind, start = min(choice)
        if kind == "S":
            ev = ahead[at]
            at += 1
            body.append(ev)
            done1 += cost1(ev)
            pe = start + pe_time[ev[0]](ev)
            dve = max(dve, pe + LATENCY) + dve_time[ev[0]](ev)
            slot_free[n_slot % s_slots] = dve
            n_slot += 1
            if ev[0] == "T":
                row_at[ev[1]] = dve
            if at < len(ahead) and ahead[at][0] == "M":
                body.append(ahead[at])
                dve += dve_time["M"](ahead[at])
                done1 += cost1(ahead[at])
                made = dve
                at += 1
        elif kind == "ST":
            s, pair = pairs[n_pair]
            w = width2(s)
            body.append(("ST",) + s + (pair,))
            pe = start + 2 * w * COLUMN + (100 if s[1] >= 4 * s[0][1] else 0)
            needs = pv_end[n_pair // 2 - ring] if n_pair // 2 >= ring else 0.0
            act = max(act, pe + LATENCY, needs + LATENCY) + 2 * w * 0.83 + 150
            st_free[n_pair % 2] = act
            exp_end.append(act)
            n_pair += 1
            done2 += w
        else:
            s = steps[n_quad]
            body.append(("PV",) + s)
            pe = start + (width2(s) * COLUMN * 4 + 80) * (2 if sums_apart else 1)
            pv_end.append(pe)
            n_quad += 1
            if s[1] == 4 * s[0][1] + 3:
                body.append(("EV", s[0]))
                act += 1300 if sums_apart else 650
    return prologue, body


def softmax_attention(nc, tag, hd, C, q_hi, q_lo, k_hi, k_lo, v, scale, out, sums):
    sums_apart = hd == 32
    prologue, body = attention_schedule(sums_apart)
    n_items = sum(e[0] in ("S", "T") for e in body)
    p_items = sum(e[0] in ("S", "T") for e in prologue)
    n_pairs = sum(e[0] == "ST" for e in body)
    n_quads = sum(e[0] == "PV" for e in body)
    n_acc = 1 if sums_apart else 2
    stores = 32 if sums_apart else 16
    LOADS = 7 * 16
    last_unit_of_group = (3, 2, 1, 0)[-1]

    with Ctx(nc, tag) as c:
        QT = [c.sb(f"qT{k}", [P, HG, T], F16) for k in range(2)]
        KT = [c.sb(f"kT{k}", [P, HG, T], F16) for k in range(2)]
        V = [c.sb(f"v{k}", [P, NKC, HG * 32], F32) for k in range(2)]
        NP_RING = 6
        probs = c.sb("probs", [P, NP_RING, 2, QB], F32)
        part = c.sb("part", [P, 2, 4 * HG, NQB], F32)
        rowmax = c.sb("rowmax", [P, 2, 4 * HG], F32)
        shift = c.sb("shift", [P, 2, 4 * HG, 2], F16)
        otile = c.sb("otile", [P, 2, QB], F32)
        stile = c.sb("stile", [P, 2, QB], F32) if sums_apart else None

        st_ps = [c.ps(f"st{k}", [P, 2, QB]) for k in range(2)]
        s_ps = [c.ps(f"s{k}", [P, QB]) for k in range(2)]
        acc_ps = [c.ps(f"acc{k}", [P, QB]) for k in range(2)]

        ld = [c.sem(f"ld{k}") for k in range(2)]
        init = c.sem("init")
        zeroed = [c.sem(f"zeroed{k}") for k in range(2)]
        item_ready = c.sem("item_ready")
        item_free = c.sem("item_free")
        max_done = c.sem("max_done")
        hi_done = c.sem("hi_done")
        shift_ready = c.sem("shift_ready")
        row_ready = c.sem("row_ready")
        st_ready = c.sem("st_ready")
        exp_done = c.sem("exp_done")
        pv_done = c.sem("pv_done")
        acc_ready = c.sem("acc_ready")
        out_ready = c.sem("out_ready")
        group_done = c.sem("group_done")
        stored = c.sem("stored")
        tile_free = c.sem("tile_free")
        block = c.block()

        def load(eng, g, k):
            rows = [(QT, q_hi, 0), (QT, q_lo, 1), (QT, q_hi, 2),
                    (KT, k_hi, 0), (KT, k_hi, 1), (KT, k_lo, 2)]
            for dst, src, r in rows:
                eng.dma_start(dst[k][r * hd:(r + 1) * hd, :, :],
                              src[g].rearrange("h d t -> d h t")).then_inc(ld[k], 16)
            eng.dma_start(V[k][:, :, :], v[g]).then_inc(ld[k], 16)

        @block.sync
        def _(sp):
            for k in range(2):
                sp.dma_start(KT[k][MROW:NROW, :, :], C["shift_rows"]).then_inc(init, 16)
            if hd == 16:
                sp.wait_ge(zeroed[0], 2)
            load(sp, 0, 0)
            if hd == 16:
                sp.wait_ge(zeroed[1], 2)
            with sp.Fori(0, GROUPS // 2) as i:
                sp.wait_ge(group_done, i * 2 + 1)
                load(sp, i * 2 + 1, 1)
                sp.wait_ge(group_done, i * 2 + 2)
                load(sp, (i * 2 + 2) % GROUPS, 0)
            sp.wait_ge(ld[0], LOADS * (GROUPS // 2 + 1))

        @block.gpsimd
        def _(pool):
            if hd == 16:
                for k in range(2):
                    pool.memset(KT[k][0:MROW, :, :].bitcast(U32), 0).then_inc(zeroed[k], 1)
            n = 0
            pool.nop().then_inc(tile_free, 2)
            with pool.Fori(0, GROUPS // 2) as i:
                for ev in body:
                    if ev[0] != "EV":
                        continue
                    g, u = ev[1]
                    pool.wait_ge(out_ready, i * 8 + n + 1 + n_acc)
                    pool.dma_start(out[i * 2 + g, :, u * QB:(u + 1) * QB],
                                   otile[:, n % 2, :]).then_inc(stored, 16)
                    if sums_apart:
                        pool.dma_start(sums[i * 2 + g, :, u * QB:(u + 1) * QB],
                                       stile[0:P:32, n % 2, :]).then_inc(stored, 16)
                    n += 1
                    pool.wait_ge(stored, (i * 8 + n) * stores)
                    pool.nop().then_inc(tile_free, 1)

        @block.scalar
        def _(act):
            act.nop().then_inc(exp_done, 2)
            act.nop().then_inc(out_ready, n_acc)
            with act.Fori(0, GROUPS // 2) as i:
                n, v2, ended = 0, 0, 0

                def take_sums():
                    act.wait_ge(acc_ready, i * 8 + v2 + 1)
                    act.wait_ge(tile_free, i * 8 + v2 + 1)
                    ins = act.activation(otile[:, v2 % 2, :], acc_ps[v2 % n_acc][:, :], ACT.Copy)
                    if sums_apart:
                        ins = act.activation(stile[:, v2 % 2, :], acc_ps[1][:, :], ACT.Copy)
                    ins.then_inc(out_ready, 1)

                for ev in body:
                    if ev[0] == "EV":
                        ended += 1
                    if ev[0] != "ST":
                        continue
                    _, (g, u), kc, pair = ev
                    off = max(0, kc - 4 * u) * P
                    act.wait_ge(pv_done, i * n_quads + n // 2 + 1)
                    act.wait_ge(st_ready, i * n_pairs + n + 1)
                    act.activation(probs[:, n % NP_RING, :, off:QB], st_ps[n % 2][:, :, off:QB],
                                   ACT.Exp, scale=scale).then_inc(exp_done, 1)
                    n += 1
                    if ended > v2:
                        take_sums()
                        v2 += 1
                take_sums()

        @block.vector
        def _(dve):
            if hd == 16:
                for k in range(2):
                    dve.memset(QT[k][0:MROW, :, :].bitcast(U32), 0).then_inc(zeroed[k], 1)
            dve.nop().then_inc(item_free, 2)

            def events(evs, ibase, item0, unit0):
                n, w, transposed = 0, 0, 0
                for ev in evs:
                    if ev[0] == "S":
                        _, (g, u), qt, h, j, width = ev
                        dve.wait_ge(item_ready, ibase(n_items) + item0 + n + 1)
                        dve.tensor_reduce(part[:, (unit0 + w) % 2, qt * HG + h, j:j + 1],
                                          s_ps[(item0 + n) % 2][:, 0:width], AX.X,
                                          ALU.max).then_inc(item_free, 1)
                        n += 1
                    elif ev[0] == "M":
                        g, u = ev[1]
                        b = (unit0 + w) % 2
                        dve.wait_ge(item_free, ibase(n_items) + item0 + n + 2)
                        dve.tensor_reduce(rowmax[:, b, :], part[:, b, :, 0:u + 1], AX.X,
                                          ALU.max).then_inc(max_done, 1)
                        dve.wait_ge(max_done, ibase(8) + unit0 + w + 1)
                        dve.tensor_scalar(shift[:, b, :, 0], rowmax[:, b, :], -1.0 / MSHIFT, None,
                                          ALU.mult).then_inc(hi_done, 1)
                        dve.wait_ge(hi_done, ibase(8) + unit0 + w + 1)
                        dve.scalar_tensor_tensor(out=shift[:, b, :, 1], in0=rowmax[:, b, :],
                                                 scalar=-1.0 / MSHIFT, in1=shift[:, b, :, 0],
                                                 op0=ALU.mult,
                                                 op1=ALU.subtract).then_inc(shift_ready, 1)
                        w += 1
                    elif ev[0] == "T":
                        g, u = ev[1]
                        dve.wait_ge(item_ready, ibase(n_items) + item0 + n + 1)
                        rows = s_ps[(item0 + n) % 2][MROW:NROW, 0:QB // 2].bitcast(F16)
                        dve.tensor_copy(QT[g % 2][MROW:NROW, :, u * QB:(u + 1) * QB],
                                        rows.unsqueeze(1).to_broadcast([2 * HG, HG, QB])
                                        ).then_inc(row_ready, 1)
                        dve.wait_ge(row_ready, ibase(8) + unit0 + transposed + 1)
                        dve.nop().then_inc(item_free, 1)
                        transposed += 1
                        n += 1
                return n, w

            n, w = events(prologue, lambda k: 0, 0, 0)
            with dve.Fori(0, GROUPS // 2) as i:
                events(body, lambda k: i * k, n, w)

        @block.tensor
        def _(pe):
            pe.nop().then_inc(pv_done, 3)
            pe.nop().then_inc(group_done, 1)

            def pass1(ev, n, it, wait_unit):
                slot = s_ps[n % 2]
                pe.wait_ge(item_free, it * n_items + n + 1)
                if ev[0] == "S":
                    _, (g, u), qt, h, j, width = ev
                    q0 = u * QB + qt * P
                    diagonal = j == u
                    mm = pe.matmul(slot[:, 0:width], QT[g % 2][0:MROW, h, q0:q0 + P],
                                   KT[g % 2][0:MROW, h, j * QB:j * QB + width],
                                   start=True, stop=not diagonal)
                    if diagonal:
                        mm = pe.matmul(slot[:, width - P:width], C["ident16"][:, :],
                                       C["mask_qk"][:, :], start=False, stop=True)
                    mm.then_inc(item_ready, 1)
                else:
                    pe.wait_ge(shift_ready, wait_unit + 1)
                    rows = slot[MROW:NROW, 0:QB // 2].bitcast(F16)
                    for qt in range(4):
                        mm = pe.transpose(rows[:, qt * P:(qt + 1) * P],
                                          shift[:, ev[2] % 2, qt * HG:(qt + 1) * HG, :]
                                          .rearrange("p h two -> p (h two)"),
                                          C["ident_f16"][:, :])
                    mm.then_inc(item_ready, 1)

            pe.wait_ge(C["const_ready"], C["const_count"])
            pe.wait_ge(init, 32)
            pe.wait_ge(ld[0], LOADS)
            n = 0
            for ev in prologue:
                if ev[0] == "M":
                    continue
                pass1(ev if ev[0] == "S" else ev + (0,), n, 0, 0)
                n += 1
            with pe.Fori(0, GROUPS // 2) as i:
                items, w1, pairs, quads, v2 = p_items, 1, 0, 0, 0
                loaded = {0}
                for ev in body:
                    if ev[0] in ("S", "T"):
                        g = ev[1][0]
                        if g not in loaded:
                            loaded.add(g)
                            pe.wait_ge(ld[g % 2], i * LOADS + LOADS * (1 if g == 1 else 2))
                        pass1(ev if ev[0] == "S" else ev + (w1,), items, i, i * 8 + w1)
                        w1 += ev[0] == "T"
                        items += 1
                    elif ev[0] == "ST":
                        _, (g, u), kc, pair = ev
                        if kc == 0 and pair == 0:
                            pe.wait_ge(row_ready, i * 8 + v2 + 1)
                            v2 += 1
                        off = max(0, kc - 4 * u) * P
                        diagonal = kc >= 4 * u
                        pe.wait_ge(exp_done, i * n_pairs + pairs + 1)
                        for hh in range(2):
                            h = 2 * pair + hh
                            slot = st_ps[pairs % 2]
                            mm = pe.matmul(slot[:, hh, off:QB],
                                           KT[g % 2][0:NROW, h, kc * P:(kc + 1) * P],
                                           QT[g % 2][0:NROW, h, u * QB + off:(u + 1) * QB],
                                           start=True, stop=not diagonal)
                            if diagonal:
                                mm = pe.matmul(slot[:, hh, off:off + P], C["ident16"][:, :],
                                               C["mask_kq"][:, :], start=False, stop=True)
                        mm.then_inc(st_ready, 1)
                        pairs += 1
                    elif ev[0] == "PV":
                        _, (g, u), kc = ev
                        unit = 4 * g + (3 - u)
                        off = max(0, kc - 4 * u) * P
                        last = kc == 4 * u + 3
                        a = unit % n_acc
                        if kc == 0:
                            pe.wait_ge(out_ready, i * 8 + unit + 1)
                        pe.wait_ge(exp_done, i * n_pairs + 2 * quads + 4)
                        for h in range(HG):
                            pr = probs[:, (2 * quads + h // 2) % NP_RING, h % 2, off:QB]
                            mm = pe.matmul(acc_ps[a][32 * h:32 * h + 32, off:QB],
                                           V[g % 2][:, kc, 32 * h:32 * h + 32], pr,
                                           start=kc == 0, stop=last)
                        if sums_apart:
                            for h in range(HG):
                                pr = probs[:, (2 * quads + h // 2) % NP_RING, h % 2, off:QB]
                                mm = pe.matmul(acc_ps[1][32 * h:32 * h + 32, off:QB],
                                               C["ones32"][:, :], pr, start=kc == 0, stop=last)
                        mm.then_inc(pv_done, 1)
                        quads += 1
                        if last:
                            pe.wait_ge(pv_done, i * n_quads + quads + 3)
                            pe.nop().then_inc(acc_ready, 1)
                            if u == last_unit_of_group:
                                pe.nop().then_inc(group_done, 1)


def constants(nc, c, shift_rows):
    C = {"ident16": c.sb("ident16", [P, P], BF16), "ident_f16": c.sb("ident_f16", [P, P], F16),
         "identf": c.sb("identf", [P, P], F32), "mask_qk": c.sb("mask_qk", [P, P], BF16),
         "mask_kq": c.sb("mask_kq", [P, P], BF16), "ones32": c.sb("ones32", [P, 32], F32), "onesf": c.sb("onesf", [P, P], F32),
         "ones16": c.sb("ones16", [P, P], BF16), "tri16": c.sb("tri16", [P, P], BF16),
         "w_ffn": c.sb("w_ffn", [P, NF, D], F32),
         "shift_rows": shift_rows, "const_ready": c.sem("const_ready")}
    MASK = -1.0e30
    with nc.Block() as block:
        @block.gpsimd
        def _(pool):
            for k in ("ident16", "ident_f16", "identf", "mask_qk", "mask_kq"):
                pool.memset(C[k][:, :], 0.0).then_inc(C["const_ready"], 1)
            for k in ("ones32", "onesf", "ones16", "tri16"):
                pool.memset(C[k][:, :], 1.0).then_inc(C["const_ready"], 1)
            pool.wait_ge(C["const_ready"], 9)
            pool.affine_select(out=C["tri16"][:, :], in_=C["tri16"][:, :], compare_op=ALU.is_ge,
                               fill=0.0, base=0, pattern=[[1, P]],
                               channel_multiplier=-1).then_inc(C["const_ready"], 1)
            for k in ("ident16", "ident_f16", "identf"):
                pool.affine_select(out=C[k][:, :], in_=C[k][:, :], compare_op=ALU.not_equal,
                                   fill=1.0, base=0, pattern=[[-1, P]],
                                   channel_multiplier=1).then_inc(C["const_ready"], 1)
            pool.affine_select(out=C["mask_qk"][:, :], in_=C["mask_qk"][:, :], compare_op=ALU.is_ge,
                               fill=MASK, base=0, pattern=[[-1, P]],
                               channel_multiplier=1).then_inc(C["const_ready"], 1)
            pool.affine_select(out=C["mask_kq"][:, :], in_=C["mask_kq"][:, :], compare_op=ALU.is_ge,
                               fill=MASK, base=0, pattern=[[1, P]],
                               channel_multiplier=-1).then_inc(C["const_ready"], 1)
            pool.wait_ge(C["const_ready"], 15)
    C["const_count"] = 15
    return C

NT = B * T // P
NB = B * T // QB
NF = D // P
LIN_K, LIN_V = D, 2 * D
EPS = 1e-5


class Steps:

    def __init__(self, sem, names, credit=2):
        self.sem, self.names, self.credit, self.at = sem, list(names), credit, 0
        assert len(set(self.names)) == len(self.names)

    def start(self, eng):
        eng.nop().then_inc(self.sem, self.credit * len(self.names))

    def step(self, name, ins):
        assert self.names[self.at] == name, (self.names[self.at], name)
        self.at = (self.at + 1) % len(self.names)
        return ins.then_inc(self.sem, 1)

    def wait(self, eng, name, blk):
        n = len(self.names)
        eng.wait_ge(self.sem, (blk + self.credit) * n + self.names.index(name) + 1)


def blocks(eng, body, per=2):
    with eng.Fori(0, NB // per) as i:
        for k in range(per):
            body(i * per + k, k, i)


class Banks:

    def __init__(self, c, jobs, steps, ring=8):
        assert len(jobs) % ring == 0
        self.jobs, self.steps, self.ring = jobs, steps, ring
        self.index = {j[0]: n for n, j in enumerate(jobs)}
        self.banks = [c.ps(f"bank{k}", [P, QB]) for k in range(ring)]

    def bank(self, name):
        return self.banks[self.index[name] % self.ring]

    def take(self, pe, name, blk, *needs):
        n = self.index[name]
        _, eng, drained = self.jobs[n - self.ring]
        last = {}
        for e, step, ago in needs + ((eng, drained, 0 if n >= self.ring else 1),):
            at = (-ago, self.steps[e].names.index(step), step)
            last[e] = max(last.get(e, at), at)
        for e, (ago, _, step) in last.items():
            self.steps[e].wait(pe, step, blk + ago)
        return self.banks[n % self.ring]


class Chain:

    def __init__(self, eng, sem):
        self.eng, self.sem, self.n = eng, sem, 0

    def link(self, ins):
        self.n += 1
        ins.then_inc(self.sem, 1)
        self.eng.wait_ge(self.sem, self.n)


def moments(dve, link, st, mean, var, diff):
    link(dve.tensor_tensor(mean, st[:, :, 1], st[:, :, 4], ALU.add))
    link(dve.tensor_tensor(diff, st[:, :, 1], st[:, :, 4], ALU.subtract))
    link(dve.tensor_scalar(mean, mean, 0.5, None, ALU.mult))
    link(dve.tensor_tensor(diff, diff, diff, ALU.mult))
    link(dve.tensor_tensor(var, st[:, :, 2], st[:, :, 5], ALU.add))
    link(dve.tensor_scalar(var, var, 1.0 / D, EPS, ALU.mult, ALU.add))
    link(dve.scalar_tensor_tensor(out=var, in0=diff, scalar=0.25, in1=var, op0=ALU.mult,
                                  op1=ALU.add))


def inverse_root(dve, link, std, var, rstd):
    link(dve.reciprocal(rstd, std))
    link(dve.tensor_tensor(std, rstd, rstd, ALU.mult))
    link(dve.tensor_tensor(std, std, var, ALU.mult))
    link(dve.tensor_scalar(std, std, -0.5, 1.5, ALU.mult, ALU.add))
    link(dve.tensor_tensor(rstd, rstd, std, ALU.mult))


def normalize_input(nc, x, xn_all, mean2, rstd2):
    with Ctx(nc, "ln") as c:
        st = c.sb("st", [P, NT, 6], F32)
        mean = c.sb("mean", [P, NT], F32)
        var = c.sb("var", [P, NT], F32)
        std = c.sb("std", [P, NT], F32)
        diff = c.sb("diff", [P, NT], F32)
        PARTS = 4
        per = NT // PARTS
        ld = [c.sem(f"ld{j}") for j in range(PARTS)]
        ch, stats, var_ready, std_ready, norm = (c.sem(n) for n in
                                                 ("ch", "stats", "var_ready", "std_ready", "norm"))
        block = c.block()
        xt = x.rearrange("b (t p) d -> p (b t) d", p=P)

        @block.sync
        def _(sp):
            for j in range(PARTS):
                sp.dma_start(xn_all[:, j * per:(j + 1) * per, :],
                             xt[:, j * per:(j + 1) * per, :]).then_inc(ld[j], 16)

        @block.scalar
        def _(act):
            for n in range(2):
                act.wait_ge(var_ready, n + 1)
                act.activation(std[:, :], var[:, :], ACT.Sqrt).then_inc(std_ready, 1)

        @block.vector
        def _(dve):
            chain = Chain(dve, ch)
            for j in range(PARTS):
                dve.wait_ge(ld[j], 16)
                with dve.Fori(0, per) as t:
                    dve.bn_stats(st[:, t + j * per, :], xn_all[:, t + j * per, :]).then_inc(stats, 1)
            dve.wait_ge(stats, NT)
            moments(dve, chain.link, st, mean[:, :], var[:, :], diff[:, :])
            dve.nop().then_inc(var_ready, 1)
            dve.wait_ge(std_ready, 1)
            inverse_root(dve, chain.link, std[:, :], var[:, :], rstd2[:, :])
            with dve.Fori(0, NT) as t:
                dve.tensor_scalar(xn_all[:, t, :], xn_all[:, t, :], mean[:, bass.ds(t, 1)],
                                  rstd2[:, bass.ds(t, 1)], ALU.subtract, ALU.mult).then_inc(norm, 1)
                dve.wait_ge(norm, t + 1)
                dve.bn_stats(st[:, t, :], xn_all[:, t, :]).then_inc(stats, 1)
            dve.wait_ge(stats, 2 * NT)
            moments(dve, chain.link, st, mean2[:, :], var[:, :], diff[:, :])
            dve.nop().then_inc(var_ready, 1)
            dve.wait_ge(std_ready, 2)
            inverse_root(dve, chain.link, std[:, :], var[:, :], rstd2[:, :])


def project_first(nc, C, W, xn_all, mean2, rstd2, qf_all, kv_sum, scale_qk, qk_out, v_out):
    T_NAMES = ("T xn0", "T xn1", "T z0", "T z1")
    jobs = [(n, "act", n) for n in T_NAMES]
    for f in range(2):
        jobs += [(f"q{f}", "act", f"q{f}")]
    for t in range(2):
        jobs += [(f"kv{t}", "act", f"v{t}")]
    for f in range(2):
        jobs += [(f"rot q{f}", "dve", f"rot q{f}")]
    for t in range(2, 4):
        jobs += [(f"kv{t}", "act", f"v{t}")]
    for f in range(4):
        jobs += [(f"f{f}", "act", f"f{f}")]
    for t in range(2):
        jobs += [(f"fv{t}", "act", f"fv{t}")]
    for f in range(4):
        jobs += [(f"rot f{f}", "dve", f"rot f{f}")]
    for f in range(2):
        jobs += [(f"sum{f}", "dve", f"sum{f}")]
    pe_names = [j[0] for j in jobs]
    act_names = list(T_NAMES) + ["q0", "q1", "k0", "v0", "k1", "v1", "k2", "v2", "k3", "v3",
                                 "exp q0", "exp q1", "f0", "f1", "f2", "f3", "fv0", "fv1", "exp k",
                                 "hi q", "hi k"]
    dve_names = ["x next", "z next0", "z next1", "z next2", "z next3",
                 "rot q0", "add q0", "min q0", "rot q1", "add q1", "min q1",
                 "k lo", "k hi", "min k", "feat q0", "feat q1",
                 "rot f0", "add f0", "rot f1", "add f1", "feat k",
                 "rot f2", "add f2", "lo q", "rot f3", "add f3", "lo k", "sum0", "sum1"]
    pool_names = ["cos q0", "cos q1", "k1cos", "k2sin", "k1sin", "k2cos",
                  "cos f0", "cos f1", "cos f2", "cos f3"]

    with Ctx(nc, "pr") as c:
        wl = c.sb("wl", [P, NF, 3 * D], F32)
        wf = c.sb("wf", [P, NF, 3, H, 16], F32)
        cos_q = c.sb("cos_q", [P, T], F32)
        sin_q = c.sb("sin_q", [P, T], F32)
        cos_f = c.sb("cos_f", [P, T], F32)
        sin_f = c.sb("sin_f", [P, T], F32)
        cos_k = c.sb("cos_k", [P, NKC, 8], F32)
        sin_k = c.sb("sin_k", [P, NKC, 8], F32)
        rotate = c.sb("rotate", [P, P], F32)
        gb = c.sb("gb", [P, NF, 2], F32)
        x4 = c.sb("x4", [P, 4, D], F32)
        z = [c.sb(f"z{k}", [P, 4, D], F32) for k in range(2)]
        xnT = c.sb("xnT", [P, NF, QB], F32)
        hT = c.sb("hT", [P, NF, QB], F32)
        qs = c.sb("qs", [P, 2, QB], F32)
        qc = c.sb("qc", [P, 2, QB], F32)
        qr = c.sb("qr", [P, 2, QB], F32)
        ks = c.sb("ks", [P, 4, H, 2, 8], F32)
        kp = c.sb("kp", [P, 4, 4, H, 8], F32)
        kr = c.sb("kr", [P, 4, H, 2, 8], F32)
        ke = c.sb("ke", [P, 4 * D], F32)
        vl = c.sb("vl", [P, 4, NF, P + 8], F32)
        fs = c.sb("fs", [P, 4, QB], F32)
        fr = c.sb("fr", [P, 4, QB], F32)
        part16 = c.sb("part16", [P, 2, 4, QB], F16)
        vt = c.sb("vt", [P, 4, H, 2, 16], F32)
        ld, ones, zero = c.sem("ld"), c.sem("ones"), c.sem("zero")
        pe_s = Steps(c.sem("pe"), pe_names)
        act_s = Steps(c.sem("act"), act_names)
        dve_s = Steps(c.sem("dve"), dve_names)
        pool_s = Steps(c.sem("pool"), pool_names)
        held = {e: c.sem(f"held_{e}") for e in ("pe", "act", "dve", "pool")}
        raw_out, vt_out = c.sem("raw_out"), c.sem("vt_out")
        block = c.block()
        banks = Banks(c, jobs, {"act": act_s, "dve": dve_s})
        LOADS = [0]

        @block.sync
        def _(sp):
            def load(dst, src):
                sp.dma_start(dst, src).then_inc(ld, 16)
                LOADS[0] += 16
            load(wl[:, :, :], W["W_qkv"].rearrange("(c p) n -> p c n", p=P))
            for part in range(3):
                for f in range(NF):
                    load(wf[:, f, part, :, :], W["ffn_Wqkv"][f * P:(f + 1) * P, :].rearrange(
                        "p (h s d) -> p h s d", h=H, s=3)[:, :, part, :])
            load(cos_q[:, :], W["cos_q"])
            load(sin_q[:, :], W["sin_q"])
            load(cos_f[:, :], W["cos_f"])
            load(sin_f[:, :], W["sin_f"])
            load(cos_k[:, :, :], W["cos_k"])
            load(sin_k[:, :, :], W["sin_k"])
            load(rotate[:, :], W["rotate"])
            with nc.allow_non_contiguous_dma(reason="a few hundred floats"):
                load(gb[:, :, 0], W["ln1_g"].rearrange("(c p) -> p c", p=P))
                load(gb[:, :, 1], W["ln1_b"].rearrange("(c p) -> p c", p=P))

            def body(blk, k, i):
                b, j = i // 2, (i % 2) * 2 + k
                act_s.wait(sp, "fv1", blk)
                for g in range(4):
                    sp.dma_start(v_out[b, g, :, bass.ds(j * 4, 4), :],
                                 vt[:, :, g * HG:(g + 1) * HG, :, :]
                                 .rearrange("p t h s d -> p t (h s d)")).then_inc(vt_out, 16)
                dve_s.wait(sp, "lo k", blk)
                for side in range(2):
                    for lower in range(2):
                        dst = qk_out[side][lower].rearrange("(b c g) h d t -> b c (g h d) t", b=B, c=NF)
                        sp.dma_start(dst[b, :, :, bass.ds(j * QB, QB)].rearrange("c p t -> p c t"),
                                     part16[:, lower, 2 * side:2 * side + 2, :]).then_inc(raw_out, 16)
            blocks(sp, body)
            sp.wait_ge(raw_out, 1 + 64 * NB)
            sp.wait_ge(vt_out, 1 + 64 * NB)

        @block.gpsimd
        def _(pool):
            pool.memset(vt[:, :, :, 1, :], 1.0).then_inc(ones, 1)
            pool.memset(vl[:, :, :, P:P + 8], 1.0).then_inc(ones, 1)
            pool_s.start(pool)
            pool.wait_ge(ld, LOADS[0])
            tt = pool.tensor_tensor

            def body(blk, k, i):
                tok = bass.ds((i % 2) * 2 * QB + k * QB, QB)
                tile = bass.ds((i % 2) * 8 + k * 4, 4)
                for f in range(2):
                    act_s.wait(pool, f"q{f}", blk)
                    dve_s.wait(pool, f"feat q{f}", blk - 1)
                    pool.nop().then_inc(held["pool"], 1)
                    pool_s.step(f"cos q{f}", tt(qc[:, f, :], qs[:, f, :], cos_q[:, tok], ALU.mult))
                act_s.wait(pool, "k3", blk)
                dve_s.wait(pool, "k hi", blk - 1)
                pool.nop().then_inc(held["pool"], 1)
                ck = cos_k[:, tile, :].unsqueeze(2).to_broadcast([P, 4, H, 8])
                sk = sin_k[:, tile, :].unsqueeze(2).to_broadcast([P, 4, H, 8])
                for n, (name, half, table) in enumerate((("k1cos", 0, ck), ("k2sin", 1, sk),
                                                         ("k1sin", 0, sk), ("k2cos", 1, ck))):
                    pool_s.step(name, tt(kp[:, n], ks[:, :, :, half, :], table, ALU.mult))
                for f in range(4):
                    act_s.wait(pool, f"f{f}", blk)
                    dve_s.wait(pool, "lo k", blk - 1)
                    pool.nop().then_inc(held["pool"], 1)
                    pool_s.step(f"cos f{f}", tt(fr[:, f, :], fs[:, f, :], cos_f[:, tok], ALU.mult))
            blocks(pool, body)

        @block.scalar
        def _(act):
            act_s.start(act)
            act.nop().then_inc(vt_out, 1)
            act.nop().then_inc(raw_out, 1)
            act.wait_ge(ld, LOADS[0])
            act.wait_ge(ones, 2)
            def body(blk, k, i):
                def src(name):
                    pe_s.wait(act, name, blk)
                    return banks.bank(name)

                for f in range(2):
                    act_s.step(f"T xn{f}", act.activation(xnT[:, f, :], src(f"T xn{f}")[:, :], ACT.Copy))
                for f in range(2):
                    act_s.step(f"T z{f}", act.activation(hT[:, f, :], src(f"T z{f}")[:, :],
                                                         ACT.Identity, bias=gb[:, f, 1:2],
                                                         scale=gb[:, f, 0:1]))
                for f in range(2):
                    pool_s.wait(act, f"cos q{f}", blk - 1)
                    act_s.step(f"q{f}", act.activation(qs[:, f, :], src(f"q{f}")[:, :], ACT.Copy))
                for t in range(4):
                    s = src(f"kv{t}")
                    pool_s.wait(act, "k2cos", blk - 1)
                    act_s.step(f"k{t}", act.activation(
                        ks[:, t].rearrange("p h s d -> p (h s d)"), s[:, 0:D], ACT.Copy))
                    act_s.step(f"v{t}", act.activation(
                        vl[:, t, :, 0:P], s[:, D:2 * D].rearrange("p (c d) -> p c d", c=NF), ACT.Copy))
                for f in range(2):
                    dve_s.wait(act, f"min q{f}", blk)
                    act_s.step(f"exp q{f}", act.activation(qc[:, f, :], qc[:, f, :], ACT.Exp))
                for f in range(4):
                    dve_s.wait(act, f"add f{f}", blk - 1)
                    act_s.step(f"f{f}", act.activation(fs[:, f, :], src(f"f{f}")[:, :], ACT.Copy))
                for t in range(2):
                    act.wait_ge(vt_out, blk * 64 + 1)
                    act_s.step(f"fv{t}", act.activation(
                        vt[:, 2 * t:2 * t + 2, :, 0, :],
                        src(f"fv{t}")[:, :].rearrange("p (t h d) -> p t h d", t=2, h=H), ACT.Copy))
                dve_s.wait(act, "min k", blk)
                act_s.step("exp k", act.activation(ke[:, :], ke[:, :], ACT.Exp))
                act.wait_ge(raw_out, blk * 64 + 1)
                for side, name in enumerate("qk"):
                    dve_s.wait(act, f"add f{2 * side + 1}", blk)
                    act_s.step(f"hi {name}", act.activation(
                        part16[:, 0, 2 * side:2 * side + 2, :], fr[:, 2 * side:2 * side + 2, :],
                        ACT.Copy, scale=scale_qk[side]))
            blocks(act, body)

        @block.vector
        def _(dve):
            tt = dve.tensor_tensor

            def z_tile(t, slot, n):
                return dve.tensor_scalar(z[slot][:, n, :], xn_all[:, bass.ds(t, 1), :].rearrange("p a d -> p (a d)"),
                                         mean2[:, bass.ds(t, 1)], rstd2[:, bass.ds(t, 1)], ALU.subtract, ALU.mult)

            dve.tensor_copy(x4[:, :, :], xn_all[:, 0:4, :]).then_inc(zero, 1)
            for n in range(4):
                z_tile(n, 0, n).then_inc(zero, 1)
            dve.memset(kv_sum[:, :, :], 0.0).then_inc(zero, 1)
            dve.wait_ge(zero, 6)
            dve_s.start(dve)
            dve.wait_ge(ld, LOADS[0])

            def body(blk, k, i):
                def src(name):
                    pe_s.wait(dve, name, blk)
                    return banks.bank(name)

                tok = bass.ds((i % 2) * 2 * QB + k * QB, QB)
                nxt = (blk + 1) % NB
                pe_s.wait(dve, "T xn1", blk)
                dve_s.step("x next", dve.tensor_copy(x4[:, :, :],
                                                     xn_all[:, bass.ds(nxt * 4, 4), :]))
                for n in range(4):
                    dve_s.step(f"z next{n}", z_tile(nxt * 4 + n, (k + 1) % 2, n))
                for f in range(2):
                    s = src(f"rot q{f}")
                    dve_s.wait(dve, f"feat q{f}", blk - 1)
                    dve_s.step(f"rot q{f}", tt(qr[:, f, :], s[:, :], sin_q[:, tok], ALU.mult))
                    dve_s.wait(dve, f"rot q{f}", blk)
                    pool_s.wait(dve, f"cos q{f}", blk)
                    dve_s.step(f"add q{f}", tt(qr[:, f, :], qr[:, f, :], qc[:, f, :], ALU.add))
                    dve_s.wait(dve, f"add q{f}", blk)
                    dve_s.step(f"min q{f}", dve.tensor_scalar(qc[:, f, :], qr[:, f, :], 0.0, None, ALU.min))
                pool_s.wait(dve, "k2cos", blk)
                dve_s.wait(dve, "feat k", blk - 1)
                pe_s.wait(dve, "sum1", blk - 1)
                dve_s.step("k lo", tt(kr[:, :, :, 0, :], kp[:, 0], kp[:, 1], ALU.subtract))
                dve_s.step("k hi", tt(kr[:, :, :, 1, :], kp[:, 2], kp[:, 3], ALU.add))
                dve_s.wait(dve, "k hi", blk)
                flat = kr[:, :, :, :, :].rearrange("p t h s d -> p (t h s d)")
                dve_s.step("min k", dve.tensor_scalar(ke[:, :], flat, 0.0, None, ALU.min))
                for f in range(2):
                    act_s.wait(dve, f"exp q{f}", blk)
                    dve_s.step(f"feat q{f}", dve.scalar_tensor_tensor(
                        out=qf_all[:, f, bass.ds(blk * QB, QB)], in0=qr[:, f, :], scalar=0.0,
                        in1=qc[:, f, :], op0=ALU.max, op1=ALU.add))
                for f in range(4):
                    s = src(f"rot f{f}")
                    pool_s.wait(dve, f"cos f{f}", blk)
                    dve_s.step(f"rot f{f}", tt(fs[:, f, :], s[:, :], sin_f[:, tok], ALU.mult))
                    dve_s.wait(dve, f"rot f{f}", blk)
                    dve_s.step(f"add f{f}", tt(fr[:, f, :], fr[:, f, :], fs[:, f, :], ALU.add))
                    if f >= 2:
                        side = f - 2
                        act_s.wait(dve, f"hi {'qk'[side]}", blk)
                        dve_s.step(f"lo {'qk'[side]}", dve.scalar_tensor_tensor(
                            out=part16[:, 1, 2 * side:2 * side + 2, :],
                            in0=fr[:, 2 * side:2 * side + 2, :], scalar=scale_qk[side],
                            in1=part16[:, 0, 2 * side:2 * side + 2, :], op0=ALU.mult,
                            op1=ALU.subtract))
                    if f == 1:
                        act_s.wait(dve, "exp k", blk)
                        dve_s.step("feat k", dve.scalar_tensor_tensor(
                            out=flat, in0=flat, scalar=0.0, in1=ke[:, :], op0=ALU.max, op1=ALU.add))
                for f in range(2):
                    s = src(f"sum{f}")
                    acc = kv_sum[:, bass.ds((i // 2) * NF + f, 1), :].rearrange("p a n -> p (a n)")
                    dve_s.wait(dve, f"sum{f}", blk - 1)
                    dve_s.step(f"sum{f}", tt(acc, acc, s[:, 0:P + 8], ALU.add))
            blocks(dve, body)

        @block.tensor
        def _(pe):
            pe_s.start(pe)
            pe.wait_ge(C["const_ready"], C["const_count"])
            pe.wait_ge(ld, LOADS[0])
            def body(blk, k, i):
                def dst(name, *needs):
                    return banks.take(pe, name, blk, *needs)

                def accumulate(name, pairs, width=QB, needs=()):
                    d = dst(name, *needs)
                    for n, (lhsT, rhs) in enumerate(pairs):
                        mm = pe.matmul(d[:, 0:width], lhsT, rhs, start=n == 0, stop=n == len(pairs) - 1)
                    pe_s.step(name, mm)

                for name, src, made in (("T xn", x4, "x next"), ("T z", z[k], "z next3")):
                    for f in range(2):
                        d = dst(f"{name}{f}", ("dve", made, 1))
                        for t in range(4):
                            mm = pe.transpose(d[:, t * P:(t + 1) * P],
                                              src[:, t, f * P:(f + 1) * P], C["identf"][:, :])
                        pe_s.step(f"{name}{f}", mm)

                def feature_rows(name, weights, act_T, made):
                    accumulate(name, [(weights(n), act_T[:, n, :]) for n in range(NF)],
                               needs=(("act", made, 0),))

                def token_rows(name, act_T, t, weights):
                    accumulate(name, [(act_T[:, n, t * P:(t + 1) * P], weights(n)) for n in range(NF)])

                for f in range(2):
                    feature_rows(f"q{f}", lambda n: wl[:, n, f * P:(f + 1) * P], xnT, "T xn1")
                for t in range(2):
                    token_rows(f"kv{t}", xnT, t, lambda n: wl[:, n, D:3 * D])
                for f in range(2):
                    accumulate(f"rot q{f}", [(rotate[:, :], qs[:, f, :])],
                               needs=(("act", f"q{f}", 0),))
                for t in range(2, 4):
                    token_rows(f"kv{t}", xnT, t, lambda n: wl[:, n, D:3 * D])
                for f in range(4):
                    feature_rows(f"f{f}", lambda n: wf[:, n, f // 2, (f % 2) * 8:(f % 2) * 8 + 8, :]
                                 .rearrange("p h d -> p (h d)"), hT, "T z1")
                for m in range(2):
                    d = dst(f"fv{m}")
                    for t in range(2):
                        for n in range(NF):
                            mm = pe.matmul(d[:, t * D:(t + 1) * D],
                                           hT[:, n, (2 * m + t) * P:(2 * m + t + 1) * P],
                                           wf[:, n, 2, :, :].rearrange("p h d -> p (h d)"),
                                           start=n == 0, stop=n == NF - 1)
                    pe_s.step(f"fv{m}", mm)
                for f in range(4):
                    accumulate(f"rot f{f}", [(rotate[:, :], fs[:, f, :])],
                               needs=(("act", f"f{f}", 0),))
                for f in range(2):
                    accumulate(f"sum{f}", [(kr[:, t].rearrange("p h s d -> p (h s d)")[:, f * P:(f + 1) * P],
                                            vl[:, t, f, :]) for t in range(4)], P + 8,
                               needs=(("dve", "feat k", 0), ("act", "v3", 0)))
            blocks(pe, body)

E = 8
CAP = 2 * B * T // E
FF = 4 * D
NFF = FF // P
NCT = CAP // P
SPLIT_TOP = 4096.0
FLOOR = 1e-6


def prepare(nc, C, W, score, zeros, exp_in, zero_fill):
    with Ctx(nc, "prep") as c:
        wf = c.sb("wf", [P, NF, H, 3, 16], F32)
        wq = c.sb("wq", [P, 2, NF, 2 * D], F32)
        sq = c.sb("sq", [P, NF, 2 * D], F32)
        gb = c.sb("gb", [P, 2, NF], F32)
        gb2 = c.sb("gb2", [P, 2, NF], F32)
        kern = c.sb("kern", [P, NF, D], F32)
        lora_a = c.sb("lora_a", [P, NF, 16], F32)
        lora_b = c.sb("lora_b", [16, D], F32)
        aT = c.sb("aT", [16, NF, P], F32)
        top = c.sb("top", [P, 4], F32)
        bound = c.sb("bound", [P, 4], F32)
        small = c.sb("small", [P, 8], F32)
        red = c.sb("red", [P, 2], F32)
        redall = c.sb("redall", [P, 2], F32)
        ps = [c.ps(f"ps{k}", [P, 2 * D]) for k in range(6)]
        ld, ch, sq_s, mm_s, red_s, all_s, root_s, rooted, pool_s, cp_s = (
            c.sem(n) for n in ("ld", "ch", "sq", "mm", "red", "all", "root", "rooted", "pool", "cp"))
        block = c.block()
        n_loads = [0]

        @block.sync
        def _(sp):
            def load(dst, src):
                sp.dma_start(dst, src).then_inc(ld, 16)
                n_loads[0] += 16
            load(wf[:, :, :, :, :].rearrange("p c h s d -> p c (h s d)"),
                 W["ffn_Wqkv"].rearrange("(c p) n -> p c n", p=P))
            load(wq[:, 0], W["Wq"].rearrange("(c p) n -> p c n", p=P))
            load(wq[:, 1], W["Wk"].rearrange("(c p) n -> p c n", p=P))
            load(kern[:, :, :], W["kernel"].rearrange("(c p) n -> p c n", p=P))
            load(lora_a[:, :, :], W["a"].rearrange("(c p) n -> p c n", p=P))
            load(lora_b[:, :], W["b"])
            with nc.allow_non_contiguous_dma(reason="a few hundred floats"):
                load(gb[:, 0, :], W["ln1_g"].rearrange("(c p) -> p c", p=P))
                load(gb[:, 1, :], W["ln1_b"].rearrange("(c p) -> p c", p=P))
            sp.wait_ge(pool_s, 1)
            rows = exp_in.rearrange("(p r) d -> p r d", p=P)
            sp.dma_start(rows, zeros[:, :].unsqueeze(1).to_broadcast([P, E * CAP // P, D])
                         ).then_inc(zero_fill, 16)

        @block.gpsimd
        def _(pool):
            pool.memset(zeros[:, :], 0.0).then_inc(pool_s, 1)
            pool.wait_ge(red_s, 1)
            pool.partition_all_reduce(redall[:, :], red[:, :], P, bass.bass_isa.ReduceOp.max
                                      ).then_inc(all_s, 1)

        @block.scalar
        def _(act):
            act.wait_ge(root_s, 1)
            act.activation(small[:, 0:5], small[:, 0:5], ACT.Sqrt).then_inc(rooted, 1)

        @block.tensor
        def _(pe):
            pe.wait_ge(C["const_ready"], C["const_count"])
            pe.wait_ge(ld, n_loads[0])
            for n in range(4):
                pe.wait_ge(sq_s, n + 1)
                width = D if n < 2 else 2 * D
                for f in range(NF):
                    mm = pe.matmul(ps[n][:, 0:width], C["onesf"][:, :], sq[:, f, 0:width],
                                   start=f == 0, stop=f == NF - 1)
                mm.then_inc(mm_s, 1)
            pe.wait_ge(sq_s, 5)
            pe.matmul(ps[4][:, 0:NF], C["onesf"][:, :], gb2[:, 1, :], start=True, stop=True).then_inc(mm_s, 1)
            for f in range(NF):
                mm = pe.transpose(ps[5][0:16, f * P:(f + 1) * P], lora_a[:, f, :], C["identf"][:, :])
            mm.then_inc(mm_s, 1)
            pe.wait_ge(cp_s, 1)
            for f in range(NF):
                mm = pe.matmul(ps[0][:, f * D:(f + 1) * D], aT[:, f, :], lora_b[:, :], start=True, stop=True)
            mm.then_inc(mm_s, 1)

        @block.vector
        def _(dve):
            chain = Chain(dve, ch)
            link = chain.link
            dve.wait_ge(ld, n_loads[0])
            for n in range(4):
                for f in range(NF):
                    if n < 2:
                        src = wf[:, f, :, n, :]
                        dst = sq[:, f, 0:D].rearrange("p (h d) -> p h d", h=H)
                    else:
                        src, dst = wq[:, n - 2, f, :], sq[:, f, :]
                    link(dve.tensor_tensor(dst, src, src, ALU.mult))
                dve.nop().then_inc(sq_s, 1)
                width = D if n < 2 else 2 * D
                dve.wait_ge(mm_s, n + 1)
                link(dve.tensor_reduce(top[:, n:n + 1], ps[n][:, 0:width], AX.X, ALU.max))
            link(dve.tensor_tensor(gb2[:, :, :], gb[:, :, :], gb[:, :, :], ALU.mult))
            dve.nop().then_inc(sq_s, 1)
            dve.wait_ge(mm_s, 5)
            link(dve.tensor_reduce(small[:, 4:5], ps[4][:, 0:NF], AX.X, ALU.add))
            link(dve.tensor_reduce(red[:, 0:1], gb[:, 0, :], AX.X, ALU.max, apply_absolute_value=True))
            link(dve.tensor_reduce(red[:, 1:2], kern[:, :, :], AX.XY, ALU.max, apply_absolute_value=True))
            dve.nop().then_inc(red_s, 1)
            link(dve.tensor_copy(small[:, 0:4], top[:, :]))
            dve.nop().then_inc(root_s, 1)
            dve.wait_ge(rooted, 1)
            dve.wait_ge(all_s, 1)
            slack = 1.01 * float(D) ** 0.5
            link(dve.tensor_scalar(bound[:, :], small[:, 0:4], slack, None, ALU.mult))
            link(dve.scalar_tensor_tensor(out=small[:, 5:6], in0=small[:, 4:5], scalar=float(D) ** -0.5,
                                          in1=redall[:, 0:1], op0=ALU.mult, op1=ALU.add))
            link(dve.tensor_scalar(bound[:, 0:2], bound[:, 0:2], small[:, 5:6], 2.0 ** 0.5, ALU.mult, ALU.mult))
            link(dve.tensor_scalar(bound[:, :], bound[:, :], FLOOR, None, ALU.max))
            link(dve.reciprocal(top[:, :], bound[:, :]))
            link(dve.tensor_scalar(top[:, :], top[:, :], SPLIT_TOP, None, ALU.mult))
            for layer in range(2):
                s = score[layer]
                n = 2 * layer
                link(dve.tensor_copy(s[:, 0:2], top[:, n:n + 2]))
                link(dve.tensor_tensor(s[:, 2:3], bound[:, n:n + 1], bound[:, n + 1:n + 2], ALU.mult))
                link(dve.tensor_scalar(s[:, 2:3], s[:, 2:3], SPLIT_TOP ** -2 / 4.0, None, ALU.mult))
            link(dve.tensor_scalar(small[:, 6:7], redall[:, 1:2], 1.0 / 7.0, 1e-30, ALU.mult, ALU.max))
            link(dve.reciprocal(small[:, 7:8], small[:, 6:7]))
            half_even = 1.5 * 2.0 ** 23
            link(dve.tensor_scalar(kern[:, :, :], kern[:, :, :], small[:, 7:8], None, ALU.mult))
            link(dve.tensor_scalar(kern[:, :, :], kern[:, :, :], half_even, half_even, ALU.add, ALU.subtract))
            link(dve.tensor_scalar(kern[:, :, :], kern[:, :, :], 7.0, -8.0, ALU.min, ALU.max))
            dve.wait_ge(mm_s, 6)
            link(dve.tensor_copy(aT[:, :, :], ps[5][0:16, 0:D].rearrange("r (f p) -> r f p", f=NF)))
            dve.nop().then_inc(cp_s, 1)
            dve.wait_ge(mm_s, 7)
            link(dve.scalar_tensor_tensor(out=C["w_ffn"][:, :, :], in0=kern[:, :, :], scalar=small[:, 6:7],
                                          in1=ps[0][:, :].rearrange("p (f n) -> p f n", f=NF),
                                          op0=ALU.mult, op1=ALU.add))


def linear_out(nc, C, W, qf_all, kv_sum, s_out):
    act_names = ["tr0", "tr1", "out0", "out1"]
    dve_names = ["copy"] + [f"{s}{t}" for t in range(4) for s in ("max", "rec", "nrm")]
    jobs = [(f"num{t}", "dve", f"nrm{t}") for t in range(4)]
    jobs += [("tr0", "act", "tr0"), ("tr1", "act", "tr1"), ("out0", "act", "out0"), ("out1", "act", "out1")]
    WID = P + 8
    with Ctx(nc, "lo") as c:
        w_out = c.sb("w_out", [P, NF, D], F32)
        heads = c.sb("heads", [P, WID], F32)
        kvd = c.sb("kvd", [P, B * NF, WID], F32)
        qf = [c.sb(f"qf{k}", [P, NF, QB], F32) for k in range(2)]
        den = c.sb("den", [P, 4, H], F32)
        nrm = c.sb("nrm", [P, 4, D], F32)
        nT = c.sb("nT", [P, 4, NF, P], F32)
        ot = c.sb("ot", [P, 4, D], F32)
        ld, kv_ready, stored = c.sem("ld"), c.sem("kv_ready"), c.sem("stored")
        pe_s = Steps(c.sem("pe"), [j[0] for j in jobs])
        act_s = Steps(c.sem("act"), act_names)
        dve_s = Steps(c.sem("dve"), dve_names)
        banks = Banks(c, jobs, {"act": act_s, "dve": dve_s})
        block = c.block()

        @block.sync
        def _(sp):
            sp.dma_start(w_out[:, :, :], W["W_out"].rearrange("(c p) n -> p c n", p=P)).then_inc(ld, 16)
            sp.dma_start(heads[:, :], W["heads"]).then_inc(ld, 16)

            def body(blk, k, i):
                act_s.wait(sp, "out1", blk)
                sp.dma_start(s_out[bass.ds(blk * 4, 4), :, :].rearrange("t p d -> p t d"),
                             ot[:, :, :]).then_inc(stored, 16)
            blocks(sp, body)
            sp.wait_ge(stored, 1 + 16 * NB)

        @block.vector
        def _(dve):
            dve.wait_ge(ld, 32)
            for n in range(B * NF):
                dve.tensor_tensor(kvd[:, n, :], kv_sum[:, n, :], heads[:, :], ALU.mult).then_inc(kv_ready, 1)
            dve_s.start(dve)

            def body(blk, k, i):
                pe_s.wait(dve, "num3", blk - 2)
                dve_s.step("copy", dve.tensor_copy(qf[k][:, :, :], qf_all[:, :, bass.ds(blk * QB, QB)]))
                pe_s.wait(dve, "tr1", blk - 1)
                for t in range(4):
                    pe_s.wait(dve, f"num{t}", blk)
                    s = banks.bank(f"num{t}")[:, 0:NF * WID].rearrange("p (c n) -> p c n", c=NF)
                    d = den[:, t, :].rearrange("p (c h) -> p c h", c=NF)
                    dve_s.step(f"max{t}", dve.tensor_scalar(d, s[:, :, P:WID], 1e-6, None, ALU.max))
                    dve_s.wait(dve, f"max{t}", blk)
                    dve_s.step(f"rec{t}", dve.reciprocal(d, d))
                    dve_s.wait(dve, f"rec{t}", blk)
                    n = nrm[:, t, :].rearrange("p (c h d) -> p c h d", c=NF, h=8)
                    dve_s.step(f"nrm{t}", dve.tensor_tensor(
                        n, s[:, :, 0:P].rearrange("p c (h d) -> p c h d", h=8),
                        d.unsqueeze(3).to_broadcast([P, NF, 8, 16]), ALU.mult))
            blocks(dve, body)

        @block.scalar
        def _(act):
            act_s.start(act)
            act.nop().then_inc(stored, 1)

            def body(blk, k, i):
                for m in range(2):
                    pe_s.wait(act, f"tr{m}", blk)
                    act_s.step(f"tr{m}", act.activation(
                        nT[:, 2 * m:2 * m + 2, :, :].rearrange("p t c n -> p (t c n)"),
                        banks.bank(f"tr{m}")[:, :], ACT.Copy))
                act.wait_ge(stored, blk * 16 + 1)
                for m in range(2):
                    pe_s.wait(act, f"out{m}", blk)
                    act_s.step(f"out{m}", act.activation(
                        ot[:, 2 * m:2 * m + 2, :].rearrange("p t n -> p (t n)"),
                        banks.bank(f"out{m}")[:, :], ACT.Copy))
            blocks(act, body)

        @block.tensor
        def _(pe):
            pe_s.start(pe)
            pe.wait_ge(ld, 32)
            pe.wait_ge(kv_ready, B * NF)

            def body(blk, k, i):
                b = i // 2
                for t in range(4):
                    d = banks.take(pe, f"num{t}", blk, ("dve", "copy", 0))
                    for f in range(NF):
                        mm = pe.matmul(d[:, f * WID:(f + 1) * WID], qf[k][:, f, t * P:(t + 1) * P],
                                       kvd[:, bass.ds(b * NF + f, 1), :].rearrange("p a n -> p (a n)"),
                                       start=True, stop=True)
                    pe_s.step(f"num{t}", mm)
                for m in range(2):
                    d = banks.take(pe, f"tr{m}", blk, ("dve", f"nrm{2 * m + 1}", 0))
                    for t in range(2):
                        for f in range(NF):
                            mm = pe.transpose(d[:, (t * NF + f) * P:(t * NF + f + 1) * P],
                                              nrm[:, 2 * m + t, f * P:(f + 1) * P], C["identf"][:, :])
                    pe_s.step(f"tr{m}", mm)
                for m in range(2):
                    d = banks.take(pe, f"out{m}", blk, ("act", f"tr{m}", 0))
                    for t in range(2):
                        for f in range(NF):
                            mm = pe.matmul(d[:, t * D:(t + 1) * D], nT[:, 2 * m + t, f, :], w_out[:, f, :],
                                           start=f == 0, stop=f == NF - 1)
                    pe_s.step(f"out{m}", mm)
            blocks(pe, body)


def invert_sums(nc, tag, sums, inverse):
    with Ctx(nc, tag) as c:
        tile = c.sb("tile", [P, QB], F32)
        ld, inverted, stored = c.sem("ld"), c.sem("inverted"), c.sem("stored")
        block = c.block()

        @block.sync
        def _(sp):
            sp.dma_start(tile[:, :], sums.rearrange("x (q t) -> x q t", t=QB)).then_inc(ld, 16)
            sp.wait_ge(inverted, 1)
            sp.dma_start(inverse.rearrange("x (q t) -> x q t", t=QB), tile[:, :]).then_inc(stored, 16)
            sp.wait_ge(stored, 16)

        @block.vector
        def _(dve):
            dve.wait_ge(ld, 16)
            dve.reciprocal(tile[:, :], tile[:, :]).then_inc(inverted, 1)


class Attended:

    def __init__(self, c, att, inverse, pe_s, last_use):
        self.att = att.rearrange("(b g) p t -> b p g t", b=B)
        self.inverse = inverse.rearrange("(b g h) t -> b h g t", b=B, h=HG)
        self.pe_s, self.last_use = pe_s, last_use
        self.a = [c.sb(f"a{k}", [P, 4, QB], F32) for k in range(NB // B)]
        self.r = [c.sb(f"r{k}", [P, 4, QB], F32) for k in range(NB // B)]
        self.ld = [c.sem(f"ld{k}") for k in range(NB // B)]
        self.divided = c.sem("divided")

    def load(self, sp, blk, k, i):
        self.pe_s.wait(sp, self.last_use, blk - NB // B)
        tok = slice(k * QB, (k + 1) * QB)
        sp.dma_start(self.a[k][:, :, :], self.att[bass.ds(i, 1), :, :, tok].rearrange("b p g t -> (b p) g t")).then_inc(self.ld[k], 16)
        for h in range(HG):
            sp.dma_start(self.r[k][32 * h:32 * h + 32, :, :],
                         self.inverse[bass.ds(i, 1), h, :, tok].to_broadcast([32, 4, QB])
                         ).then_inc(self.ld[k], 16)

    def divide(self, pool):
        def body(blk, k, i):
            pool.wait_ge(self.ld[k], i * 80 + 80)
            pool.tensor_tensor(self.a[k][:, :, :], self.a[k][:, :, :], self.r[k][:, :, :],
                               ALU.mult).then_inc(self.divided, 1)
        blocks(pool, body, NB // B)

    def wait(self, pe, blk):
        pe.wait_ge(self.divided, blk + 1)


def after_attention(nc, C, W, att, inverse, x_all, stats):
    jobs = [(f"x{t}", "dve", f"add{t}") for t in range(4)]
    dve_names = [f"{s}{t}" for t in range(4) for s in ("add", "stat")]
    with Ctx(nc, "aa") as c:
        w = c.sb("w", [P, 4, D], F32)
        w_ld, zeroed = c.sem("w_ld"), c.sem("zeroed")
        pe_s = Steps(c.sem("pe"), [j[0] for j in jobs], credit=NB // B)
        dve_s = Steps(c.sem("dve"), dve_names)
        banks = Banks(c, jobs, {"dve": dve_s}, ring=4)
        attended = Attended(c, att, inverse, pe_s, "x3")
        block = c.block()

        @block.sync
        def _(sp):
            sp.wait_ge(zeroed, 1)
            for h in range(HG):
                sp.dma_start(w[32 * h:32 * h + 16, :, :],
                             W["Wproj"].rearrange("(g h d) n -> h d g n", g=4, h=HG)[h]).then_inc(w_ld, 16)

            blocks(sp, lambda blk, k, i: attended.load(sp, blk, k, i), NB // B)

        @block.gpsimd
        def _(pool):
            attended.divide(pool)

        @block.vector
        def _(dve):
            dve.memset(w[:, :, :], 0.0).then_inc(zeroed, 1)
            dve_s.start(dve)

            def body(blk, k, i):
                for t in range(4):
                    x = x_all[:, bass.ds(blk * 4 + t, 1), :].rearrange("p a d -> p (a d)")
                    pe_s.wait(dve, f"x{t}", blk)
                    dve_s.step(f"add{t}", dve.tensor_tensor(x, x, banks.bank(f"x{t}")[:, 0:D], ALU.add))
                    dve_s.wait(dve, f"add{t}", blk)
                    dve_s.step(f"stat{t}", dve.bn_stats(stats[:, blk * 4 + t, :], x))
            blocks(dve, body)

        @block.tensor
        def _(pe):
            pe_s.start(pe)
            pe.wait_ge(w_ld, 64)

            def body(blk, k, i):
                attended.wait(pe, blk)
                for t in range(4):
                    d = banks.take(pe, f"x{t}", blk)
                    for g in range(4):
                        mm = pe.matmul(d[:, 0:D], attended.a[k][:, g, t * P:(t + 1) * P], w[:, g, :],
                                       start=g == 0, stop=g == 3)
                    pe_s.step(f"x{t}", mm)
            blocks(pe, body, NB // B)


def row_statistics(nc, tag, stats, mean, rstd):
    with Ctx(nc, tag) as c:
        var = c.sb("var", [P, NT], F32)
        std = c.sb("std", [P, NT], F32)
        diff = c.sb("diff", [P, NT], F32)
        ch, var_ready, std_ready = c.sem("ch"), c.sem("var_ready"), c.sem("std_ready")
        block = c.block()

        @block.scalar
        def _(act):
            act.wait_ge(var_ready, 1)
            act.activation(std[:, :], var[:, :], ACT.Sqrt).then_inc(std_ready, 1)

        @block.vector
        def _(dve):
            chain = Chain(dve, ch)
            moments(dve, chain.link, stats, mean[:, :], var[:, :], diff[:, :])
            dve.nop().then_inc(var_ready, 1)
            dve.wait_ge(std_ready, 1)
            inverse_root(dve, chain.link, std[:, :], var[:, :], rstd[:, :])


def gate_logits(nc, C, W, x_all, mean, rstd, z_all, logits):
    jobs = [("T0", "act", "T0"), ("T1", "act", "T1"), ("log", "dve", "log"), ("none", "dve", "log")]
    with Ctx(nc, "gl") as c:
        z = [c.sb(f"z{k}", [P, 4, D], F32) for k in range(2)]
        hT = c.sb("hT", [P, NF, QB], F32)
        wg = c.sb("wg", [P, NF, E], F32)
        gb = c.sb("gb", [P, NF, 2], F32)
        ld = c.sem("ld")
        pe_s = Steps(c.sem("pe"), ["T0", "T1", "log"])
        act_s = Steps(c.sem("act"), ["T0", "T1", "keep"])
        dve_s = Steps(c.sem("dve"), ["z0", "z1", "z2", "z3", "log"])
        banks = Banks(c, jobs, {"act": act_s, "dve": dve_s}, ring=4)
        block = c.block()

        @block.sync
        def _(sp):
            with nc.allow_non_contiguous_dma(reason="a few hundred floats"):
                sp.dma_start(wg[:, :, :], W["Wgate"].rearrange("(c p) e -> p c e", p=P)).then_inc(ld, 16)
                sp.dma_start(gb[:, :, 0], W["ln2_g"].rearrange("(c p) -> p c", p=P)).then_inc(ld, 16)
                sp.dma_start(gb[:, :, 1], W["ln2_b"].rearrange("(c p) -> p c", p=P)).then_inc(ld, 16)

        @block.vector
        def _(dve):
            dve_s.start(dve)

            def body(blk, k, i):
                pe_s.wait(dve, "T1", blk - 2)
                act_s.wait(dve, "keep", blk - 2)
                for t in range(4):
                    n = blk * 4 + t
                    dve_s.step(f"z{t}", dve.tensor_scalar(
                        z[k][:, t, :], x_all[:, bass.ds(n, 1), :].rearrange("p a d -> p (a d)"),
                        mean[:, bass.ds(n, 1)], rstd[:, bass.ds(n, 1)], ALU.subtract, ALU.mult))
                pe_s.wait(dve, "log", blk)
                dve_s.step("log", dve.tensor_copy(
                    logits[:, bass.ds(blk * 4, 4), :],
                    banks.bank("log")[:, 0:4 * E].rearrange("p (t e) -> p t e", t=4)))
            blocks(dve, body)

        @block.scalar
        def _(act):
            act_s.start(act)
            act.wait_ge(ld, 48)

            def body(blk, k, i):
                for f in range(NF):
                    pe_s.wait(act, f"T{f}", blk)
                    act_s.step(f"T{f}", act.activation(hT[:, f, :], banks.bank(f"T{f}")[:, :], ACT.Identity,
                                                       bias=gb[:, f, 1:2], scale=gb[:, f, 0:1]))
                act_s.step("keep", act.activation(z_all[:, bass.ds(blk * 4, 4), :], z[k][:, :, :], ACT.Copy))
            blocks(act, body)

        @block.tensor
        def _(pe):
            pe_s.start(pe)
            pe.wait_ge(ld, 48)

            def body(blk, k, i):
                for f in range(NF):
                    d = banks.take(pe, f"T{f}", blk, ("dve", "z3", 0))
                    for t in range(4):
                        mm = pe.transpose(d[:, t * P:(t + 1) * P], z[k][:, t, f * P:(f + 1) * P],
                                          C["identf"][:, :])
                    pe_s.step(f"T{f}", mm)
                d = banks.take(pe, "log", blk, ("act", "T1", 0))
                for t in range(4):
                    for f in range(NF):
                        mm = pe.matmul(d[:, t * E:(t + 1) * E], hT[:, f, t * P:(t + 1) * P], wg[:, f, :],
                                       start=f == 0, stop=f == NF - 1)
                pe_s.step("log", mm)
            blocks(pe, body)


def route(nc, C, W, logits, z_all, exp_in, zero_fill, gather_at, gate):
    with Ctx(nc, "rt") as c:
        big = lambda n, dt=F32: c.sb(n, [P, NT, E], dt)
        G, key, pos, tot, run, tmp, one = (big(n) for n in ("G", "key", "pos", "tot", "run", "tmp", "one"))
        hot = [big("hot0"), big("hot1")]
        mask = big("mask", BF16)
        m1 = c.sb("m1", [P, NT], F32)
        pr = c.sb("pr", [P, 2, NT], F32)
        base = c.sb("base", [P, 2, NT], F32)
        keep = c.sb("keep", [P, 2, NT], F32)
        at = c.sb("at", [P, 2, NT], F32)
        scatter_at = c.sb("scatter_at", [P, 2, NT], U32)
        iota8 = c.sb("iota8", [P, 2, E], F32)
        cum, total = c.ps("cum", [P, NT * E]), c.ps("total", [P, NT * E])
        ld, ch, e_in, e_out, m_ready, counted, placed = (
            c.sem(n) for n in ("ld", "ch", "e_in", "e_out", "m_ready", "counted", "placed"))
        sent = c.sem("sent")
        block = c.block()
        wide = lambda a: a.unsqueeze(2).to_broadcast([P, NT, E])
        along = lambda a: a.unsqueeze(1).to_broadcast([P, NT, E])

        @block.sync
        def _(sp):
            sp.dma_start(iota8[:, :, :], W["iota8"]).then_inc(ld, 16)

        @block.scalar
        def _(act):
            act.wait_ge(e_in, 1)
            act.activation(G[:, :, :], logits[:, :, :], ACT.Exp).then_inc(e_out, 1)

        @block.tensor
        def _(pe):
            pe.wait_ge(m_ready, 1)
            m = mask[:, :, :].rearrange("p t e -> p (t e)")
            pe.matmul(cum[:, :], C["tri16"][:, :], m, start=True, stop=True)
            pe.matmul(total[:, :], C["ones16"][:, :], m, start=True, stop=True).then_inc(counted, 1)

        @block.vector
        def _(dve):
            link = Chain(dve, ch).link
            tt, ts, red = dve.tensor_tensor, dve.tensor_scalar, dve.tensor_reduce
            descending, index = iota8[:, 0, :], iota8[:, 1, :]
            link(red(m1[:, :], logits[:, :, :], AX.X, ALU.max))
            link(tt(logits[:, :, :], logits[:, :, :], wide(m1[:, :]), ALU.subtract))
            dve.nop().then_inc(e_in, 1)
            dve.wait_ge(e_out, 1)
            link(red(m1[:, :], G[:, :, :], AX.X, ALU.add))
            link(dve.reciprocal(m1[:, :], m1[:, :]))
            link(tt(G[:, :, :], G[:, :, :], wide(m1[:, :]), ALU.mult))
            dve.wait_ge(ld, 16)
            for r in range(2):
                g = gate[:, r, :]
                link(red(g, G[:, :, :], AX.X, ALU.max))
                link(tt(key[:, :, :], G[:, :, :], wide(g), ALU.is_equal))
                link(tt(key[:, :, :], key[:, :, :], along(descending), ALU.mult))
                link(red(m1[:, :], key[:, :, :], AX.X, ALU.max))
                link(tt(hot[r][:, :, :], key[:, :, :], wide(m1[:, :]), ALU.is_equal))
                if r == 0:
                    link(dve.scalar_tensor_tensor(out=G[:, :, :], in0=hot[0][:, :, :], scalar=-2.0,
                                                  in1=G[:, :, :], op0=ALU.mult, op1=ALU.add))
            link(tt(mask[:, :, :], hot[0][:, :, :], hot[1][:, :, :], ALU.add))
            dve.nop().then_inc(m_ready, 1)
            link(dve.memset(one[:, :, :], 1.0))
            dve.wait_ge(counted, 1)
            link(dve.tensor_copy(tot[:, :, :].rearrange("p t e -> p (t e)"), total[:, :]))
            for e in range(E):
                link(dve.tensor_tensor_scan(run[:, :, e], one[:, :, e], tot[:, :, e], 0.0,
                                            ALU.mult, ALU.add))
            link(tt(run[:, :, :], run[:, :, :], tot[:, :, :], ALU.subtract))
            link(tt(pos[:, :, :].rearrange("p t e -> p (t e)"),
                    run[:, :, :].rearrange("p t e -> p (t e)"), cum[:, :], ALU.add))
            link(ts(pos[:, :, :], pos[:, :, :], -1.0, None, ALU.add))
            for r in range(2):
                link(tt(tmp[:, :, :], hot[r][:, :, :], pos[:, :, :], ALU.mult))
                link(red(pr[:, r, :], tmp[:, :, :], AX.X, ALU.add))
                link(tt(tmp[:, :, :], hot[r][:, :, :], along(index), ALU.mult))
                link(red(base[:, r, :], tmp[:, :, :], AX.X, ALU.add))
            link(ts(base[:, :, :], base[:, :, :], float(CAP), None, ALU.mult))
            link(ts(keep[:, :, :], pr[:, :, :], float(CAP), None, ALU.is_lt))
            link(ts(at[:, :, :], keep[:, :, :], -4.0 * E * CAP, 4.0 * E * CAP, ALU.mult, ALU.add))
            link(tt(at[:, :, :], at[:, :, :], base[:, :, :], ALU.add))
            link(tt(at[:, :, :], at[:, :, :], pr[:, :, :], ALU.add))
            link(dve.tensor_copy(scatter_at[:, :, :], at[:, :, :]))
            dve.nop().then_inc(placed, 1)
            link(ts(pr[:, :, :], pr[:, :, :], float(CAP - 1), None, ALU.min))
            link(tt(pr[:, :, :], pr[:, :, :], base[:, :, :], ALU.add))
            link(dve.tensor_copy(gather_at[:, :, :], pr[:, :, :]))
            link(tt(gate[:, :, :], gate[:, :, :], keep[:, :, :], ALU.mult))

        @block.gpsimd
        def _(pool):
            pool.wait_ge(zero_fill, 16)
            pool.wait_ge(placed, 1)
            for t in range(NT):
                for r in range(2):
                    pool.indirect_dma_start(
                        out=exp_in[:, :],
                        out_offset=bass.IndirectOffsetOnAxis(ap=scatter_at[:, r, t:t + 1], axis=0),
                        in_=z_all[:, t, :], in_offset=None, bounds_check=E * CAP - 1,
                        oob_is_err=False).then_inc(sent, 16)
            pool.wait_ge(sent, 16 * 2 * NT)


def experts(nc, C, W, exp_in, exp_out):
    jobs = [(f"T{cb}{f}", "act", f"T{cb}{f}") for cb in range(2) for f in range(NF)]
    jobs += [(f"h0{f}", "act", f"h0{f}") for f in range(NFF)]
    jobs += [(f"h1{f}", "act", f"h1{f}") for f in range(NFF // 2)]
    jobs += [(f"y0{m}", "dve", f"y0{m}") for m in range(2)]
    jobs += [(f"h1{f}", "act", f"h1{f}") for f in range(NFF // 2, NFF)]
    jobs += [(f"y1{m}", "dve", f"y1{m}") for m in range(2)]
    with Ctx(nc, "ex") as c:
        xin = [c.sb(f"xin{k}", [P, NCT, D], F32) for k in range(2)]
        w1 = [c.sb(f"w1{k}", [P, NF, FF], F32) for k in range(2)]
        w2 = [c.sb(f"w2{k}", [P, NFF, D], F32) for k in range(2)]
        xT = c.sb("xT", [P, NF, CAP], F32)
        hT = [c.sb(f"hT{k}", [P, NFF, QB], F32) for k in range(2)]
        ot = c.sb("ot", [P, 2, 2, 2, D], F32)
        b1n = c.sb("b1n", [E * NFF, P], F32)
        b1 = c.sb("b1", [P, E * NFF], F32)
        b2 = c.sb("b2", [P, E, D], F32)
        gb = c.sb("gb", [P, NF, 2], F32)
        ld = [c.sem(f"ld{k}") for k in range(2)]
        w_ld, b_t, b_ready, stored = c.sem("w_ld"), c.sem("b_t"), c.sem("b_ready"), c.sem("stored")
        ot_free = c.sem("ot_free")
        held = c.sem("held")
        pe_s = Steps(c.sem("pe"), [j[0] for j in jobs])
        act_s = Steps(c.sem("act"), [j[0] for j in jobs if j[1] == "act"])
        dve_s = Steps(c.sem("dve"), [j[0] for j in jobs if j[1] == "dve"])
        banks = Banks(c, jobs, {"act": act_s, "dve": dve_s})
        block = c.block()

        def experts_loop(eng, body):
            with eng.Fori(0, E // 2) as i:
                for k in range(2):
                    body(i * 2 + k, k, i)

        @block.sync
        def _(sp):
            sp.dma_start(b1n[:, :], W["b1"].rearrange("e (f p) -> (e f) p", p=P)).then_inc(w_ld, 16)
            sp.dma_start(b2[:, :, :], W["b2"].unsqueeze(0).to_broadcast([P, E, D])).then_inc(w_ld, 16)
            with nc.allow_non_contiguous_dma(reason="a few hundred floats"):
                sp.dma_start(gb[:, :, 0], W["ln2_g"].rearrange("(c p) -> p c", p=P)).then_inc(w_ld, 16)
                sp.dma_start(gb[:, :, 1], W["ln2_b"].rearrange("(c p) -> p c", p=P)).then_inc(w_ld, 16)

            def body(e, k, i):
                pe_s.wait(sp, "y11", e - 2)
                sp.dma_start(xin[k][:, :, :], exp_in.rearrange("(e t p) d -> e p t d", e=E, p=P)[e]
                             ).then_inc(ld[k], 16)
                sp.dma_start(w1[k][:, :, :], W["W1"][e].rearrange("(c p) n -> p c n", p=P)).then_inc(ld[k], 16)
                sp.dma_start(w2[k][:, :, :], W["W2"][e].rearrange("(c p) n -> p c n", p=P)).then_inc(ld[k], 16)
            experts_loop(sp, body)

        @block.gpsimd
        def _(pool):
            rows = exp_out.rearrange("(e c m t p) d -> e c m p t d", e=E, c=2, m=2, p=P)

            def body(e, k, i):
                for cb in range(2):
                    for m in range(2):
                        dve_s.wait(pool, f"y{cb}{m}", e)
                        pool.dma_start(rows[e, cb, m], ot[:, cb, m, :, :]).then_inc(stored, 16)
                        pool.wait_ge(stored, e * 64 + (2 * cb + m + 1) * 16)
                        pool.nop().then_inc(ot_free, 1)
            pool.nop().then_inc(ot_free, 4)
            experts_loop(pool, body)

        @block.scalar
        def _(act):
            act_s.start(act)
            act.wait_ge(w_ld, 64)
            act.wait_ge(b_ready, 1)

            def body(e, k, i):
                for cb in range(2):
                    for f in range(NF):
                        pe_s.wait(act, f"T{cb}{f}", e)
                        act_s.step(f"T{cb}{f}", act.activation(
                            xT[:, f, cb * QB:(cb + 1) * QB], banks.bank(f"T{cb}{f}")[:, :], ACT.Identity,
                            bias=gb[:, f, 1:2], scale=gb[:, f, 0:1]))
                for cb in range(2):
                    for f in range(NFF):
                        pe_s.wait(act, f"h{cb}{f}", e)
                        act.nop().then_inc(held, 1)
                        act_s.step(f"h{cb}{f}", act.activation(
                            hT[cb][:, f, :], banks.bank(f"h{cb}{f}")[:, :], ACT.Gelu,
                            bias=b1[:, bass.ds(e * NFF + f, 1)]))
            experts_loop(act, body)

        @block.vector
        def _(dve):
            dve.wait_ge(b_t, 1)
            dve.tensor_copy(b1[:, :], banks.banks[0][:, 0:E * NFF]).then_inc(b_ready, 1)
            dve.wait_ge(b_ready, 1)
            dve_s.start(dve)
            dve.wait_ge(w_ld, 64)

            def body(e, k, i):
                for cb in range(2):
                    for m in range(2):
                        dve.wait_ge(ot_free, e * 4 + 2 * cb + m + 1)
                        pe_s.wait(dve, f"y{cb}{m}", e)
                        dve_s.step(f"y{cb}{m}", dve.tensor_tensor(
                            ot[:, cb, m, :, :],
                            banks.bank(f"y{cb}{m}")[:, :].rearrange("p (t d) -> p t d", t=2),
                            b2[:, bass.ds(e, 1), :].to_broadcast([P, 2, D]), ALU.add))
            experts_loop(dve, body)

        @block.tensor
        def _(pe):
            pe.wait_ge(w_ld, 64)
            pe.transpose(banks.banks[0][:, 0:E * NFF], b1n[:, :], C["identf"][0:E * NFF, 0:E * NFF]
                         ).then_inc(b_t, 1)
            pe.wait_ge(b_ready, 1)
            pe_s.start(pe)

            def body(e, k, i):
                pe.wait_ge(ld[k], i * 48 + 48)

                def hidden(cb, fs):
                    for f in fs:
                        d = banks.take(pe, f"h{cb}{f}", e, ("act", f"T{cb}1", 0))
                        for n in range(NF):
                            mm = pe.matmul(d[:, :], w1[k][:, n, f * P:(f + 1) * P],
                                           xT[:, n, cb * QB:(cb + 1) * QB], start=n == 0, stop=n == NF - 1)
                        pe_s.step(f"h{cb}{f}", mm)

                def result(cb):
                    for m in range(2):
                        d = banks.take(pe, f"y{cb}{m}", e, ("act", f"h{cb}{NFF - 1}", 0))
                        for t in range(2):
                            for n in range(NFF):
                                mm = pe.matmul(d[:, t * D:(t + 1) * D],
                                               hT[cb][:, n, (2 * m + t) * P:(2 * m + t + 1) * P],
                                               w2[k][:, n, :], start=n == 0, stop=n == NFF - 1)
                        pe_s.step(f"y{cb}{m}", mm)

                for cb in range(2):
                    for f in range(NF):
                        d = banks.take(pe, f"T{cb}{f}", e)
                        for t in range(4):
                            mm = pe.transpose(d[:, t * P:(t + 1) * P],
                                              xin[k][:, cb * 4 + t, f * P:(f + 1) * P], C["identf"][:, :])
                        pe_s.step(f"T{cb}{f}", mm)
                hidden(0, range(NFF))
                hidden(1, range(NFF // 2))
                result(0)
                hidden(1, range(NFF // 2, NFF))
                result(1)
            experts_loop(pe, body)


def combine(nc, C, x, s_out, exp_out, gather_at, gate, x_all, stats):
    with Ctx(nc, "cb") as c:
        rows = c.sb("rows", [P, 4, 2, D], F32)
        xs = [c.sb(f"xs{k}", [P, 4, D], F32) for k in range(2)]
        ss = [c.sb(f"ss{k}", [P, 4, D], F32) for k in range(2)]
        f = c.sb("f", [P, 4, D], F32)
        got = [c.sem(f"got{t}") for t in range(4)]
        ld = [c.sem(f"ld{k}") for k in range(2)]
        dve_s = Steps(c.sem("dve"), [f"{s}{t}" for t in range(4) for s in ("one", "two")]
                      + [f"{s}{t}" for t in range(4) for s in ("mul", "add", "stat")])
        act_s = Steps(c.sem("act"), [f"silu{t}" for t in range(4)])
        block = c.block()

        @block.sync
        def _(sp):
            def body(blk, k, i):
                dve_s.wait(sp, "add3", blk - 2)
                sp.dma_start(xs[k][:, :, :], x.rearrange("b (n p) d -> p (b n) d", p=P)[
                    :, bass.ds(blk * 4, 4), :]).then_inc(ld[k], 16)
                sp.dma_start(ss[k][:, :, :], s_out[bass.ds(blk * 4, 4), :, :].rearrange("t p d -> p t d")
                             ).then_inc(ld[k], 16)
            blocks(sp, body)

        @block.gpsimd
        def _(pool):
            for n in range(NT):
                t = n % 4
                dve_s.wait(pool, f"two{t}", n // 4 - 1)
                for r in range(2):
                    pool.indirect_dma_start(
                        out=rows[:, t, r, :], out_offset=None, in_=exp_out[:, :],
                        in_offset=bass.IndirectOffsetOnAxis(ap=gather_at[:, r, n:n + 1], axis=0)
                    ).then_inc(got[t], 16)

        @block.scalar
        def _(act):
            act_s.start(act)

            def body(blk, k, i):
                for t in range(4):
                    dve_s.wait(act, f"two{t}", blk)
                    act_s.step(f"silu{t}", act.activation(f[:, t, :], f[:, t, :], ACT.Silu))
            blocks(act, body)

        @block.vector
        def _(dve):
            dve_s.start(dve)

            def body(blk, k, i):
                for t in range(4):
                    n = blk * 4 + t
                    x1 = x_all[:, bass.ds(n, 1), :].rearrange("p a d -> p (a d)")
                    dve.wait_ge(got[t], blk * 32 + 32)
                    dve_s.wait(dve, f"mul{t}", blk - 1)
                    dve_s.step(f"one{t}", dve.scalar_tensor_tensor(
                        out=f[:, t, :], in0=rows[:, t, 0, :],
                        scalar=gate[:, 0, bass.ds(n, 1)], in1=x1, op0=ALU.mult, op1=ALU.add))
                    dve_s.wait(dve, f"one{t}", blk)
                    dve_s.step(f"two{t}", dve.scalar_tensor_tensor(
                        out=f[:, t, :], in0=rows[:, t, 1, :],
                        scalar=gate[:, 1, bass.ds(n, 1)], in1=f[:, t, :], op0=ALU.mult, op1=ALU.add))
                dve.wait_ge(ld[k], i * 32 + 32)
                for t in range(4):
                    n = blk * 4 + t
                    x2 = x_all[:, bass.ds(n, 1), :].rearrange("p a d -> p (a d)")
                    act_s.wait(dve, f"silu{t}", blk)
                    dve_s.step(f"mul{t}", dve.tensor_tensor(f[:, t, :], f[:, t, :], ss[k][:, t, :], ALU.mult))
                    dve_s.wait(dve, f"mul{t}", blk)
                    dve_s.step(f"add{t}", dve.tensor_tensor(x2, f[:, t, :], xs[k][:, t, :], ALU.add))
                    dve_s.wait(dve, f"add{t}", blk)
                    dve_s.step(f"stat{t}", dve.bn_stats(stats[:, n, :], x2))
            blocks(dve, body)


def project_second(nc, C, W, x_all, mean, rstd, scale_qk, qk_out, v_out, g_all):
    jobs = [("T0", "act", "T0"), ("T1", "act", "T1")]
    jobs += [(f"{s}{f}", "dve", f"lo {s}{f}") for s in "qk" for f in range(4)]
    jobs += [(f"v{t}", "act", f"v{t}") for t in range(4)]
    jobs += [(f"y{m}", "dve", f"y{m}") for m in range(2)]
    act_names = ["T0", "T1"] + [f"hi {s}{f}" for s in "qk" for f in range(4)]
    act_names += [f"v{t}" for t in range(4)] + ["silu"]
    dve_names = [f"z{t}" for t in range(4)] + [f"lo {s}{f}" for s in "qk" for f in range(4)] + ["y0", "y1"]
    with Ctx(nc, "p2") as c:
        w = c.sb("w", [P, 3, NF, 2 * D], F32)
        bias = c.sb("bias", [P, D], F32)
        z = [c.sb(f"z{k}", [P, 4, D], F32) for k in range(2)]
        xT = c.sb("xT", [P, NF, QB], F32)
        parts = c.sb("parts", [P, 2, 2, 4, QB], F16)
        vt = c.sb("vt", [P, 4, 2 * D], F32)
        yt = c.sb("yt", [P, 4, D], F32)
        w_ld, part_out, vt_out = c.sem("w_ld"), c.sem("part_out"), c.sem("vt_out")
        held = c.sem("held")
        pe_s = Steps(c.sem("pe"), [j[0] for j in jobs])
        act_s = Steps(c.sem("act"), act_names)
        dve_s = Steps(c.sem("dve"), dve_names)
        banks = Banks(c, jobs, {"act": act_s, "dve": dve_s})
        block = c.block()

        @block.sync
        def _(sp):
            for n, name in enumerate(("Wq", "Wk", "Wv")):
                sp.dma_start(w[:, n], W[name].rearrange("(c p) n -> p c n", p=P)).then_inc(w_ld, 16)
            sp.dma_start(bias[:, :], W["bias"].unsqueeze(0).to_broadcast([P, D])).then_inc(w_ld, 16)

            def body(blk, k, i):
                b, j = i // 2, (i % 2) * 2 + k
                dve_s.wait(sp, "lo k3", blk)
                for side in range(2):
                    for lower in range(2):
                        dst = qk_out[side][lower].rearrange("(b g) h d t -> b g (h d) t", b=B)
                        sp.dma_start(dst[b, :, :, bass.ds(j * QB, QB)].rearrange("g p t -> p g t"),
                                     parts[:, side, lower, :, :]).then_inc(part_out, 16)
                act_s.wait(sp, "v3", blk)
                for g in range(4):
                    sp.dma_start(v_out[b, g, :, bass.ds(j * 4, 4), :],
                                 vt[:, :, g * P:(g + 1) * P]).then_inc(vt_out, 16)
            blocks(sp, body)
            sp.wait_ge(part_out, 1 + 64 * NB)
            sp.wait_ge(vt_out, 1 + 64 * NB)

        @block.scalar
        def _(act):
            act_s.start(act)
            act.nop().then_inc(vt_out, 1)
            act.nop().then_inc(part_out, 1)

            def body(blk, k, i):
                for f in range(NF):
                    pe_s.wait(act, f"T{f}", blk)
                    act_s.step(f"T{f}", act.activation(xT[:, f, :], banks.bank(f"T{f}")[:, :], ACT.Copy))
                act.wait_ge(part_out, blk * 64 + 1)
                for side, s in enumerate("qk"):
                    for f in range(4):
                        pe_s.wait(act, f"{s}{f}", blk)
                        act_s.step(f"hi {s}{f}", act.activation(
                            parts[:, side, 0, f, :], banks.bank(f"{s}{f}")[:, :], ACT.Copy,
                            scale=scale_qk[side]))
                act.wait_ge(vt_out, blk * 64 + 1)
                for t in range(4):
                    pe_s.wait(act, f"v{t}", blk)
                    act_s.step(f"v{t}", act.activation(vt[:, t, :], banks.bank(f"v{t}")[:, :], ACT.Copy))
                dve_s.wait(act, "y1", blk)
                act.nop().then_inc(held, 1)
                act_s.step("silu", act.activation(g_all[:, bass.ds(blk * 4, 4), :], yt[:, :, :], ACT.Silu))
            blocks(act, body)

        @block.vector
        def _(dve):
            dve_s.start(dve)
            dve.wait_ge(w_ld, 64)

            def body(blk, k, i):
                pe_s.wait(dve, "T1", blk - 2)
                for t in range(4):
                    n = blk * 4 + t
                    dve_s.step(f"z{t}", dve.tensor_scalar(
                        z[k][:, t, :], x_all[:, bass.ds(n, 1), :].rearrange("p a d -> p (a d)"),
                        mean[:, bass.ds(n, 1)], rstd[:, bass.ds(n, 1)], ALU.subtract, ALU.mult))
                for side, s in enumerate("qk"):
                    for f in range(4):
                        act_s.wait(dve, f"hi {s}{f}", blk)
                        dve_s.step(f"lo {s}{f}", dve.scalar_tensor_tensor(
                            out=parts[:, side, 1, f, :], in0=banks.bank(f"{s}{f}")[:, :],
                            scalar=scale_qk[side], in1=parts[:, side, 0, f, :], op0=ALU.mult,
                            op1=ALU.subtract))
                act_s.wait(dve, "silu", blk - 1)
                for m in range(2):
                    pe_s.wait(dve, f"y{m}", blk)
                    dve_s.step(f"y{m}", dve.tensor_tensor(
                        yt[:, 2 * m:2 * m + 2, :], banks.bank(f"y{m}")[:, :].rearrange("p (t d) -> p t d", t=2),
                        bias[:, :].unsqueeze(1).to_broadcast([P, 2, D]), ALU.add))
            blocks(dve, body)

        @block.tensor
        def _(pe):
            pe_s.start(pe)
            pe.wait_ge(w_ld, 64)

            def body(blk, k, i):
                for f in range(NF):
                    d = banks.take(pe, f"T{f}", blk, ("dve", "z3", 0))
                    for t in range(4):
                        mm = pe.transpose(d[:, t * P:(t + 1) * P], z[k][:, t, f * P:(f + 1) * P],
                                          C["identf"][:, :])
                    pe_s.step(f"T{f}", mm)
                for side, s in enumerate("qk"):
                    for f in range(4):
                        d = banks.take(pe, f"{s}{f}", blk, ("act", "T1", 0))
                        for n in range(NF):
                            mm = pe.matmul(d[:, :], w[:, side, n, f * P:(f + 1) * P], xT[:, n, :],
                                           start=n == 0, stop=n == NF - 1)
                        pe_s.step(f"{s}{f}", mm)
                for t in range(4):
                    d = banks.take(pe, f"v{t}", blk)
                    for n in range(NF):
                        mm = pe.matmul(d[:, :], xT[:, n, t * P:(t + 1) * P], w[:, 2, n, :],
                                       start=n == 0, stop=n == NF - 1)
                    pe_s.step(f"v{t}", mm)
                for m in range(2):
                    d = banks.take(pe, f"y{m}", blk)
                    for t in range(2):
                        for n in range(NF):
                            mm = pe.matmul(d[:, t * D:(t + 1) * D],
                                           xT[:, n, (2 * m + t) * P:(2 * m + t + 1) * P],
                                           C["w_ffn"][:, n, :], start=n == 0, stop=n == NF - 1)
                    pe_s.step(f"y{m}", mm)
            blocks(pe, body)


def finish(nc, C, W, att, inverse, x_all, g_all, out):
    jobs = [(f"x{t}", "dve", f"mul{t}") for t in range(4)]
    dve_names = [f"{s}{t}" for t in range(4) for s in ("mul", "add")]
    with Ctx(nc, "fi") as c:
        w = c.sb("w", [P, 4, D], F32)
        o = [c.sb(f"o{k}", [P, 4, D], F32) for k in range(2)]
        w_ld = c.sem("w_ld")
        stored = [c.sem(f"stored{k}") for k in range(2)]
        pe_s = Steps(c.sem("pe"), [j[0] for j in jobs], credit=NB // B)
        dve_s = Steps(c.sem("dve"), dve_names)
        banks = Banks(c, jobs, {"dve": dve_s}, ring=4)
        attended = Attended(c, att, inverse, pe_s, "x3")
        block = c.block()

        @block.sync
        def _(sp):
            sp.dma_start(w[:, :, :], W["Wo"].rearrange("(g p) n -> p g n", p=P)).then_inc(w_ld, 16)

            blocks(sp, lambda blk, k, i: attended.load(sp, blk, k, i), NB // B)

        @block.gpsimd
        def _(pool):
            attended.divide(pool)

        @block.scalar
        def _(act):
            def body(blk, k, i):
                dve_s.wait(act, "add3", blk)
                act.dma_start(out.rearrange("b (n p) d -> p (b n) d", p=P)[:, bass.ds(blk * 4, 4), :],
                              o[k][:, :, :]).then_inc(stored[k], 16)
            blocks(act, body)
            for k in range(2):
                act.wait_ge(stored[k], 1 + 16 * NB // 2)

        @block.vector
        def _(dve):
            dve_s.start(dve)
            for k in range(2):
                dve.nop().then_inc(stored[k], 1)

            def body(blk, k, i):
                dve.wait_ge(stored[k], i * 16 + 1)
                for t in range(4):
                    n = bass.ds(blk * 4 + t, 1)
                    flat = lambda a: a.rearrange("p a d -> p (a d)")
                    pe_s.wait(dve, f"x{t}", blk)
                    dve_s.step(f"mul{t}", dve.tensor_tensor(o[k][:, t, :], flat(g_all[:, n, :]),
                                                            banks.bank(f"x{t}")[:, 0:D], ALU.mult))
                    dve_s.wait(dve, f"mul{t}", blk)
                    dve_s.step(f"add{t}", dve.tensor_tensor(o[k][:, t, :], o[k][:, t, :],
                                                            flat(x_all[:, n, :]), ALU.add))
            blocks(dve, body)

        @block.tensor
        def _(pe):
            pe_s.start(pe)
            pe.wait_ge(w_ld, 16)

            def body(blk, k, i):
                attended.wait(pe, blk)
                for t in range(4):
                    d = banks.take(pe, f"x{t}", blk)
                    for g in range(4):
                        mm = pe.matmul(d[:, 0:D], attended.a[k][:, g, t * P:(t + 1) * P], w[:, g, :],
                                       start=g == 0, stop=g == 3)
                    pe_s.step(f"x{t}", mm)
            blocks(pe, body, NB // B)


def build(nc, W, x, out):
    dram = lambda name, shape, dt: nc.dram_tensor(name, shape, dt, kind="Internal").ap()
    exp_in = dram("exp_in", [E * CAP, D], F32)
    exp_out = dram("exp_out", [E * CAP, D], F32)
    s_out = dram("s_out", [NT, P, D], F32)
    att = [dram(f"att{n}", [GROUPS, P, T], F32) for n in range(2)]
    sums = [att[0].rearrange("g (h r) t -> g h r t", r=32)[:, :, 16, :], dram("sums1", [GROUPS, HG, T], F32)]
    inverse = [dram(f"inverse{n}", [GROUPS * HG, T], F32) for n in range(2)]
    v = [dram(f"v{n}", [B, 4, P, NKC, P], F32) for n in range(2)]
    qk = [[[dram(f"{s}{part}{n}", [GROUPS, HG, hd, T], F16) for part in ("hi", "lo")] for s in "qk"]
          for n, hd in ((0, 16), (1, 32))]

    def attention(c, n, hd, scores):
        softmax_attention(nc, f"at{n}", hd, c, *qk[n][0], *qk[n][1], v[n].rearrange("b g p c n -> (b g) p c n"),
                          scores[n][:, 2:3], att[n], sums[n])
        invert_sums(nc, f"iv{n}", sums[n].rearrange("g h t -> (g h) t"), inverse[n])

    with Ctx(nc, "all") as c:
        C = constants(nc, c, W["shift_rows"])
        x_all = c.sb("x_all", [P, NT, D], F32)
        score = [c.sb(f"score{n}", [P, 3], F32) for n in range(2)]
        mean = c.sb("mean", [P, NT], F32)
        rstd = c.sb("rstd", [P, NT], F32)
        stats = c.sb("stats", [P, NT, 6], F32)
        gate = c.sb("gate", [P, 2, NT], F32)
        gather_at = c.sb("gather_at", [P, 2, NT], U32)
        zeros = c.sb("zeros", [P, D], F32)
        zero_fill = c.sem("zero_fill")
        scales = lambda n: [score[n][:, 0:1], score[n][:, 1:2]]

        prepare(nc, C, W, score, zeros, exp_in, zero_fill)
        normalize_input(nc, x, x_all, mean, rstd)
        with Ctx(nc, "lin") as lin:
            qf_all = lin.sb("qf_all", [P, NF, B * T], F32)
            kv_sum = lin.sb("kv_sum", [P, B * NF, P + 8], F32)
            project_first(nc, C, W, x_all, mean, rstd, qf_all, kv_sum, scales(0), qk[0], v[0])
            linear_out(nc, C, W, qf_all, kv_sum, s_out)
        attention(C, 0, 16, score)
        after_attention(nc, C, W, att[0], inverse[0], x_all, stats)
        row_statistics(nc, "rs1", stats, mean, rstd)
        with Ctx(nc, "moe") as moe:
            z_all = moe.sb("z_all", [P, NT, D], F32)
            logits = moe.sb("logits", [P, NT, E], F32)
            gate_logits(nc, C, W, x_all, mean, rstd, z_all, logits)
            route(nc, C, W, logits, z_all, exp_in, zero_fill, gather_at, gate)
        experts(nc, C, W, exp_in, exp_out)
        combine(nc, C, x, s_out, exp_out, gather_at, gate, x_all, stats)
        row_statistics(nc, "rs2", stats, mean, rstd)
        with Ctx(nc, "g") as last:
            g_all = last.sb("g_all", [P, NT, D], F32)
            project_second(nc, C, W, x_all, mean, rstd, scales(1), qk[1], v[1], g_all)
            attention(C, 1, 32, score)
            finish(nc, C, W, att[1], inverse[1], x_all, g_all, out)


_NAMES = {"L0_attn_x": "x", "L0_attn_W_qkv": "W_qkv", "L0_attn_W_out": "W_out", "L0_ffn_ln1_g": "ln1_g",
          "L0_ffn_ln1_b": "ln1_b", "L0_ffn_Wqkv": "ffn_Wqkv", "L0_ffn_Wproj": "Wproj",
          "L0_ffn_ln2_g": "ln2_g", "L0_ffn_ln2_b": "ln2_b", "L0_ffn_Wgate": "Wgate", "L0_ffn_W1": "W1",
          "L0_ffn_b1": "b1", "L0_ffn_W2": "W2", "L0_ffn_b2": "b2", "L1_attn_Wq": "Wq",
          "L1_attn_Wk": "Wk", "L1_attn_Wv": "Wv", "L1_attn_Wo": "Wo", "L1_ffn_kernel": "kernel",
          "L1_ffn_bias": "bias", "L1_ffn_a": "a", "L1_ffn_b": "b"}


def tables():
    import numpy as np
    t = np.arange(2048, dtype=np.float32)
    power = np.arange(0, 16, 2, dtype=np.float32) / np.float32(16)
    ang = {b: (t[:, None] * (np.float32(1) / np.float32(b) ** power)[None, :]).astype(np.float32)
           for b in (500000.0, 10000.0)}
    rows = lambda a: np.ascontiguousarray(np.tile(a, (1, 16)).T).astype(np.float32)
    tiles = lambda a: np.ascontiguousarray(a.reshape(16, 128, 8).transpose(1, 0, 2))
    rotate = np.zeros((128, 128), np.float32)
    for m in range(128):
        rotate[m + 8 if m % 16 < 8 else m - 8, m] = -1.0 if m % 16 < 8 else 1.0
    lin, soft = ang[500000.0], ang[10000.0]
    heads = np.zeros((128, 136), np.float32)
    for r in range(128):
        heads[r, r // 16 * 16:r // 16 * 16 + 16] = 1.0
        heads[r, 128 + r // 16] = 1.0
    iota8 = np.tile(np.stack([8 - np.arange(8), np.arange(8)]).astype(np.float32)[None], (128, 1, 1))
    shift_rows = np.zeros((2 * HG, HG, T), np.float16)
    for h in range(HG):
        shift_rows[2 * h:2 * h + 2, h] = MSHIFT
    return {"heads": heads, "iota8": iota8, "shift_rows": shift_rows,
            "cos_q": rows(np.cos(lin)) * np.float32(0.25), "sin_q": rows(np.sin(lin)) * np.float32(0.25),
            "cos_f": rows(np.cos(soft)), "sin_f": rows(np.sin(soft)),
            "cos_k": tiles(np.cos(lin)), "sin_k": tiles(np.sin(lin)), "rotate": rotate}


def kernel(**inputs):
    import numpy as _np
    import concourse.bacc as _bacc
    from concourse.bass_utils import run_bass_kernel_spmd as _run

    nc = _bacc.Bacc("TRN2", target_bir_lowering=False, num_devices=1)
    given = {short: _np.ascontiguousarray(inputs[name]) for name, short in _NAMES.items()}
    given.update({name: _np.ascontiguousarray(a) for name, a in tables().items()})
    arrays, W = {}, {}
    for name, a in given.items():
        arrays[f"in_{name}"] = a
        W[name] = nc.dram_tensor(f"in_{name}", a.shape, mybir.dt.from_np(a.dtype), kind="ExternalInput").ap()
    out = nc.dram_tensor("out_0", (B, T, D), F32, kind="ExternalOutput").ap()
    build(nc, W, W["x"], out)
    r = _run(nc, [arrays], core_ids=[0])
    return r.results[0]["out_0"]
```

```python
import concourse.bass as bass
from concourse import mybir
from contextlib import ExitStack

F32 = mybir.dt.float32
F16 = mybir.dt.float16
BF16 = mybir.dt.bfloat16
U32 = mybir.dt.uint32
ALU = mybir.AluOpType
ACT = mybir.ActivationFunctionType
AX = mybir.AxisListType

P = 128
B, T, D, H = 2, 2048, 256, 16
GROUPS = 8
HG = 4
QB = 512
NQB = T // QB
NKC = T // P
MROW = 96
NROW = MROW + 2 * HG
MSHIFT = 2.0 ** 15


class Ctx:

    def __init__(self, nc, tag):
        self.nc, self.tag, self.stack = nc, tag, ExitStack()

    def __enter__(self):
        self.stack.__enter__()
        return self

    def __exit__(self, *a):
        return self.stack.__exit__(*a)

    def sb(self, name, shape, dt):
        return self.stack.enter_context(self.nc.sbuf_tensor(f"{self.tag}_{name}", shape, dt))

    def ps(self, name, shape, dt=F32):
        return self.stack.enter_context(self.nc.psum_tensor(f"{self.tag}_{name}", shape, dt))

    def sem(self, name):
        return self.stack.enter_context(self.nc.semaphore(f"{self.tag}_{name}"))

    def block(self):
        return self.stack.enter_context(self.nc.Block())


def attention_schedule(sums_apart, st_heads, st_slots, s_slots, ahead_share=0.02):
    order = [3, 2, 1, 0]

    def pass1(g, u):
        items = []
        for qt in range(4):
            for h in range(HG):
                for j in range(u + 1):
                    width = QB if j < u else (qt + 1) * P
                    items.append(("S", (g, u), qt, h, j, width))
        return items

    def stream(units):
        out, late = [], None
        for g, u in units:
            for n, it in enumerate(pass1(g, u)):
                out.append(it)
                if late and n == 3:
                    out.append(("T", late))
                    late = None
            out.append(("M", (g, u)))
            late = (g, u)
        out.append(("T", late))
        return out

    prologue = stream([(0, order[0])])
    ahead = stream([(0, u) for u in order[1:]] + [(1, u) for u in order] + [(2, order[0])])
    steps = [((g, u), kc) for g in range(2) for u in order for kc in range(4 * u + 4)]
    width2 = lambda s: QB - max(0, s[1] - 4 * s[0][1]) * P
    parts = HG // st_heads
    pairs = [(s, part) for s in steps for part in range(parts)]

    LATENCY, COLUMN = 180, 0.417
    pe_time = {"S": lambda ev: ev[5] * COLUMN + (50 if ev[4] == ev[1][1] else 0),
               "T": lambda ev: 100}
    dve_time = {"S": lambda ev: ev[5] * 1.04 + 65, "T": lambda ev: 1250, "M": lambda ev: 400}
    cost1 = lambda ev: dve_time[ev[0]](ev)
    total1, total2 = sum(map(cost1, ahead)), sum(map(width2, steps)) * parts
    done1 = done2 = 0
    pe = dve = act = 0.0
    slot_free = [0.0] * s_slots
    st_free = [0.0] * st_slots
    acc_free, sums_due = 0.0, []
    exp_end, pv_end, row_at = [], [], {(0, order[0]): 0.0}
    at = n_slot = n_pair = n_quad = 0
    made = 0.0
    body = []
    ring = 3
    while at < len(ahead) or n_pair < len(pairs) or n_quad < len(steps):
        choice = []
        if at < len(ahead):
            ready = slot_free[n_slot % s_slots] + LATENCY
            if ahead[at][0] == "T":
                ready = max(ready, made + LATENCY)
            if n_pair == len(pairs) or done1 / total1 <= done2 / total2 + ahead_share:
                patience = 600 if done1 / total1 < done2 / total2 else 0
                choice.append((max(pe, ready) - patience, 0, "S", max(pe, ready)))
        if n_pair < len(pairs):
            s, pair = pairs[n_pair]
            if s[0] in row_at:
                quad = n_pair // parts
                ready = max(st_free[n_pair % st_slots], row_at[s[0]]) + LATENCY
                if quad - n_quad < 2:
                    choice.append((max(pe, ready), 1, "ST", max(pe, ready)))
            elif not any(c[2] == "S" for c in choice):
                ready = max(pe, slot_free[n_slot % s_slots] + LATENCY)
                choice.append((ready, 0, "S", ready))
        if n_quad < len(steps) and parts * (n_quad + 1) <= n_pair and not (
                steps[n_quad][1] == 0 and sums_due):
            ready = exp_end[parts * (n_quad + 1) - 1] + LATENCY
            if steps[n_quad][1] == 0:
                ready = max(ready, acc_free + LATENCY)
            choice.append((max(pe, ready), 2, "PV", max(pe, ready)))
        _, _, kind, start = min(choice)
        if kind == "S":
            ev = ahead[at]
            at += 1
            body.append(ev)
            done1 += cost1(ev)
            pe = start + pe_time[ev[0]](ev)
            dve = max(dve, pe + LATENCY) + dve_time[ev[0]](ev)
            slot_free[n_slot % s_slots] = dve
            n_slot += 1
            if ev[0] == "T":
                row_at[ev[1]] = dve
            if at < len(ahead) and ahead[at][0] == "M":
                body.append(ahead[at])
                dve += dve_time["M"](ahead[at])
                done1 += cost1(ahead[at])
                made = dve
                at += 1
        elif kind == "ST":
            s, pair = pairs[n_pair]
            w = width2(s)
            body.append(("ST",) + s + (pair,))
            pe = start + st_heads * (w * COLUMN + (50 if s[1] >= 4 * s[0][1] else 0))
            needs = pv_end[n_pair // parts - ring] if n_pair // parts >= ring else 0.0
            act = max(act, pe + LATENCY, needs + LATENCY) + st_heads * w * 0.83 + 150
            st_free[n_pair % st_slots] = act
            exp_end.append(act)
            if sums_due:
                act = max(act, sums_due.pop(0) + LATENCY) + (1300 if sums_apart else 650)
                acc_free = act
            n_pair += 1
            done2 += w
        else:
            s = steps[n_quad]
            body.append(("PV",) + s)
            pe = start + (width2(s) * COLUMN * 4 + 80) * (2 if sums_apart else 1)
            pv_end.append(pe)
            n_quad += 1
            if s[1] == 4 * s[0][1] + 3:
                body.append(("EV", s[0]))
                sums_due.append(pe)
    return prologue, body


def softmax_attention(nc, tag, hd, C, q_hi, q_lo, k_hi, k_lo, v, scale, out, sums):
    sums_apart = hd == 32
    st_heads, st_slots = (1, 3) if sums_apart else (2, 2)
    st_parts = HG // st_heads
    S_SLOTS = 3
    prologue, body = attention_schedule(sums_apart, st_heads, st_slots, S_SLOTS)
    n_items = sum(e[0] in ("S", "T") for e in body)
    p_items = sum(e[0] in ("S", "T") for e in prologue)
    n_pairs = sum(e[0] == "ST" for e in body)
    n_quads = sum(e[0] == "PV" for e in body)
    stores = 32 if sums_apart else 16
    LOADS = 7 * 16
    last_unit_of_group = (3, 2, 1, 0)[-1]

    def slot(n, of, ring):
        return (n % of) % ring

    def previous(n, of, ring):
        m = n - 1
        while slot(m, of, ring) != slot(n, of, ring):
            m -= 1
        return m

    with Ctx(nc, tag) as c:
        QT = [c.sb(f"qT{k}", [P, HG, T], F16) for k in range(2)]
        KT = [c.sb(f"kT{k}", [P, HG, T], F16) for k in range(2)]
        V = [c.sb(f"v{k}", [P, NKC, HG * 32], F32) for k in range(2)]
        NP_RING = 6
        probs = c.sb("probs", [P, NP_RING, 2, QB], F32)
        part = c.sb("part", [P, 2, 4 * HG, NQB], F32)
        rowmax = c.sb("rowmax", [P, 2, 4 * HG], F32)
        shift = c.sb("shift", [P, 2, 4 * HG, 2], F16)
        otile = c.sb("otile", [P, 2, QB], F32)
        stile = c.sb("stile", [P, 2, QB], F32) if sums_apart else None

        st_ps = [c.ps(f"st{k}", [P, st_heads, QB]) for k in range(st_slots)]
        s_ps = [c.ps(f"s{k}", [P, QB]) for k in range(S_SLOTS)]
        acc_ps = [c.ps(f"acc{k}", [P, QB]) for k in range(2 if sums_apart else 1)]

        ld = [c.sem(f"ld{k}") for k in range(2)]
        init = c.sem("init")
        zeroed = [c.sem(f"zeroed{k}") for k in range(2)]
        item_ready = c.sem("item_ready")
        item_free = c.sem("item_free")
        max_done = c.sem("max_done")
        hi_done = c.sem("hi_done")
        shift_ready = c.sem("shift_ready")
        row_ready = c.sem("row_ready")
        st_ready = c.sem("st_ready")
        exp_done = c.sem("exp_done")
        pv_done = c.sem("pv_done")
        acc_ready = c.sem("acc_ready")
        out_ready = c.sem("out_ready")
        group_done = c.sem("group_done")
        stored = c.sem("stored")
        tile_free = c.sem("tile_free")
        block = c.block()

        def load(eng, g, k):
            rows = [(QT, q_hi, 0), (QT, q_lo, 1), (QT, q_hi, 2),
                    (KT, k_hi, 0), (KT, k_hi, 1), (KT, k_lo, 2)]
            for dst, src, r in rows:
                eng.dma_start(dst[k][r * hd:(r + 1) * hd, :, :],
                              src[g].rearrange("h d t -> d h t")).then_inc(ld[k], 16)
            eng.dma_start(V[k][:, :, :], v[g]).then_inc(ld[k], 16)

        @block.sync
        def _(sp):
            for k in range(2):
                sp.dma_start(KT[k][MROW:NROW, :, :], C["shift_rows"]).then_inc(init, 16)
            if hd == 16:
                sp.wait_ge(zeroed[0], 2)
            load(sp, 0, 0)
            if hd == 16:
                sp.wait_ge(zeroed[1], 2)
            with sp.Fori(0, GROUPS // 2) as i:
                sp.wait_ge(group_done, i * 2 + 1)
                load(sp, i * 2 + 1, 1)
                sp.wait_ge(group_done, i * 2 + 2)
                load(sp, (i * 2 + 2) % GROUPS, 0)
            sp.wait_ge(ld[0], LOADS * (GROUPS // 2 + 1))

        @block.gpsimd
        def _(pool):
            if hd == 16:
                for k in range(2):
                    pool.memset(KT[k][0:MROW, :, :].bitcast(U32), 0).then_inc(zeroed[k], 1)
            n = 0
            pool.nop().then_inc(tile_free, 2)
            with pool.Fori(0, GROUPS // 2) as i:
                for ev in body:
                    if ev[0] != "EV":
                        continue
                    g, u = ev[1]
                    pool.wait_ge(out_ready, i * 8 + n + 2)
                    pool.dma_start(out[i * 2 + g, :, u * QB:(u + 1) * QB],
                                   otile[:, n % 2, :]).then_inc(stored, 16)
                    if sums_apart:
                        pool.dma_start(sums[i * 2 + g, :, u * QB:(u + 1) * QB],
                                       stile[0:P:32, n % 2, :]).then_inc(stored, 16)
                    n += 1
                    pool.wait_ge(stored, (i * 8 + n) * stores)
                    pool.nop().then_inc(tile_free, 1)

        @block.scalar
        def _(act):
            act.nop().then_inc(exp_done, st_slots)
            act.nop().then_inc(out_ready, 1)
            with act.Fori(0, GROUPS // 2) as i:
                n, v2, ended = 0, 0, 0

                def take_sums():
                    act.wait_ge(acc_ready, i * 8 + v2 + 1)
                    act.wait_ge(tile_free, i * 8 + v2 + 1)
                    ins = act.activation(otile[:, v2 % 2, :], acc_ps[0][:, :], ACT.Copy)
                    if sums_apart:
                        ins = act.activation(stile[:, v2 % 2, :], acc_ps[1][:, :], ACT.Copy)
                    ins.then_inc(out_ready, 1)

                for ev in body:
                    if ev[0] == "EV":
                        ended += 1
                    if ev[0] != "ST":
                        continue
                    _, (g, u), kc, part = ev
                    off = max(0, kc - 4 * u) * P
                    act.wait_ge(pv_done, i * n_quads + n // st_parts + 1)
                    act.wait_ge(st_ready, i * n_pairs + n + 1)
                    head = n * st_heads
                    act.activation(probs[:, head // 2 % NP_RING, head % 2:head % 2 + st_heads, off:QB],
                                   st_ps[slot(n, n_pairs, st_slots)][:, :, off:QB],
                                   ACT.Exp, scale=scale).then_inc(exp_done, 1)
                    n += 1
                    if ended > v2:
                        take_sums()
                        v2 += 1
                take_sums()

        @block.vector
        def _(dve):
            if hd == 16:
                for k in range(2):
                    dve.memset(QT[k][0:MROW, :, :].bitcast(U32), 0).then_inc(zeroed[k], 1)
            dve.nop().then_inc(item_free, S_SLOTS)

            def events(evs, ibase, item0, unit0):
                n, w, transposed = 0, 0, 0
                for ev in evs:
                    if ev[0] == "S":
                        _, (g, u), qt, h, j, width = ev
                        dve.wait_ge(item_ready, ibase(n_items) + item0 + n + 1)
                        dve.tensor_reduce(part[:, (unit0 + w) % 2, qt * HG + h, j:j + 1],
                                          s_ps[slot(item0 - p_items + n, n_items, S_SLOTS)][:, 0:width], AX.X,
                                          ALU.max).then_inc(item_free, 1)
                        n += 1
                    elif ev[0] == "M":
                        g, u = ev[1]
                        b = (unit0 + w) % 2
                        dve.wait_ge(item_free, ibase(n_items) + item0 + n + S_SLOTS)
                        dve.tensor_reduce(rowmax[:, b, :], part[:, b, :, 0:u + 1], AX.X,
                                          ALU.max).then_inc(max_done, 1)
                        dve.wait_ge(max_done, ibase(8) + unit0 + w + 1)
                        dve.tensor_scalar(shift[:, b, :, 0], rowmax[:, b, :], -1.0 / MSHIFT, None,
                                          ALU.mult).then_inc(hi_done, 1)
                        dve.wait_ge(hi_done, ibase(8) + unit0 + w + 1)
                        dve.scalar_tensor_tensor(out=shift[:, b, :, 1], in0=rowmax[:, b, :],
                                                 scalar=-1.0 / MSHIFT, in1=shift[:, b, :, 0],
                                                 op0=ALU.mult,
                                                 op1=ALU.subtract).then_inc(shift_ready, 1)
                        w += 1
                    elif ev[0] == "T":
                        g, u = ev[1]
                        dve.wait_ge(item_ready, ibase(n_items) + item0 + n + 1)
                        rows = s_ps[slot(item0 - p_items + n, n_items, S_SLOTS)][MROW:NROW, 0:QB // 2].bitcast(F16)
                        dve.tensor_copy(QT[g % 2][MROW:NROW, :, u * QB:(u + 1) * QB],
                                        rows.unsqueeze(1).to_broadcast([2 * HG, HG, QB])
                                        ).then_inc(row_ready, 1)
                        dve.wait_ge(row_ready, ibase(8) + unit0 + transposed + 1)
                        dve.nop().then_inc(item_free, 1)
                        transposed += 1
                        n += 1
                return n, w

            n, w = events(prologue, lambda k: 0, 0, 0)
            with dve.Fori(0, GROUPS // 2) as i:
                events(body, lambda k: i * k, n, w)

        @block.tensor
        def _(pe):
            pe.nop().then_inc(pv_done, 3)
            pe.nop().then_inc(group_done, 1)

            def pass1(ev, n, it, wait_unit):
                place = s_ps[slot(n - p_items, n_items, S_SLOTS)]
                before = previous(n - p_items, n_items, S_SLOTS) + p_items
                pe.wait_ge(item_free, it * n_items + before + 1 + S_SLOTS)
                if ev[0] == "S":
                    _, (g, u), qt, h, j, width = ev
                    q0 = u * QB + qt * P
                    diagonal = j == u
                    mm = pe.matmul(place[:, 0:width], QT[g % 2][0:MROW, h, q0:q0 + P],
                                   KT[g % 2][0:MROW, h, j * QB:j * QB + width],
                                   start=True, stop=not diagonal)
                    if diagonal:
                        mm = pe.matmul(place[:, width - P:width], C["ident16"][:, :],
                                       C["mask_qk"][:, :], start=False, stop=True)
                    mm.then_inc(item_ready, 1)
                else:
                    pe.wait_ge(shift_ready, wait_unit + 1)
                    rows = place[MROW:NROW, 0:QB // 2].bitcast(F16)
                    for qt in range(4):
                        mm = pe.transpose(rows[:, qt * P:(qt + 1) * P],
                                          shift[:, ev[2] % 2, qt * HG:(qt + 1) * HG, :]
                                          .rearrange("p h two -> p (h two)"),
                                          C["ident_f16"][:, :])
                    mm.then_inc(item_ready, 1)

            pe.wait_ge(C["const_ready"], C["const_count"])
            pe.wait_ge(init, 32)
            pe.wait_ge(ld[0], LOADS)
            n = 0
            for ev in prologue:
                if ev[0] == "M":
                    continue
                pass1(ev if ev[0] == "S" else ev + (0,), n, 0, 0)
                n += 1
            with pe.Fori(0, GROUPS // 2) as i:
                items, w1, pairs, quads, v2 = p_items, 1, 0, 0, 0
                loaded = {0}
                for ev in body:
                    if ev[0] in ("S", "T"):
                        g = ev[1][0]
                        if g not in loaded:
                            loaded.add(g)
                            pe.wait_ge(ld[g % 2], i * LOADS + LOADS * (1 if g == 1 else 2))
                        pass1(ev if ev[0] == "S" else ev + (w1,), items, i, i * 8 + w1)
                        w1 += ev[0] == "T"
                        items += 1
                    elif ev[0] == "ST":
                        _, (g, u), kc, part = ev
                        if kc == 0 and part == 0:
                            pe.wait_ge(row_ready, i * 8 + v2 + 1)
                            v2 += 1
                        off = max(0, kc - 4 * u) * P
                        diagonal = kc >= 4 * u
                        before = previous(pairs, n_pairs, st_slots)
                        pe.wait_ge(exp_done, i * n_pairs + before + 1 + st_slots)
                        for hh in range(st_heads):
                            h = st_heads * part + hh
                            place = st_ps[slot(pairs, n_pairs, st_slots)]
                            mm = pe.matmul(place[:, hh, off:QB],
                                           KT[g % 2][0:NROW, h, kc * P:(kc + 1) * P],
                                           QT[g % 2][0:NROW, h, u * QB + off:(u + 1) * QB],
                                           start=True, stop=not diagonal)
                            if diagonal:
                                mm = pe.matmul(place[:, hh, off:off + P], C["ident16"][:, :],
                                               C["mask_kq"][:, :], start=False, stop=True)
                        mm.then_inc(st_ready, 1)
                        pairs += 1
                    elif ev[0] == "PV":
                        _, (g, u), kc = ev
                        unit = 4 * g + (3 - u)
                        off = max(0, kc - 4 * u) * P
                        last = kc == 4 * u + 3
                        if kc == 0:
                            pe.wait_ge(out_ready, i * 8 + unit + 1)
                        pe.wait_ge(exp_done, i * n_pairs + st_parts * (quads + 1) + st_slots)
                        for h in range(HG):
                            pr = probs[:, (2 * quads + h // 2) % NP_RING, h % 2, off:QB]
                            mm = pe.matmul(acc_ps[0][32 * h:32 * h + 32, off:QB],
                                           V[g % 2][:, kc, 32 * h:32 * h + 32], pr,
                                           start=kc == 0, stop=last)
                        if sums_apart:
                            for h in range(HG):
                                pr = probs[:, (2 * quads + h // 2) % NP_RING, h % 2, off:QB]
                                mm = pe.matmul(acc_ps[1][32 * h:32 * h + 32, off:QB],
                                               C["ones32"][:, :], pr, start=kc == 0, stop=last)
                        mm.then_inc(pv_done, 1)
                        quads += 1
                        if last:
                            pe.wait_ge(pv_done, i * n_quads + quads + 3)
                            pe.nop().then_inc(acc_ready, 1)
                            if u == last_unit_of_group:
                                pe.nop().then_inc(group_done, 1)


def constants(nc, c, shift_rows):
    C = {"ident16": c.sb("ident16", [P, P], BF16), "ident_f16": c.sb("ident_f16", [P, P], F16),
         "identf": c.sb("identf", [P, P], F32), "mask_qk": c.sb("mask_qk", [P, P], BF16),
         "mask_kq": c.sb("mask_kq", [P, P], BF16), "ones32": c.sb("ones32", [P, 32], F32), "onesf": c.sb("onesf", [P, P], F32),
         "ones16": c.sb("ones16", [P, P], BF16), "tri16": c.sb("tri16", [P, P], BF16),
         "w_ffn": c.sb("w_ffn", [P, NF, D], F32),
         "shift_rows": shift_rows, "const_ready": c.sem("const_ready")}
    MASK = -1.0e30
    with nc.Block() as block:
        @block.gpsimd
        def _(pool):
            for k in ("ident16", "ident_f16", "identf", "mask_qk", "mask_kq"):
                pool.memset(C[k][:, :], 0.0).then_inc(C["const_ready"], 1)
            for k in ("ones32", "onesf", "ones16", "tri16"):
                pool.memset(C[k][:, :], 1.0).then_inc(C["const_ready"], 1)
            pool.wait_ge(C["const_ready"], 9)
            pool.affine_select(out=C["tri16"][:, :], in_=C["tri16"][:, :], compare_op=ALU.is_ge,
                               fill=0.0, base=0, pattern=[[1, P]],
                               channel_multiplier=-1).then_inc(C["const_ready"], 1)
            for k in ("ident16", "ident_f16", "identf"):
                pool.affine_select(out=C[k][:, :], in_=C[k][:, :], compare_op=ALU.not_equal,
                                   fill=1.0, base=0, pattern=[[-1, P]],
                                   channel_multiplier=1).then_inc(C["const_ready"], 1)
            pool.affine_select(out=C["mask_qk"][:, :], in_=C["mask_qk"][:, :], compare_op=ALU.is_ge,
                               fill=MASK, base=0, pattern=[[-1, P]],
                               channel_multiplier=1).then_inc(C["const_ready"], 1)
            pool.affine_select(out=C["mask_kq"][:, :], in_=C["mask_kq"][:, :], compare_op=ALU.is_ge,
                               fill=MASK, base=0, pattern=[[1, P]],
                               channel_multiplier=-1).then_inc(C["const_ready"], 1)
            pool.wait_ge(C["const_ready"], 15)
    C["const_count"] = 15
    return C

NT = B * T // P
NB = B * T // QB
NF = D // P
EPS = 1e-5


class Steps:

    def __init__(self, sem, names, credit=2):
        self.sem, self.names, self.credit, self.at = sem, list(names), credit, 0
        assert len(set(self.names)) == len(self.names)

    def start(self, eng, blocks_before=None):
        eng.nop().then_inc(self.sem, (self.credit if blocks_before is None else blocks_before)
                           * len(self.names))

    def step(self, name, ins):
        assert self.names[self.at] == name, (self.names[self.at], name)
        self.at = (self.at + 1) % len(self.names)
        return ins.then_inc(self.sem, 1)

    def skip(self, eng, names, blk):
        eng.wait_ge(self.sem, (blk + self.credit) * len(self.names) + self.names.index(names[0]))
        for name in names:
            self.step(name, eng.nop())

    def wait(self, eng, name, blk):
        n = len(self.names)
        eng.wait_ge(self.sem, (blk + self.credit) * n + self.names.index(name) + 1)


def blocks(eng, body, per=2):
    with eng.Fori(0, NB // per) as i:
        for k in range(per):
            body(i * per + k, k, i)


def blocks_ahead(eng, body):
    with eng.Fori(0, NB // 2 - 1) as i:
        for k in range(2):
            body(i * 2 + k, k, i, False)
    for k in range(2):
        body(NB - 2 + k, k, NB // 2 - 1, k == 1)


class Banks:

    def __init__(self, c, jobs, steps, ring=8):
        assert len(jobs) % ring == 0
        self.jobs, self.steps, self.ring = jobs, steps, ring
        self.index = {j[0]: n for n, j in enumerate(jobs)}
        self.banks = [c.ps(f"bank{k}", [P, QB]) for k in range(ring)]

    def bank(self, name):
        return self.banks[self.index[name] % self.ring]

    def take(self, pe, name, blk, *needs):
        n = self.index[name]
        _, eng, drained = self.jobs[n - self.ring]
        last = {}
        for e, step, ago in needs + ((eng, drained, 0 if n >= self.ring else 1),):
            at = (-ago, self.steps[e].names.index(step), step)
            last[e] = max(last.get(e, at), at)
        for e, (ago, _, step) in last.items():
            self.steps[e].wait(pe, step, blk + ago)
        return self.banks[n % self.ring]


class Chain:

    def __init__(self, eng, sem):
        self.eng, self.sem, self.n = eng, sem, 0

    def link(self, ins):
        self.n += 1
        ins.then_inc(self.sem, 1)
        self.eng.wait_ge(self.sem, self.n)


def moments(dve, link, st, mean, var, diff):
    link(dve.tensor_tensor(mean, st[:, :, 1], st[:, :, 4], ALU.add))
    link(dve.tensor_tensor(diff, st[:, :, 1], st[:, :, 4], ALU.subtract))
    link(dve.tensor_scalar(mean, mean, 0.5, None, ALU.mult))
    link(dve.tensor_tensor(diff, diff, diff, ALU.mult))
    link(dve.tensor_tensor(var, st[:, :, 2], st[:, :, 5], ALU.add))
    link(dve.tensor_scalar(var, var, 1.0 / D, EPS, ALU.mult, ALU.add))
    link(dve.scalar_tensor_tensor(out=var, in0=diff, scalar=0.25, in1=var, op0=ALU.mult,
                                  op1=ALU.add))


def inverse_root(dve, link, std, var, rstd):
    link(dve.reciprocal(rstd, std))
    link(dve.tensor_tensor(std, rstd, rstd, ALU.mult))
    link(dve.tensor_tensor(std, std, var, ALU.mult))
    link(dve.tensor_scalar(std, std, -0.5, 1.5, ALU.mult, ALU.add))
    link(dve.tensor_tensor(rstd, rstd, std, ALU.mult))


def first_operands(nc, c, x, W, x_all):
    F = {"wl": c.sb("wl", [P, NF, 3 * D], F32), "wf": c.sb("wf", [P, NF, 3, H, 16], F32),
         "cos_q": c.sb("cos_q", [P, T], F32), "sin_q": c.sb("sin_q", [P, T], F32),
         "cos_f": c.sb("cos_f", [P, T], F32), "sin_f": c.sb("sin_f", [P, T], F32),
         "cos_k": c.sb("cos_k", [P, NKC, 8], F32), "sin_k": c.sb("sin_k", [P, NKC, 8], F32),
         "rotate": c.sb("rotate", [P, P], F32), "gb": c.sb("gb", [P, NF, 2], F32),
         "x_ld": [c.sem(f"x_ld{k}") for k in range(NB)], "ld": c.sem("ld"), "loads": 0}

    def load_all(sp):
        def load(dst, src):
            sp.dma_start(dst, src).then_inc(F["ld"], 16)
            F["loads"] += 16

        def load_x(blk):
            rows = slice(4 * blk, 4 * blk + 4)
            sp.dma_start(x_all[:, rows, :], x.rearrange("b (t p) d -> p (b t) d", p=P)[:, rows, :]
                         ).then_inc(F["x_ld"][blk], 16)
        load_x(0)
        load(F["wl"][:, :, :], W["W_qkv"].rearrange("(c p) n -> p c n", p=P))
        load(F["rotate"][:, :], W["rotate"])
        with nc.allow_non_contiguous_dma(reason="a few hundred floats"):
            load(F["gb"][:, :, 0], W["ln1_g"].rearrange("(c p) -> p c", p=P))
            load(F["gb"][:, :, 1], W["ln1_b"].rearrange("(c p) -> p c", p=P))
        for part in range(3):
            for f in range(NF):
                load(F["wf"][:, f, part, :, :], W["ffn_Wqkv"][f * P:(f + 1) * P, :].rearrange(
                    "p (h s d) -> p h s d", h=H, s=3)[:, :, part, :])
        load_x(1)
        for name in ("cos_q", "sin_q", "cos_f", "sin_f"):
            load(F[name][:, :], W[name])
        load(F["cos_k"][:, :, :], W["cos_k"])
        load(F["sin_k"][:, :, :], W["sin_k"])
        for blk in range(2, NB):
            load_x(blk)
    return F, load_all


def project_first(nc, C, F, xn_all, qf_all, kv_sum, scale_qk, qk_out, v_out):
    T_NAMES = ("T xn0", "T xn1", "T z0", "T z1")
    jobs = [(n, "act", n) for n in T_NAMES]
    for f in range(2):
        jobs += [(f"q{f}", "act", f"q{f}")]
    for t in range(2):
        jobs += [(f"kv{t}", "act", f"v{t}")]
    for f in range(2):
        jobs += [(f"rot q{f}", "dve", f"rot q{f}")]
    for t in range(2, 4):
        jobs += [(f"kv{t}", "act", f"v{t}")]
    for f in range(4):
        jobs += [(f"f{f}", "act", f"f{f}")]
    for t in range(2):
        jobs += [(f"fv{t}", "act", f"fv{t}")]
    for f in range(4):
        jobs += [(f"rot f{f}", "dve", f"rot f{f}")]
    for f in range(2):
        jobs += [(f"sum{f}", "dve", f"sum{f}")]
    pe_names = [j[0] for j in jobs]
    act_names = list(T_NAMES) + ["sqrt1", "q0", "q1", "k0", "v0", "k1", "v1", "k2", "v2", "k3", "v3", "sqrt2",
                                 "exp q0", "exp q1", "f0", "f1", "f2", "f3", "fv0", "fv1", "exp k",
                                 "hi q", "hi k"]
    ahead1 = [f"stat1 {t}" for t in range(4)] + [f"moment1 {n}" for n in range(7)]
    ahead2 = [f"root1 {n}" for n in range(5)] + [f"xn{t}" for t in range(4)]
    ahead2 += [f"stat2 {t}" for t in range(4)] + [f"moment2 {n}" for n in range(7)]
    ahead3 = [f"root2 {n}" for n in range(5)]
    ahead3 += ["x next", "z next0", "z next1", "z next2", "z next3"]
    dve_names = ahead1 + [
                 "rot q0", "add q0", "min q0", "rot q1", "add q1", "min q1",
                 *ahead2, "k lo", "k hi", "min k", "feat q0", "feat q1", *ahead3,
                 "rot f0", "add f0", "rot f1", "add f1", "feat k",
                 "rot f2", "add f2", "lo q", "rot f3", "add f3", "lo k", "sum0", "sum1"]
    pool_names = ["cos q0", "cos q1", "k1cos", "k2sin", "k1sin", "k2cos",
                  "cos f0", "cos f1", "cos f2", "cos f3"]

    with Ctx(nc, "pr") as c:
        wl, wf, cos_q, sin_q, cos_f, sin_f, cos_k, sin_k, rotate, gb, ld = (
            F[n] for n in ("wl", "wf", "cos_q", "sin_q", "cos_f", "sin_f", "cos_k", "sin_k",
                           "rotate", "gb", "ld"))
        LOADS = F["loads"]
        stats = c.sb("stats", [P, 4, 6], F32)
        mean, var, std, diff, rstd = (c.sb(n, [P, 4], F32) for n in ("mean", "var", "std", "diff", "rstd"))
        x4 = c.sb("x4", [P, 4, D], F32)
        z = [c.sb(f"z{k}", [P, 4, D], F32) for k in range(2)]
        xnT = c.sb("xnT", [P, NF, QB], F32)
        hT = c.sb("hT", [P, NF, QB], F32)
        qs = c.sb("qs", [P, 2, QB], F32)
        qc = c.sb("qc", [P, 2, QB], F32)
        qr = c.sb("qr", [P, 2, QB], F32)
        ks = c.sb("ks", [P, 4, H, 2, 8], F32)
        kp = c.sb("kp", [P, 4, 4, H, 8], F32)
        kr = c.sb("kr", [P, 4, H, 2, 8], F32)
        ke = c.sb("ke", [P, 4 * D], F32)
        vl = c.sb("vl", [P, 4, NF, P + 8], F32)
        fs = c.sb("fs", [P, 4, QB], F32)
        fr = c.sb("fr", [P, 4, QB], F32)
        part16 = c.sb("part16", [P, 2, 4, QB], F16)
        vt = c.sb("vt", [P, 4, H, 2, 16], F32)
        ones, zero = c.sem("ones"), c.sem("zero")
        pe_s = Steps(c.sem("pe"), pe_names)
        act_s = Steps(c.sem("act"), act_names)
        dve_s = Steps(c.sem("dve"), dve_names)
        pool_s = Steps(c.sem("pool"), pool_names)
        held = {e: c.sem(f"held_{e}") for e in ("pe", "act", "dve", "pool")}
        raw_out, vt_out = c.sem("raw_out"), c.sem("vt_out")
        block = c.block()
        banks = Banks(c, jobs, {"act": act_s, "dve": dve_s})

        @block.sync
        def _(sp):
            def body(blk, k, i):
                b, j = i // 2, (i % 2) * 2 + k
                act_s.wait(sp, "fv1", blk)
                for g in range(4):
                    sp.dma_start(v_out[b, g, :, bass.ds(j * 4, 4), :],
                                 vt[:, :, g * HG:(g + 1) * HG, :, :]
                                 .rearrange("p t h s d -> p t (h s d)")).then_inc(vt_out, 16)
                dve_s.wait(sp, "lo k", blk)
                for side in range(2):
                    for lower in range(2):
                        dst = qk_out[side][lower].rearrange("(b c g) h d t -> b c (g h d) t", b=B, c=NF)
                        sp.dma_start(dst[b, :, :, bass.ds(j * QB, QB)].rearrange("c p t -> p c t"),
                                     part16[:, lower, 2 * side:2 * side + 2, :]).then_inc(raw_out, 16)
            blocks(sp, body)
            sp.wait_ge(raw_out, 1 + 64 * NB)
            sp.wait_ge(vt_out, 1 + 64 * NB)

        @block.gpsimd
        def _(pool):
            pool.memset(vt[:, :, :, 1, :], 1.0).then_inc(ones, 1)
            pool.memset(vl[:, :, :, P:P + 8], 1.0).then_inc(ones, 1)
            pool_s.start(pool)
            pool.wait_ge(ld, LOADS)
            tt = pool.tensor_tensor

            def body(blk, k, i):
                tok = bass.ds((i % 2) * 2 * QB + k * QB, QB)
                tile = bass.ds((i % 2) * 8 + k * 4, 4)
                for f in range(2):
                    act_s.wait(pool, f"q{f}", blk)
                    dve_s.wait(pool, f"feat q{f}", blk - 1)
                    pool.nop().then_inc(held["pool"], 1)
                    pool_s.step(f"cos q{f}", tt(qc[:, f, :], qs[:, f, :], cos_q[:, tok], ALU.mult))
                act_s.wait(pool, "k3", blk)
                dve_s.wait(pool, "k hi", blk - 1)
                pool.nop().then_inc(held["pool"], 1)
                ck = cos_k[:, tile, :].unsqueeze(2).to_broadcast([P, 4, H, 8])
                sk = sin_k[:, tile, :].unsqueeze(2).to_broadcast([P, 4, H, 8])
                for n, (name, half, table) in enumerate((("k1cos", 0, ck), ("k2sin", 1, sk),
                                                         ("k1sin", 0, sk), ("k2cos", 1, ck))):
                    pool_s.step(name, tt(kp[:, n], ks[:, :, :, half, :], table, ALU.mult))
                for f in range(4):
                    act_s.wait(pool, f"f{f}", blk)
                    dve_s.wait(pool, "lo k", blk - 1)
                    pool.nop().then_inc(held["pool"], 1)
                    pool_s.step(f"cos f{f}", tt(fr[:, f, :], fs[:, f, :], cos_f[:, tok], ALU.mult))
            blocks(pool, body)

        @block.scalar
        def _(act):
            act_s.start(act, 1)
            act.nop().then_inc(vt_out, 1)
            act.nop().then_inc(raw_out, 1)
            def sqrt(n, blk):
                dve_s.wait(act, f"moment{n} 6", blk)
                act_s.step(f"sqrt{n}", act.activation(std[:, :], var[:, :], ACT.Sqrt))

            act_s.skip(act, act_names[:4], -1)
            sqrt(1, -1)
            act_s.skip(act, act_names[5:act_names.index("sqrt2")], -1)
            sqrt(2, -1)
            act_s.skip(act, act_names[act_names.index("sqrt2") + 1:], -1)
            act.wait_ge(ld, LOADS)
            act.wait_ge(ones, 2)

            def body(blk, k, i, last):
                def src(name):
                    pe_s.wait(act, name, blk)
                    return banks.bank(name)

                for f in range(2):
                    act_s.step(f"T xn{f}", act.activation(xnT[:, f, :], src(f"T xn{f}")[:, :], ACT.Copy))
                for f in range(2):
                    act_s.step(f"T z{f}", act.activation(hT[:, f, :], src(f"T z{f}")[:, :],
                                                         ACT.Identity, bias=gb[:, f, 1:2],
                                                         scale=gb[:, f, 0:1]))
                if last:
                    act_s.skip(act, ["sqrt1"], blk)
                else:
                    sqrt(1, blk)
                for f in range(2):
                    pool_s.wait(act, f"cos q{f}", blk - 1)
                    act_s.step(f"q{f}", act.activation(qs[:, f, :], src(f"q{f}")[:, :], ACT.Copy))
                for t in range(4):
                    s = src(f"kv{t}")
                    pool_s.wait(act, "k2cos", blk - 1)
                    act_s.step(f"k{t}", act.activation(
                        ks[:, t].rearrange("p h s d -> p (h s d)"), s[:, 0:D], ACT.Copy))
                    act_s.step(f"v{t}", act.activation(
                        vl[:, t, :, 0:P], s[:, D:2 * D].rearrange("p (c d) -> p c d", c=NF), ACT.Copy))
                if last:
                    act_s.skip(act, ["sqrt2"], blk)
                else:
                    sqrt(2, blk)
                for f in range(2):
                    dve_s.wait(act, f"min q{f}", blk)
                    act_s.step(f"exp q{f}", act.activation(qc[:, f, :], qc[:, f, :], ACT.Exp))
                for f in range(4):
                    dve_s.wait(act, f"add f{f}", blk - 1)
                    act_s.step(f"f{f}", act.activation(fs[:, f, :], src(f"f{f}")[:, :], ACT.Copy))
                for t in range(2):
                    act.wait_ge(vt_out, blk * 64 + 1)
                    act_s.step(f"fv{t}", act.activation(
                        vt[:, 2 * t:2 * t + 2, :, 0, :],
                        src(f"fv{t}")[:, :].rearrange("p (t h d) -> p t h d", t=2, h=H), ACT.Copy))
                dve_s.wait(act, "min k", blk)
                act_s.step("exp k", act.activation(ke[:, :], ke[:, :], ACT.Exp))
                act.wait_ge(raw_out, blk * 64 + 1)
                for side, name in enumerate("qk"):
                    dve_s.wait(act, f"add f{2 * side + 1}", blk)
                    act_s.step(f"hi {name}", act.activation(
                        part16[:, 0, 2 * side:2 * side + 2, :], fr[:, 2 * side:2 * side + 2, :],
                        ACT.Copy, scale=scale_qk[side]))
            blocks_ahead(act, body)

        @block.vector
        def _(dve):
            tt = dve.tensor_tensor

            rows = lambda n: xn_all[:, bass.ds(n, 1), :].rearrange("p a d -> p (a d)")

            def linked(names, blk, work):
                names = iter(names)

                def link(ins):
                    name = next(names)
                    dve_s.step(name, ins)
                    dve_s.wait(dve, name, blk)
                work(link)

            def statistics(n, blk):
                for t in range(4):
                    dve_s.step(f"stat{n} {t}", dve.bn_stats(stats[:, t, :], rows((blk + 1) * 4 + t)))
                dve_s.wait(dve, f"stat{n} 3", blk)
                linked([f"moment{n} {m}" for m in range(7)], blk,
                       lambda link: moments(dve, link, stats, mean[:, :], var[:, :], diff[:, :]))

            def root(n, blk):
                act_s.wait(dve, f"sqrt{n}", blk)
                linked([f"root{n} {m}" for m in range(5)], blk,
                       lambda link: inverse_root(dve, link, std[:, :], var[:, :], rstd[:, :]))

            def normalised(dst, t, blk):
                return dve.tensor_scalar(dst, rows((blk + 1) * 4 + t), mean[:, t:t + 1],
                                         rstd[:, t:t + 1], ALU.subtract, ALU.mult)

            def first_norm(blk):
                root(1, blk)
                for t in range(4):
                    dve_s.step(f"xn{t}", normalised(rows((blk + 1) * 4 + t), t, blk))
                dve_s.wait(dve, "xn3", blk)
                dve.nop().then_inc(held["dve"], 1)
                statistics(2, blk)

            def second_norm(blk, slot):
                root(2, blk)
                if not isinstance(blk, int) or blk >= 0:
                    pe_s.wait(dve, "T xn1", blk)
                    dve.nop().then_inc(held["dve"], 1)
                dve_s.step("x next", dve.tensor_copy(x4[:, :, :], xn_all[:, bass.ds((blk + 1) * 4, 4), :]))
                for t in range(4):
                    dve_s.step(f"z next{t}", normalised(z[slot][:, t, :], t, blk))

            dve.memset(kv_sum[:, :, :], 0.0).then_inc(zero, 1)
            dve.wait_ge(zero, 1)
            dve_s.start(dve, 1)
            dve.wait_ge(F["x_ld"][0], 16)
            statistics(1, -1)
            q0, k_lo, f0 = (dve_names.index(n) for n in ("rot q0", "k lo", "rot f0"))
            dve_s.skip(dve, dve_names[q0:q0 + 6], -1)
            first_norm(-1)
            dve_s.skip(dve, dve_names[k_lo:k_lo + 5], -1)
            second_norm(-1, 0)
            dve_s.skip(dve, dve_names[f0:], -1)
            for blk in range(1, NB):
                dve.wait_ge(F["x_ld"][blk], 16)
            dve.wait_ge(ld, LOADS)

            def body(blk, k, i, last):
                def src(name):
                    pe_s.wait(dve, name, blk)
                    return banks.bank(name)

                tok = bass.ds((i % 2) * 2 * QB + k * QB, QB)
                if last:
                    dve_s.skip(dve, ahead1, blk)
                else:
                    statistics(1, blk)
                for f in range(2):
                    s = src(f"rot q{f}")
                    dve_s.wait(dve, f"feat q{f}", blk - 1)
                    dve_s.step(f"rot q{f}", tt(qr[:, f, :], s[:, :], sin_q[:, tok], ALU.mult))
                    dve_s.wait(dve, f"rot q{f}", blk)
                    pool_s.wait(dve, f"cos q{f}", blk)
                    dve_s.step(f"add q{f}", tt(qr[:, f, :], qr[:, f, :], qc[:, f, :], ALU.add))
                    dve_s.wait(dve, f"add q{f}", blk)
                    dve_s.step(f"min q{f}", dve.tensor_scalar(qc[:, f, :], qr[:, f, :], 0.0, None, ALU.min))
                if last:
                    dve_s.skip(dve, ahead2, blk)
                else:
                    first_norm(blk)
                pool_s.wait(dve, "k2cos", blk)
                dve_s.wait(dve, "feat k", blk - 1)
                pe_s.wait(dve, "sum1", blk - 1)
                dve_s.step("k lo", tt(kr[:, :, :, 0, :], kp[:, 0], kp[:, 1], ALU.subtract))
                dve_s.step("k hi", tt(kr[:, :, :, 1, :], kp[:, 2], kp[:, 3], ALU.add))
                dve_s.wait(dve, "k hi", blk)
                flat = kr[:, :, :, :, :].rearrange("p t h s d -> p (t h s d)")
                dve_s.step("min k", dve.tensor_scalar(ke[:, :], flat, 0.0, None, ALU.min))
                for f in range(2):
                    act_s.wait(dve, f"exp q{f}", blk)
                    dve_s.step(f"feat q{f}", dve.scalar_tensor_tensor(
                        out=qf_all[:, f, bass.ds(blk * QB, QB)], in0=qr[:, f, :], scalar=0.0,
                        in1=qc[:, f, :], op0=ALU.max, op1=ALU.add))
                if last:
                    dve_s.skip(dve, ahead3, blk)
                else:
                    second_norm(blk, 1 - k)
                for f in range(4):
                    s = src(f"rot f{f}")
                    pool_s.wait(dve, f"cos f{f}", blk)
                    dve_s.step(f"rot f{f}", tt(fs[:, f, :], s[:, :], sin_f[:, tok], ALU.mult))
                    dve_s.wait(dve, f"rot f{f}", blk)
                    dve_s.step(f"add f{f}", tt(fr[:, f, :], fr[:, f, :], fs[:, f, :], ALU.add))
                    if f >= 2:
                        side = f - 2
                        act_s.wait(dve, f"hi {'qk'[side]}", blk)
                        dve_s.step(f"lo {'qk'[side]}", dve.scalar_tensor_tensor(
                            out=part16[:, 1, 2 * side:2 * side + 2, :],
                            in0=fr[:, 2 * side:2 * side + 2, :], scalar=scale_qk[side],
                            in1=part16[:, 0, 2 * side:2 * side + 2, :], op0=ALU.mult,
                            op1=ALU.subtract))
                    if f == 1:
                        act_s.wait(dve, "exp k", blk)
                        dve_s.step("feat k", dve.scalar_tensor_tensor(
                            out=flat, in0=flat, scalar=0.0, in1=ke[:, :], op0=ALU.max, op1=ALU.add))
                for f in range(2):
                    s = src(f"sum{f}")
                    acc = kv_sum[:, bass.ds((i // 2) * NF + f, 1), :].rearrange("p a n -> p (a n)")
                    dve_s.wait(dve, f"sum{f}", blk - 1)
                    dve_s.step(f"sum{f}", tt(acc, acc, s[:, 0:P + 8], ALU.add))
            blocks_ahead(dve, body)

        @block.tensor
        def _(pe):
            pe_s.start(pe)
            pe.wait_ge(C["const_ready"], C["const_count"])
            pe.wait_ge(ld, LOADS)
            def body(blk, k, i):
                def dst(name, *needs):
                    return banks.take(pe, name, blk, *needs)

                def accumulate(name, pairs, width=QB, needs=()):
                    d = dst(name, *needs)
                    for n, (lhsT, rhs) in enumerate(pairs):
                        mm = pe.matmul(d[:, 0:width], lhsT, rhs, start=n == 0, stop=n == len(pairs) - 1)
                    pe_s.step(name, mm)

                for name, src, made in (("T xn", x4, "x next"), ("T z", z[k], "z next3")):
                    for f in range(2):
                        d = dst(f"{name}{f}", ("dve", made, 1))
                        for t in range(4):
                            mm = pe.transpose(d[:, t * P:(t + 1) * P],
                                              src[:, t, f * P:(f + 1) * P], C["identf"][:, :])
                        pe_s.step(f"{name}{f}", mm)

                def feature_rows(name, weights, act_T, made):
                    accumulate(name, [(weights(n), act_T[:, n, :]) for n in range(NF)],
                               needs=(("act", made, 0),))

                def token_rows(name, act_T, t, weights):
                    accumulate(name, [(act_T[:, n, t * P:(t + 1) * P], weights(n)) for n in range(NF)])

                for f in range(2):
                    feature_rows(f"q{f}", lambda n: wl[:, n, f * P:(f + 1) * P], xnT, "T xn1")
                for t in range(2):
                    token_rows(f"kv{t}", xnT, t, lambda n: wl[:, n, D:3 * D])
                for f in range(2):
                    accumulate(f"rot q{f}", [(rotate[:, :], qs[:, f, :])],
                               needs=(("act", f"q{f}", 0),))
                for t in range(2, 4):
                    token_rows(f"kv{t}", xnT, t, lambda n: wl[:, n, D:3 * D])
                for f in range(4):
                    feature_rows(f"f{f}", lambda n: wf[:, n, f // 2, (f % 2) * 8:(f % 2) * 8 + 8, :]
                                 .rearrange("p h d -> p (h d)"), hT, "T z1")
                for m in range(2):
                    d = dst(f"fv{m}")
                    for t in range(2):
                        for n in range(NF):
                            mm = pe.matmul(d[:, t * D:(t + 1) * D],
                                           hT[:, n, (2 * m + t) * P:(2 * m + t + 1) * P],
                                           wf[:, n, 2, :, :].rearrange("p h d -> p (h d)"),
                                           start=n == 0, stop=n == NF - 1)
                    pe_s.step(f"fv{m}", mm)
                for f in range(4):
                    accumulate(f"rot f{f}", [(rotate[:, :], fs[:, f, :])],
                               needs=(("act", f"f{f}", 0),))
                for f in range(2):
                    accumulate(f"sum{f}", [(kr[:, t].rearrange("p h s d -> p (h s d)")[:, f * P:(f + 1) * P],
                                            vl[:, t, f, :]) for t in range(4)], P + 8,
                               needs=(("dve", "feat k", 0), ("act", "v3", 0)))
            blocks(pe, body)

E = 8
CAP = 2 * B * T // E
FF = 4 * D
NFF = FF // P
NCT = CAP // P
SPLIT_TOP = 4096.0
FLOOR = 1e-6


def prepare(nc, C, W, score, zeros, exp_in, zero_fill, load_next):
    with Ctx(nc, "prep") as c:
        wf = c.sb("wf", [P, NF, H, 3, 16], F32)
        wq = c.sb("wq", [P, 2, NF, 2 * D], F32)
        sq = c.sb("sq", [P, NF, 2 * D], F32)
        gb = c.sb("gb", [P, 2, NF], F32)
        gb2 = c.sb("gb2", [P, 2, NF], F32)
        kern = c.sb("kern", [P, NF, D], F32)
        lora_a = c.sb("lora_a", [P, NF, 16], F32)
        lora_b = c.sb("lora_b", [16, D], F32)
        aT = c.sb("aT", [16, NF, P], F32)
        top = c.sb("top", [P, 4], F32)
        bound = c.sb("bound", [P, 4], F32)
        small = c.sb("small", [P, 8], F32)
        red = c.sb("red", [P, 2], F32)
        redall = c.sb("redall", [P, 2], F32)
        ps = [c.ps(f"ps{k}", [P, 2 * D]) for k in range(6)]
        ld, ch, sq_s, mm_s, red_s, all_s, root_s, rooted, pool_s, cp_s = (
            c.sem(n) for n in ("ld", "ch", "sq", "mm", "red", "all", "root", "rooted", "pool", "cp"))
        block = c.block()
        n_loads = [0]

        @block.sync
        def _(sp):
            def load(dst, src):
                sp.dma_start(dst, src).then_inc(ld, 16)
                n_loads[0] += 16
            load(wf[:, :, :, :, :].rearrange("p c h s d -> p c (h s d)"),
                 W["ffn_Wqkv"].rearrange("(c p) n -> p c n", p=P))
            load(wq[:, 0], W["Wq"].rearrange("(c p) n -> p c n", p=P))
            load(wq[:, 1], W["Wk"].rearrange("(c p) n -> p c n", p=P))
            load(kern[:, :, :], W["kernel"].rearrange("(c p) n -> p c n", p=P))
            load(lora_a[:, :, :], W["a"].rearrange("(c p) n -> p c n", p=P))
            load(lora_b[:, :], W["b"])
            with nc.allow_non_contiguous_dma(reason="a few hundred floats"):
                load(gb[:, 0, :], W["ln1_g"].rearrange("(c p) -> p c", p=P))
                load(gb[:, 1, :], W["ln1_b"].rearrange("(c p) -> p c", p=P))
            load_next(sp)
            sp.wait_ge(pool_s, 1)
            rows = exp_in.rearrange("(p r) d -> p r d", p=P)
            sp.dma_start(rows, zeros[:, :].unsqueeze(1).to_broadcast([P, E * CAP // P, D])
                         ).then_inc(zero_fill, 16)

        @block.gpsimd
        def _(pool):
            pool.memset(zeros[:, :], 0.0).then_inc(pool_s, 1)
            pool.wait_ge(red_s, 1)
            pool.partition_all_reduce(redall[:, :], red[:, :], P, bass.bass_isa.ReduceOp.max
                                      ).then_inc(all_s, 1)

        @block.scalar
        def _(act):
            act.wait_ge(root_s, 1)
            act.activation(small[:, 0:5], small[:, 0:5], ACT.Sqrt).then_inc(rooted, 1)

        @block.tensor
        def _(pe):
            pe.wait_ge(C["const_ready"], C["const_count"])
            pe.wait_ge(ld, n_loads[0])
            for n in range(4):
                pe.wait_ge(sq_s, n + 1)
                width = D if n < 2 else 2 * D
                for f in range(NF):
                    mm = pe.matmul(ps[n][:, 0:width], C["onesf"][:, :], sq[:, f, 0:width],
                                   start=f == 0, stop=f == NF - 1)
                mm.then_inc(mm_s, 1)
            pe.wait_ge(sq_s, 5)
            pe.matmul(ps[4][:, 0:NF], C["onesf"][:, :], gb2[:, 1, :], start=True, stop=True).then_inc(mm_s, 1)
            for f in range(NF):
                mm = pe.transpose(ps[5][0:16, f * P:(f + 1) * P], lora_a[:, f, :], C["identf"][:, :])
            mm.then_inc(mm_s, 1)
            pe.wait_ge(cp_s, 1)
            for f in range(NF):
                mm = pe.matmul(ps[0][:, f * D:(f + 1) * D], aT[:, f, :], lora_b[:, :], start=True, stop=True)
            mm.then_inc(mm_s, 1)

        @block.vector
        def _(dve):
            chain = Chain(dve, ch)
            link = chain.link
            dve.wait_ge(ld, n_loads[0])
            for n in range(4):
                for f in range(NF):
                    if n < 2:
                        src = wf[:, f, :, n, :]
                        dst = sq[:, f, 0:D].rearrange("p (h d) -> p h d", h=H)
                    else:
                        src, dst = wq[:, n - 2, f, :], sq[:, f, :]
                    link(dve.tensor_tensor(dst, src, src, ALU.mult))
                dve.nop().then_inc(sq_s, 1)
                width = D if n < 2 else 2 * D
                dve.wait_ge(mm_s, n + 1)
                link(dve.tensor_reduce(top[:, n:n + 1], ps[n][:, 0:width], AX.X, ALU.max))
            link(dve.tensor_tensor(gb2[:, :, :], gb[:, :, :], gb[:, :, :], ALU.mult))
            dve.nop().then_inc(sq_s, 1)
            dve.wait_ge(mm_s, 5)
            link(dve.tensor_reduce(small[:, 4:5], ps[4][:, 0:NF], AX.X, ALU.add))
            link(dve.tensor_reduce(red[:, 0:1], gb[:, 0, :], AX.X, ALU.max, apply_absolute_value=True))
            link(dve.tensor_reduce(red[:, 1:2], kern[:, :, :], AX.XY, ALU.max, apply_absolute_value=True))
            dve.nop().then_inc(red_s, 1)
            link(dve.tensor_copy(small[:, 0:4], top[:, :]))
            dve.nop().then_inc(root_s, 1)
            dve.wait_ge(rooted, 1)
            dve.wait_ge(all_s, 1)
            slack = 1.01 * float(D) ** 0.5
            link(dve.tensor_scalar(bound[:, :], small[:, 0:4], slack, None, ALU.mult))
            link(dve.scalar_tensor_tensor(out=small[:, 5:6], in0=small[:, 4:5], scalar=float(D) ** -0.5,
                                          in1=redall[:, 0:1], op0=ALU.mult, op1=ALU.add))
            link(dve.tensor_scalar(bound[:, 0:2], bound[:, 0:2], small[:, 5:6], 2.0 ** 0.5, ALU.mult, ALU.mult))
            link(dve.tensor_scalar(bound[:, :], bound[:, :], FLOOR, None, ALU.max))
            link(dve.reciprocal(top[:, :], bound[:, :]))
            link(dve.tensor_scalar(top[:, :], top[:, :], SPLIT_TOP, None, ALU.mult))
            for layer in range(2):
                s = score[layer]
                n = 2 * layer
                link(dve.tensor_copy(s[:, 0:2], top[:, n:n + 2]))
                link(dve.tensor_tensor(s[:, 2:3], bound[:, n:n + 1], bound[:, n + 1:n + 2], ALU.mult))
                link(dve.tensor_scalar(s[:, 2:3], s[:, 2:3], SPLIT_TOP ** -2 / 4.0, None, ALU.mult))
            link(dve.tensor_scalar(small[:, 6:7], redall[:, 1:2], 1.0 / 7.0, 1e-30, ALU.mult, ALU.max))
            link(dve.reciprocal(small[:, 7:8], small[:, 6:7]))
            half_even = 1.5 * 2.0 ** 23
            link(dve.tensor_scalar(kern[:, :, :], kern[:, :, :], small[:, 7:8], None, ALU.mult))
            link(dve.tensor_scalar(kern[:, :, :], kern[:, :, :], half_even, half_even, ALU.add, ALU.subtract))
            link(dve.tensor_scalar(kern[:, :, :], kern[:, :, :], 7.0, -8.0, ALU.min, ALU.max))
            dve.wait_ge(mm_s, 6)
            link(dve.tensor_copy(aT[:, :, :], ps[5][0:16, 0:D].rearrange("r (f p) -> r f p", f=NF)))
            dve.nop().then_inc(cp_s, 1)
            dve.wait_ge(mm_s, 7)
            link(dve.scalar_tensor_tensor(out=C["w_ffn"][:, :, :], in0=kern[:, :, :], scalar=small[:, 6:7],
                                          in1=ps[0][:, :].rearrange("p (f n) -> p f n", f=NF),
                                          op0=ALU.mult, op1=ALU.add))


def linear_out(nc, C, W, qf_all, kv_sum, s_out, pool_work, load_next):
    act_names = ["tr0", "tr1", "out0", "out1"]
    dve_names = ["copy"] + [f"{s}{t}" for t in range(4) for s in ("max", "rec", "nrm")]
    jobs = [(f"num{t}", "dve", f"nrm{t}") for t in range(4)]
    jobs += [("tr0", "act", "tr0"), ("tr1", "act", "tr1"), ("out0", "act", "out0"), ("out1", "act", "out1")]
    WID = P + 8
    with Ctx(nc, "lo") as c:
        w_out = c.sb("w_out", [P, NF, D], F32)
        heads = c.sb("heads", [P, WID], F32)
        kvd = c.sb("kvd", [P, B * NF, WID], F32)
        qf = [c.sb(f"qf{k}", [P, NF, QB], F32) for k in range(2)]
        den = c.sb("den", [P, 4, H], F32)
        nrm = c.sb("nrm", [P, 4, D], F32)
        nT = c.sb("nT", [P, 4, NF, P], F32)
        ot = c.sb("ot", [P, 4, D], F32)
        ld, kv_ready, stored = c.sem("ld"), c.sem("kv_ready"), c.sem("stored")
        pe_s = Steps(c.sem("pe"), [j[0] for j in jobs])
        act_s = Steps(c.sem("act"), act_names)
        dve_s = Steps(c.sem("dve"), dve_names)
        banks = Banks(c, jobs, {"act": act_s, "dve": dve_s})
        block = c.block()

        block.gpsimd(pool_work)

        @block.sync
        def _(sp):
            sp.dma_start(w_out[:, :, :], W["W_out"].rearrange("(c p) n -> p c n", p=P)).then_inc(ld, 16)
            sp.dma_start(heads[:, :], W["heads"]).then_inc(ld, 16)
            load_next(sp)

            def body(blk, k, i):
                act_s.wait(sp, "out1", blk)
                sp.dma_start(s_out[bass.ds(blk * 4, 4), :, :].rearrange("t p d -> p t d"),
                             ot[:, :, :]).then_inc(stored, 16)
            blocks(sp, body)
            sp.wait_ge(stored, 1 + 16 * NB)

        @block.vector
        def _(dve):
            dve.wait_ge(ld, 32)
            for n in range(B * NF):
                dve.tensor_tensor(kvd[:, n, :], kv_sum[:, n, :], heads[:, :], ALU.mult).then_inc(kv_ready, 1)
            dve_s.start(dve)

            def body(blk, k, i):
                pe_s.wait(dve, "num3", blk - 2)
                dve_s.step("copy", dve.tensor_copy(qf[k][:, :, :], qf_all[:, :, bass.ds(blk * QB, QB)]))
                pe_s.wait(dve, "tr1", blk - 1)
                for t in range(4):
                    pe_s.wait(dve, f"num{t}", blk)
                    s = banks.bank(f"num{t}")[:, 0:NF * WID].rearrange("p (c n) -> p c n", c=NF)
                    d = den[:, t, :].rearrange("p (c h) -> p c h", c=NF)
                    dve_s.step(f"max{t}", dve.tensor_scalar(d, s[:, :, P:WID], 1e-6, None, ALU.max))
                    dve_s.wait(dve, f"max{t}", blk)
                    dve_s.step(f"rec{t}", dve.reciprocal(d, d))
                    dve_s.wait(dve, f"rec{t}", blk)
                    n = nrm[:, t, :].rearrange("p (c h d) -> p c h d", c=NF, h=8)
                    dve_s.step(f"nrm{t}", dve.tensor_tensor(
                        n, s[:, :, 0:P].rearrange("p c (h d) -> p c h d", h=8),
                        d.unsqueeze(3).to_broadcast([P, NF, 8, 16]), ALU.mult))
            blocks(dve, body)

        @block.scalar
        def _(act):
            act_s.start(act)
            act.nop().then_inc(stored, 1)

            def body(blk, k, i):
                for m in range(2):
                    pe_s.wait(act, f"tr{m}", blk)
                    act_s.step(f"tr{m}", act.activation(
                        nT[:, 2 * m:2 * m + 2, :, :].rearrange("p t c n -> p (t c n)"),
                        banks.bank(f"tr{m}")[:, :], ACT.Copy))
                act.wait_ge(stored, blk * 16 + 1)
                for m in range(2):
                    pe_s.wait(act, f"out{m}", blk)
                    act_s.step(f"out{m}", act.activation(
                        ot[:, 2 * m:2 * m + 2, :].rearrange("p t n -> p (t n)"),
                        banks.bank(f"out{m}")[:, :], ACT.Copy))
            blocks(act, body)

        @block.tensor
        def _(pe):
            pe_s.start(pe)
            pe.wait_ge(ld, 32)
            pe.wait_ge(kv_ready, B * NF)

            def body(blk, k, i):
                b = i // 2
                for t in range(4):
                    d = banks.take(pe, f"num{t}", blk, ("dve", "copy", 0))
                    for f in range(NF):
                        mm = pe.matmul(d[:, f * WID:(f + 1) * WID], qf[k][:, f, t * P:(t + 1) * P],
                                       kvd[:, bass.ds(b * NF + f, 1), :].rearrange("p a n -> p (a n)"),
                                       start=True, stop=True)
                    pe_s.step(f"num{t}", mm)
                for m in range(2):
                    d = banks.take(pe, f"tr{m}", blk, ("dve", f"nrm{2 * m + 1}", 0))
                    for t in range(2):
                        for f in range(NF):
                            mm = pe.transpose(d[:, (t * NF + f) * P:(t * NF + f + 1) * P],
                                              nrm[:, 2 * m + t, f * P:(f + 1) * P], C["identf"][:, :])
                    pe_s.step(f"tr{m}", mm)
                for m in range(2):
                    d = banks.take(pe, f"out{m}", blk, ("act", f"tr{m}", 0))
                    for t in range(2):
                        for f in range(NF):
                            mm = pe.matmul(d[:, t * D:(t + 1) * D], nT[:, 2 * m + t, f, :], w_out[:, f, :],
                                           start=f == 0, stop=f == NF - 1)
                    pe_s.step(f"out{m}", mm)
            blocks(pe, body)


class Attended:

    def __init__(self, c, att, sums, inverse, rows, pe_s, last_use):
        self.rows, self.heads = rows, P // rows
        self.chunks = H // self.heads
        self.sums, self.all_inverse = (a.rearrange("x (q t) -> x q t", t=QB) for a in (sums, inverse))
        self.tile = c.sb("sums", [P, QB], F32)
        self.sums_ld, self.inverted, self.kept = c.sem("sums_ld"), c.sem("inverted"), c.sem("kept")
        self.att = att.rearrange("(b g) (h r) t -> b (g h) r t", b=B, r=32).rearrange(
            "b (c y) r t -> b c y r t", y=self.heads)[:, :, :, 0:rows, :]
        self.inverse = inverse.rearrange("(b c y) t -> b c y t", b=B, y=self.heads)
        self.pe_s, self.last_use = pe_s, last_use
        self.a = [c.sb(f"a{k}", [P, self.chunks, QB], F32) for k in range(NB // B)]
        self.r = [c.sb(f"r{k}", [P, self.chunks, QB], F32) for k in range(NB // B)]
        self.ld = [c.sem(f"ld{k}") for k in range(NB // B)]
        self.divided = c.sem("divided")

    def load_values(self, sp, k, i):
        tok = slice(k * QB, (k + 1) * QB)
        for y in range(self.heads):
            sp.dma_start(self.a[k][y * self.rows:(y + 1) * self.rows, :, :],
                         self.att[bass.ds(i, 1), :, y, :, tok].rearrange("b c r t -> (b r) c t")
                         ).then_inc(self.ld[k], 16)

    def load_inverse(self, sp, k, i):
        tok = slice(k * QB, (k + 1) * QB)
        for y in range(self.heads):
            sp.dma_start(self.r[k][y * self.rows:(y + 1) * self.rows, :, :],
                         self.inverse[bass.ds(i, 1), :, y, tok].to_broadcast(
                             [self.rows, self.chunks, QB])).then_inc(self.ld[k], 16)

    def load(self, eng, values=True, inverses=True):
        if inverses:
            eng.dma_start(self.tile[:, :], self.sums).then_inc(self.sums_ld, 16)
        for k in range(NB // B):
            if values:
                self.load_values(eng, k, 0)
            if inverses:
                if k == 0:
                    eng.wait_ge(self.inverted, 1)
                    eng.dma_start(self.all_inverse, self.tile[:, :]).then_inc(self.kept, 16)
                    eng.wait_ge(self.kept, 16)
                self.load_inverse(eng, k, 0)
        with eng.Fori(0, B - 1) as i:
            for k in range(NB // B):
                self.pe_s.wait(eng, self.last_use, i * (NB // B) + k)
                if values:
                    self.load_values(eng, k, i + 1)
                if inverses:
                    self.load_inverse(eng, k, i + 1)

    def invert(self, dve):
        dve.wait_ge(self.sums_ld, 16)
        dve.reciprocal(self.tile[:, :], self.tile[:, :]).then_inc(self.inverted, 1)

    def divide(self, pool):
        def body(blk, k, i):
            pool.wait_ge(self.ld[k], (i + 1) * (2 * 16 * self.heads))
            pool.tensor_tensor(self.a[k][:, :, :], self.a[k][:, :, :], self.r[k][:, :, :],
                               ALU.mult).then_inc(self.divided, 1)
        blocks(pool, body, NB // B)

    def wait(self, pe, blk):
        pe.wait_ge(self.divided, blk + 1)


def after_attention(nc, W, att, sums, inverse, x_all, stats):
    jobs = [(f"x{t}", "dve", f"add{t}") for t in range(4)]
    dve_names = [f"{s}{t}" for t in range(4) for s in ("add", "stat")]
    with Ctx(nc, "aa") as c:
        w = c.sb("w", [P, NF, D], F32)
        w_ld = c.sem("w_ld")
        pe_s = Steps(c.sem("pe"), [j[0] for j in jobs], credit=NB // B)
        dve_s = Steps(c.sem("dve"), dve_names)
        banks = Banks(c, jobs, {"dve": dve_s}, ring=4)
        attended = Attended(c, att, sums, inverse, 16, pe_s, "x3")
        block = c.block()

        @block.sync
        def _(sp):
            sp.dma_start(w[:, :, :], W["Wproj"].rearrange("(c p) n -> p c n", p=P)).then_inc(w_ld, 16)
            attended.load(sp, inverses=False)

        @block.scalar
        def _(act):
            attended.load(act, values=False)

        @block.gpsimd
        def _(pool):
            attended.divide(pool)

        @block.vector
        def _(dve):
            attended.invert(dve)
            dve_s.start(dve)

            def body(blk, k, i):
                for t in range(4):
                    x = x_all[:, bass.ds(blk * 4 + t, 1), :].rearrange("p a d -> p (a d)")
                    pe_s.wait(dve, f"x{t}", blk)
                    dve_s.step(f"add{t}", dve.tensor_tensor(x, x, banks.bank(f"x{t}")[:, 0:D], ALU.add))
                    dve_s.wait(dve, f"add{t}", blk)
                    dve_s.step(f"stat{t}", dve.bn_stats(stats[:, blk * 4 + t, :], x))
            blocks(dve, body)

        @block.tensor
        def _(pe):
            pe_s.start(pe)
            pe.wait_ge(w_ld, 16)

            def body(blk, k, i):
                attended.wait(pe, blk)
                for t in range(4):
                    d = banks.take(pe, f"x{t}", blk)
                    for g in range(attended.chunks):
                        mm = pe.matmul(d[:, 0:D], attended.a[k][:, g, t * P:(t + 1) * P], w[:, g, :],
                                       start=g == 0, stop=g == attended.chunks - 1)
                    pe_s.step(f"x{t}", mm)
            blocks(pe, body, NB // B)


def row_statistics(nc, tag, stats, mean, rstd):
    with Ctx(nc, tag) as c:
        var = c.sb("var", [P, NT], F32)
        std = c.sb("std", [P, NT], F32)
        diff = c.sb("diff", [P, NT], F32)
        ch, var_ready, std_ready = c.sem("ch"), c.sem("var_ready"), c.sem("std_ready")
        block = c.block()

        @block.scalar
        def _(act):
            act.wait_ge(var_ready, 1)
            act.activation(std[:, :], var[:, :], ACT.Sqrt).then_inc(std_ready, 1)

        @block.vector
        def _(dve):
            chain = Chain(dve, ch)
            moments(dve, chain.link, stats, mean[:, :], var[:, :], diff[:, :])
            dve.nop().then_inc(var_ready, 1)
            dve.wait_ge(std_ready, 1)
            inverse_root(dve, chain.link, std[:, :], var[:, :], rstd[:, :])


def gate_logits(nc, C, W, x_all, mean, rstd, z_all, logits):
    jobs = [("T0", "act", "T0"), ("T1", "act", "T1"), ("log", "dve", "log"), ("none", "dve", "log")]
    with Ctx(nc, "gl") as c:
        z = [c.sb(f"z{k}", [P, 4, D], F32) for k in range(2)]
        hT = [c.sb(f"hT{k}", [P, NF, QB], F32) for k in range(2)]
        wg = c.sb("wg", [P, NF, E], F32)
        gb = c.sb("gb", [P, NF, 2], F32)
        ld = c.sem("ld")
        pe_s = Steps(c.sem("pe"), ["T0", "T1", "log"])
        act_s = Steps(c.sem("act"), ["keep", "T0", "T1"])
        dve_s = Steps(c.sem("dve"), ["z0", "z1", "z2", "z3", "log"])
        first_z = c.sem("first_z")
        banks = Banks(c, jobs, {"act": act_s, "dve": dve_s}, ring=4)
        block = c.block()

        @block.sync
        def _(sp):
            with nc.allow_non_contiguous_dma(reason="a few hundred floats"):
                sp.dma_start(wg[:, :, :], W["Wgate"].rearrange("(c p) e -> p c e", p=P)).then_inc(ld, 16)
                sp.dma_start(gb[:, :, 0], W["ln2_g"].rearrange("(c p) -> p c", p=P)).then_inc(ld, 16)
                sp.dma_start(gb[:, :, 1], W["ln2_b"].rearrange("(c p) -> p c", p=P)).then_inc(ld, 16)

        @block.vector
        def _(dve):
            def z_tile(n, slot, t):
                return dve.tensor_scalar(
                    z[slot][:, t, :], x_all[:, bass.ds(n, 1), :].rearrange("p a d -> p (a d)"),
                    mean[:, bass.ds(n, 1)], rstd[:, bass.ds(n, 1)], ALU.subtract, ALU.mult)

            for slot in range(2):
                for t in range(4):
                    z_tile(slot * 4 + t, slot, t).then_inc(first_z, 1)
            dve.wait_ge(first_z, 8)
            dve_s.start(dve)

            def body(blk, k, i):
                pe_s.wait(dve, "T1", blk - 1)
                act_s.wait(dve, "keep", blk)
                for t in range(4):
                    dve_s.step(f"z{t}", z_tile(((blk + 2) % NB) * 4 + t, k, t))
                pe_s.wait(dve, "log", blk)
                dve_s.step("log", dve.tensor_copy(
                    logits[:, bass.ds(blk * 4, 4), :],
                    banks.bank("log")[:, 0:4 * E].rearrange("p (t e) -> p t e", t=4)))
            blocks(dve, body)

        @block.scalar
        def _(act):
            act_s.start(act, 1)
            act.wait_ge(ld, 48)

            def transposed(blk, slot):
                for f in range(NF):
                    pe_s.wait(act, f"T{f}", blk)
                    act_s.step(f"T{f}", act.activation(hT[slot][:, f, :], banks.bank(f"T{f}")[:, :],
                                                       ACT.Identity, bias=gb[:, f, 1:2],
                                                       scale=gb[:, f, 0:1]))
            act_s.skip(act, ["keep"], -1)
            transposed(-1, 0)

            def body(blk, k, i):
                act_s.step("keep", act.activation(z_all[:, bass.ds(blk * 4, 4), :], z[k][:, :, :], ACT.Copy))
                transposed(blk, 1 - k)
            blocks(act, body)

        @block.tensor
        def _(pe):
            pe_s.start(pe, 1)
            pe.wait_ge(ld, 48)

            def transpose(blk, slot):
                for f in range(NF):
                    d = banks.take(pe, f"T{f}", blk, ("dve", "z3", 1))
                    for t in range(4):
                        mm = pe.transpose(d[:, t * P:(t + 1) * P], z[slot][:, t, f * P:(f + 1) * P],
                                          C["identf"][:, :])
                    pe_s.step(f"T{f}", mm)
            transpose(-1, 0)
            pe_s.skip(pe, ["log"], -1)

            def body(blk, k, i):
                transpose(blk, 1 - k)
                d = banks.take(pe, "log", blk, ("act", "T1", 1))
                for t in range(4):
                    for f in range(NF):
                        mm = pe.matmul(d[:, t * E:(t + 1) * E], hT[k][:, f, t * P:(t + 1) * P], wg[:, f, :],
                                       start=f == 0, stop=f == NF - 1)
                pe_s.step("log", mm)
            blocks(pe, body)


def route(nc, C, W, logits, scatter_at, gather_at, gate):
    with Ctx(nc, "rt") as c:
        big = lambda n, dt=F32: c.sb(n, [P, NT, E], dt)
        G, key, pos, tot, run, tmp, one = (big(n) for n in ("G", "key", "pos", "tot", "run", "tmp", "one"))
        hot = [big("hot0"), big("hot1")]
        mask = big("mask", BF16)
        m1 = c.sb("m1", [P, NT], F32)
        pr = c.sb("pr", [P, 2, NT], F32)
        base = c.sb("base", [P, 2, NT], F32)
        keep = c.sb("keep", [P, 2, NT], F32)
        at = c.sb("at", [P, 2, NT], F32)
        iota8 = c.sb("iota8", [P, 2, E], F32)
        cum, total = c.ps("cum", [P, NT * E]), c.ps("total", [P, NT * E])
        ld, ch, e_in, e_out, m_ready, counted = (
            c.sem(n) for n in ("ld", "ch", "e_in", "e_out", "m_ready", "counted"))
        block = c.block()
        wide = lambda a: a.unsqueeze(2).to_broadcast([P, NT, E])
        along = lambda a: a.unsqueeze(1).to_broadcast([P, NT, E])

        @block.sync
        def _(sp):
            sp.dma_start(iota8[:, :, :], W["iota8"]).then_inc(ld, 16)

        @block.scalar
        def _(act):
            act.wait_ge(e_in, 1)
            act.activation(G[:, :, :], logits[:, :, :], ACT.Exp).then_inc(e_out, 1)

        @block.tensor
        def _(pe):
            pe.wait_ge(m_ready, 1)
            m = mask[:, :, :].rearrange("p t e -> p (t e)")
            pe.matmul(cum[:, :], C["tri16"][:, :], m, start=True, stop=True)
            pe.matmul(total[:, :], C["ones16"][:, :], m, start=True, stop=True).then_inc(counted, 1)

        @block.vector
        def _(dve):
            link = Chain(dve, ch).link
            tt, ts, red = dve.tensor_tensor, dve.tensor_scalar, dve.tensor_reduce
            descending, index = iota8[:, 0, :], iota8[:, 1, :]
            link(red(m1[:, :], logits[:, :, :], AX.X, ALU.max))
            link(tt(logits[:, :, :], logits[:, :, :], wide(m1[:, :]), ALU.subtract))
            dve.nop().then_inc(e_in, 1)
            dve.wait_ge(e_out, 1)
            link(red(m1[:, :], G[:, :, :], AX.X, ALU.add))
            link(dve.reciprocal(m1[:, :], m1[:, :]))
            link(tt(G[:, :, :], G[:, :, :], wide(m1[:, :]), ALU.mult))
            dve.wait_ge(ld, 16)
            for r in range(2):
                g = gate[:, r, :]
                link(red(g, G[:, :, :], AX.X, ALU.max))
                link(tt(key[:, :, :], G[:, :, :], wide(g), ALU.is_equal))
                link(tt(key[:, :, :], key[:, :, :], along(descending), ALU.mult))
                link(red(m1[:, :], key[:, :, :], AX.X, ALU.max))
                link(tt(hot[r][:, :, :], key[:, :, :], wide(m1[:, :]), ALU.is_equal))
                if r == 0:
                    link(dve.scalar_tensor_tensor(out=G[:, :, :], in0=hot[0][:, :, :], scalar=-2.0,
                                                  in1=G[:, :, :], op0=ALU.mult, op1=ALU.add))
            link(tt(mask[:, :, :], hot[0][:, :, :], hot[1][:, :, :], ALU.add))
            dve.nop().then_inc(m_ready, 1)
            link(dve.memset(one[:, :, :], 1.0))
            dve.wait_ge(counted, 1)
            link(dve.tensor_copy(tot[:, :, :].rearrange("p t e -> p (t e)"), total[:, :]))
            for e in range(E):
                link(dve.tensor_tensor_scan(run[:, :, e], one[:, :, e], tot[:, :, e], 0.0,
                                            ALU.mult, ALU.add))
            link(tt(run[:, :, :], run[:, :, :], tot[:, :, :], ALU.subtract))
            link(tt(pos[:, :, :].rearrange("p t e -> p (t e)"),
                    run[:, :, :].rearrange("p t e -> p (t e)"), cum[:, :], ALU.add))
            link(ts(pos[:, :, :], pos[:, :, :], -1.0, None, ALU.add))
            for r in range(2):
                link(tt(tmp[:, :, :], hot[r][:, :, :], pos[:, :, :], ALU.mult))
                link(red(pr[:, r, :], tmp[:, :, :], AX.X, ALU.add))
                link(tt(tmp[:, :, :], hot[r][:, :, :], along(index), ALU.mult))
                link(red(base[:, r, :], tmp[:, :, :], AX.X, ALU.add))
            link(ts(base[:, :, :], base[:, :, :], float(CAP), None, ALU.mult))
            link(ts(keep[:, :, :], pr[:, :, :], float(CAP), None, ALU.is_lt))
            link(ts(at[:, :, :], keep[:, :, :], -4.0 * E * CAP, 4.0 * E * CAP, ALU.mult, ALU.add))
            link(tt(at[:, :, :], at[:, :, :], base[:, :, :], ALU.add))
            link(tt(at[:, :, :], at[:, :, :], pr[:, :, :], ALU.add))
            link(dve.tensor_copy(scatter_at[:, :, :], at[:, :, :]))
            link(ts(pr[:, :, :], pr[:, :, :], float(CAP - 1), None, ALU.min))
            link(tt(pr[:, :, :], pr[:, :, :], base[:, :, :], ALU.add))
            link(dve.tensor_copy(gather_at[:, :, :], pr[:, :, :]))
            link(tt(gate[:, :, :], gate[:, :, :], keep[:, :, :], ALU.mult))


def scatter_rows(pool, z_all, scatter_at, exp_in, zero_fill, sent):
    pool.wait_ge(zero_fill, 16)
    for t in range(NT):
        for r in range(2):
            pool.indirect_dma_start(
                out=exp_in[:, :],
                out_offset=bass.IndirectOffsetOnAxis(ap=scatter_at[:, r, t:t + 1], axis=0),
                in_=z_all[:, t, :], in_offset=None, bounds_check=E * CAP - 1,
                oob_is_err=False).then_inc(sent, 16)
    pool.wait_ge(sent, 16 * 2 * NT)


def expert_operands(c, W):
    X = {"w1": [c.sb(f"w1{k}", [P, NF, FF], F32) for k in range(2)],
         "w2": [c.sb(f"w2{k}", [P, NFF, D], F32) for k in range(2)],
         "ld": [c.sem(f"w_ld{k}") for k in range(2)]}

    def load_weights(sp, e, k):
        w1, w2 = (W[n][bass.ds(e, 1)].rearrange("e (c p) n -> p (e c) n", p=P) for n in ("W1", "W2"))
        sp.dma_start(X["w1"][k][:, :, :], w1).then_inc(X["ld"][k], 16)
        sp.dma_start(X["w2"][k][:, :, :], w2).then_inc(X["ld"][k], 16)
    return X, load_weights


def experts(nc, C, W, X, load_weights, exp_in, exp_out, spare):
    jobs = [(f"T{cb}{f}", "act", f"T{cb}{f}") for cb in range(2) for f in range(NF)]
    jobs += [(f"h0{f}", "act", f"h0{f}") for f in range(NFF)]
    jobs += [(f"h1{f}", "act", f"h1{f}") for f in range(NFF // 2)]
    jobs += [(f"y0{m}", "dve", f"y0{m}") for m in range(2)]
    jobs += [(f"h1{f}", "act", f"h1{f}") for f in range(NFF // 2, NFF)]
    jobs += [(f"y1{m}", "dve", f"y1{m}") for m in range(2)]
    with Ctx(nc, "ex") as c:
        xin = [c.sb(f"xin{k}", [P, NCT, D], F32) for k in range(2)]
        w1, w2 = X["w1"], X["w2"]
        xT = c.sb("xT", [P, NF, CAP], F32)
        hT = [c.sb(f"hT{k}", [P, NFF, QB], F32) for k in range(2)]
        ot = c.sb("ot", [P, 2, 2, 2, D], F32)
        b1n = c.sb("b1n", [E * NFF, P], F32)
        b1 = c.sb("b1", [P, E * NFF], F32)
        b2 = spare[:, 0, 0:E * D].rearrange("p (e d) -> p e d", e=E)
        gb = c.sb("gb", [P, NF, 2], F32)
        ld = [c.sem(f"ld{k}") for k in range(2)]
        w_ld, b_t, b_ready, stored = c.sem("w_ld"), c.sem("b_t"), c.sem("b_ready"), c.sem("stored")
        ot_free = c.sem("ot_free")
        held = c.sem("held")
        pe_s = Steps(c.sem("pe"), [j[0] for j in jobs])
        act_s = Steps(c.sem("act"), [j[0] for j in jobs if j[1] == "act"])
        dve_s = Steps(c.sem("dve"), [j[0] for j in jobs if j[1] == "dve"])
        banks = Banks(c, jobs, {"act": act_s, "dve": dve_s})
        block = c.block()

        def experts_loop(eng, body):
            with eng.Fori(0, E // 2) as i:
                for k in range(2):
                    body(i * 2 + k, k, i)

        @block.sync
        def _(sp):
            sp.dma_start(b1n[:, :], W["b1"].rearrange("e (f p) -> (e f) p", p=P)).then_inc(w_ld, 16)
            sp.dma_start(b2[:, :, :], W["b2"].unsqueeze(0).to_broadcast([P, E, D])).then_inc(w_ld, 16)
            with nc.allow_non_contiguous_dma(reason="a few hundred floats"):
                sp.dma_start(gb[:, :, 0], W["ln2_g"].rearrange("(c p) -> p c", p=P)).then_inc(w_ld, 16)
                sp.dma_start(gb[:, :, 1], W["ln2_b"].rearrange("(c p) -> p c", p=P)).then_inc(w_ld, 16)

            def load_rows(e, k):
                sp.dma_start(xin[k][:, :, :], exp_in.rearrange("(e t p) d -> p (e t) d", e=E, p=P)[
                    :, bass.ds(e * NCT, NCT), :]).then_inc(ld[k], 16)

            for k in range(2):
                load_rows(k, k)
            with sp.Fori(0, E // 2 - 1) as i:
                for k in range(2):
                    e = i * 2 + 2 + k
                    pe_s.wait(sp, "y11", e - 2)
                    load_rows(e, k)
                    load_weights(sp, e, k)

        @block.gpsimd
        def _(pool):
            rows = exp_out.rearrange("(e c m t p) d -> e c m p t d", e=E, c=2, m=2, p=P)

            def body(e, k, i):
                for cb in range(2):
                    for m in range(2):
                        dve_s.wait(pool, f"y{cb}{m}", e)
                        pool.dma_start(rows[e, cb, m], ot[:, cb, m, :, :]).then_inc(stored, 16)
                        pool.wait_ge(stored, e * 64 + (2 * cb + m + 1) * 16)
                        pool.nop().then_inc(ot_free, 1)
            pool.nop().then_inc(ot_free, 4)
            experts_loop(pool, body)

        @block.scalar
        def _(act):
            act_s.start(act)
            act.wait_ge(w_ld, 64)
            act.wait_ge(b_ready, 1)

            def body(e, k, i):
                for cb in range(2):
                    for f in range(NF):
                        pe_s.wait(act, f"T{cb}{f}", e)
                        act_s.step(f"T{cb}{f}", act.activation(
                            xT[:, f, cb * QB:(cb + 1) * QB], banks.bank(f"T{cb}{f}")[:, :], ACT.Identity,
                            bias=gb[:, f, 1:2], scale=gb[:, f, 0:1]))
                for cb in range(2):
                    for f in range(NFF):
                        pe_s.wait(act, f"h{cb}{f}", e)
                        act.nop().then_inc(held, 1)
                        act_s.step(f"h{cb}{f}", act.activation(
                            hT[cb][:, f, :], banks.bank(f"h{cb}{f}")[:, :], ACT.Gelu,
                            bias=b1[:, bass.ds(e * NFF + f, 1)]))
            experts_loop(act, body)

        @block.vector
        def _(dve):
            dve.wait_ge(b_t, 1)
            dve.tensor_copy(b1[:, :], banks.banks[0][:, 0:E * NFF]).then_inc(b_ready, 1)
            dve.wait_ge(b_ready, 1)
            dve_s.start(dve)
            dve.wait_ge(w_ld, 64)

            def body(e, k, i):
                for cb in range(2):
                    for m in range(2):
                        dve.wait_ge(ot_free, e * 4 + 2 * cb + m + 1)
                        pe_s.wait(dve, f"y{cb}{m}", e)
                        dve_s.step(f"y{cb}{m}", dve.tensor_tensor(
                            ot[:, cb, m, :, :],
                            banks.bank(f"y{cb}{m}")[:, :].rearrange("p (t d) -> p t d", t=2),
                            b2[:, bass.ds(e, 1), :].to_broadcast([P, 2, D]), ALU.add))
            experts_loop(dve, body)

        @block.tensor
        def _(pe):
            pe.wait_ge(w_ld, 64)
            pe.transpose(banks.banks[0][:, 0:E * NFF], b1n[:, :], C["identf"][0:E * NFF, 0:E * NFF]
                         ).then_inc(b_t, 1)
            pe.wait_ge(b_ready, 1)
            pe_s.start(pe)

            def body(e, k, i):
                pe.wait_ge(ld[k], i * 16 + 16)

                def hidden(cb, fs):
                    for f in fs:
                        d = banks.take(pe, f"h{cb}{f}", e, ("act", f"T{cb}1", 0))
                        for n in range(NF):
                            mm = pe.matmul(d[:, :], w1[k][:, n, f * P:(f + 1) * P],
                                           xT[:, n, cb * QB:(cb + 1) * QB], start=n == 0, stop=n == NF - 1)
                        pe_s.step(f"h{cb}{f}", mm)

                def result(cb):
                    for m in range(2):
                        d = banks.take(pe, f"y{cb}{m}", e, ("act", f"h{cb}{NFF - 1}", 0))
                        for t in range(2):
                            for n in range(NFF):
                                mm = pe.matmul(d[:, t * D:(t + 1) * D],
                                               hT[cb][:, n, (2 * m + t) * P:(2 * m + t + 1) * P],
                                               w2[k][:, n, :], start=n == 0, stop=n == NFF - 1)
                        pe_s.step(f"y{cb}{m}", mm)

                for cb in range(2):
                    for f in range(NF):
                        d = banks.take(pe, f"T{cb}{f}", e)
                        for t in range(4):
                            mm = pe.transpose(d[:, t * P:(t + 1) * P],
                                              xin[k][:, cb * 4 + t, f * P:(f + 1) * P], C["identf"][:, :])
                        pe_s.step(f"T{cb}{f}", mm)
                pe.wait_ge(X["ld"][k], i * 32 + 32)
                hidden(0, range(NFF))
                hidden(1, range(NFF // 2))
                result(0)
                hidden(1, range(NFF // 2, NFF))
                result(1)
            experts_loop(pe, body)


def combine_and_project(nc, C, W, x, s_out, exp_out, gather_at, gate, x_all, scale_qk, qk_out, v_out,
                        g_all):
    jobs = [("T0", "act", "T0"), ("T1", "act", "T1")]
    jobs += [(f"{s}{f}", "dve", f"lo {s}{f}") for s in "qk" for f in range(4)]
    jobs += [(f"v{t}", "act", f"v{t}") for t in range(4)]
    jobs += [(f"y{m}", "dve", f"y{m}") for m in range(2)]
    MOMENTS = [f"moment{n}" for n in range(7)]
    ROOT = [f"root{n}" for n in range(5)]
    gathered = [f"{s}{t}" for t in range(4) for s in ("one", "two")]
    combined = [f"{s}{t}" for t in range(4) for s in ("mul", "add", "stat")]
    silus = [f"silu{t}" for t in range(4)]
    act_names = ["T0", "T1"] + [f"hi q{f}" for f in range(4)] + silus + [f"hi k{f}" for f in range(4)]
    act_names += ["sqrt", "v0", "v1", "v2", "v3", "silu y"]
    dve_names = [f"lo q{f}" for f in range(4)] + gathered + combined + MOMENTS
    dve_names += [f"lo k{f}" for f in range(4)] + ROOT + [f"z{t}" for t in range(4)] + ["y0", "y1"]
    with Ctx(nc, "p2") as c:
        rows = c.sb("rows", [P, 4, 2, D], F32)
        xs = [c.sb(f"xs{k}", [P, 4, D], F32) for k in range(2)]
        ss = [c.sb(f"ss{k}", [P, 4, D], F32) for k in range(2)]
        fg = c.sb("fg", [P, 4, D], F32)
        stats = c.sb("stats", [P, 4, 6], F32)
        mean, var, std, diff, rstd = (c.sb(n, [P, 4], F32) for n in ("mean", "var", "std", "diff", "rstd"))
        w = c.sb("w", [P, 3, NF, 2 * D], F32)
        bias = c.sb("bias", [P, D], F32)
        z = [c.sb(f"z{k}", [P, 4, D], F32) for k in range(2)]
        xT = c.sb("xT", [P, NF, QB], F32)
        parts = c.sb("parts", [P, 2, 2, 4, QB], F16)
        vt = c.sb("vt", [P, 4, 2 * D], F32)
        yt = c.sb("yt", [P, 4, D], F32)
        got = [c.sem(f"got{t}") for t in range(4)]
        ld = [c.sem(f"ld{k}") for k in range(2)]
        w_ld, part_out, vt_out = c.sem("w_ld"), c.sem("part_out"), c.sem("vt_out")
        held, held_dve = c.sem("held"), c.sem("held_dve")
        pe_s = Steps(c.sem("pe"), [j[0] for j in jobs])
        act_s = Steps(c.sem("act"), act_names)
        dve_s = Steps(c.sem("dve"), dve_names)
        banks = Banks(c, jobs, {"act": act_s, "dve": dve_s})
        block = c.block()


        @block.sync
        def _(sp):
            def load(nxt, slot):
                if not isinstance(nxt, int) or nxt:
                    dve_s.wait(sp, "add3", nxt - 3)
                sp.dma_start(xs[slot][:, :, :], x.rearrange("b (n p) d -> p (b n) d", p=P)[
                    :, bass.ds(nxt * 4, 4), :]).then_inc(ld[slot], 16)
                sp.dma_start(ss[slot][:, :, :], s_out[bass.ds(nxt * 4, 4), :, :].rearrange("t p d -> p t d")
                             ).then_inc(ld[slot], 16)

            load(0, 0)
            for n, name in enumerate(("Wq", "Wk", "Wv")):
                sp.dma_start(w[:, n], W[name].rearrange("(c p) n -> p c n", p=P)).then_inc(w_ld, 16)
            sp.dma_start(bias[:, :], W["bias"].unsqueeze(0).to_broadcast([P, D])).then_inc(w_ld, 16)

            def body(blk, k, i, last):
                if not last:
                    load(blk + 1, 1 - k)
                b, j = i // 2, (i % 2) * 2 + k
                dve_s.wait(sp, "lo k3", blk)
                for side in range(2):
                    for lower in range(2):
                        dst = qk_out[side][lower].rearrange("(b g) h d t -> b g (h d) t", b=B)
                        sp.dma_start(dst[b, :, :, bass.ds(j * QB, QB)].rearrange("g p t -> p g t"),
                                     parts[:, side, lower, :, :]).then_inc(part_out, 16)
                act_s.wait(sp, "v3", blk)
                for g in range(4):
                    sp.dma_start(v_out[b, g, :, bass.ds(j * 4, 4), :],
                                 vt[:, :, g * P:(g + 1) * P]).then_inc(vt_out, 16)
            blocks_ahead(sp, body)
            sp.wait_ge(part_out, 1 + 64 * NB)
            sp.wait_ge(vt_out, 1 + 64 * NB)

        @block.gpsimd
        def _(pool):
            for n in range(NT):
                t = n % 4
                if n >= 4:
                    dve_s.wait(pool, f"two{t}", n // 4 - 2)
                for r in range(2):
                    pool.indirect_dma_start(
                        out=rows[:, t, r, :], out_offset=None, in_=exp_out[:, :],
                        in_offset=bass.IndirectOffsetOnAxis(ap=gather_at[:, r, n:n + 1], axis=0)
                    ).then_inc(got[t], 16)

        @block.scalar
        def _(act):
            act.nop().then_inc(vt_out, 1)
            act.nop().then_inc(part_out, 1)

            def silu(t, blk):
                dve_s.wait(act, f"two{t}", blk)
                act_s.step(f"silu{t}", act.activation(fg[:, t, :], fg[:, t, :], ACT.Silu))

            def sqrt(blk):
                dve_s.wait(act, MOMENTS[-1], blk)
                act_s.step("sqrt", act.activation(std[:, :], var[:, :], ACT.Sqrt))

            def body(blk, k, i, last):
                for f in range(NF):
                    pe_s.wait(act, f"T{f}", blk)
                    act_s.step(f"T{f}", act.activation(xT[:, f, :], banks.bank(f"T{f}")[:, :], ACT.Copy))
                act.wait_ge(part_out, blk * 64 + 1)
                for side, s in enumerate("qk"):
                    if s == "k" and last:
                        act_s.skip(act, silus, blk)
                    elif s == "k":
                        for t in range(4):
                            silu(t, blk)
                    for f in range(4):
                        pe_s.wait(act, f"{s}{f}", blk)
                        act_s.step(f"hi {s}{f}", act.activation(
                            parts[:, side, 0, f, :], banks.bank(f"{s}{f}")[:, :], ACT.Copy,
                            scale=scale_qk[side]))
                if last:
                    act_s.skip(act, ["sqrt"], blk)
                else:
                    sqrt(blk)
                act.wait_ge(vt_out, blk * 64 + 1)
                for t in range(4):
                    pe_s.wait(act, f"v{t}", blk)
                    act_s.step(f"v{t}", act.activation(vt[:, t, :], banks.bank(f"v{t}")[:, :], ACT.Copy))
                dve_s.wait(act, "y1", blk)
                act.nop().then_inc(held, 1)
                act_s.step("silu y", act.activation(g_all[:, bass.ds(blk * 4, 4), :], yt[:, :, :], ACT.Silu))

            act_s.start(act, 1)
            act_s.skip(act, act_names[:6], -1)
            for t in range(4):
                silu(t, -1)
            act_s.skip(act, [f"hi k{f}" for f in range(4)], -1)
            sqrt(-1)
            act_s.skip(act, act_names[15:], -1)
            blocks_ahead(act, body)

        @block.vector
        def _(dve):
            flat = lambda n: x_all[:, bass.ds(n, 1), :].rearrange("p a d -> p (a d)")

            def gather(blk):
                for t in range(4):
                    n = (blk + 1) * 4 + t
                    dve.wait_ge(got[t], (blk + 1) * 32 + 32)
                    dve_s.step(f"one{t}", dve.scalar_tensor_tensor(
                        out=fg[:, t, :], in0=rows[:, t, 0, :],
                        scalar=gate[:, 0, bass.ds(n, 1)], in1=flat(n), op0=ALU.mult, op1=ALU.add))
                    dve_s.wait(dve, f"one{t}", blk)
                    dve_s.step(f"two{t}", dve.scalar_tensor_tensor(
                        out=fg[:, t, :], in0=rows[:, t, 1, :],
                        scalar=gate[:, 1, bass.ds(n, 1)], in1=fg[:, t, :], op0=ALU.mult, op1=ALU.add))

            def combine(blk, slot, turn):
                dve.wait_ge(ld[slot], turn * 32 + 32)
                for t in range(4):
                    x2 = flat((blk + 1) * 4 + t)
                    act_s.wait(dve, f"silu{t}", blk)
                    dve_s.step(f"mul{t}", dve.tensor_tensor(fg[:, t, :], fg[:, t, :], ss[slot][:, t, :],
                                                            ALU.mult))
                    dve_s.wait(dve, f"mul{t}", blk)
                    dve_s.step(f"add{t}", dve.tensor_tensor(x2, fg[:, t, :], xs[slot][:, t, :], ALU.add))
                    dve_s.wait(dve, f"add{t}", blk)
                    dve.nop().then_inc(held_dve, 1)
                    dve_s.step(f"stat{t}", dve.bn_stats(stats[:, t, :], x2))
                dve_s.wait(dve, "stat3", blk)
                linked(MOMENTS, blk, lambda link: moments(dve, link, stats, mean[:, :], var[:, :], diff[:, :]))

            def linked(names, blk, work):
                names = iter(names)

                def link(ins):
                    name = next(names)
                    dve_s.step(name, ins)
                    dve_s.wait(dve, name, blk)
                work(link)

            def normalise(blk, slot):
                act_s.wait(dve, "sqrt", blk)
                linked(ROOT, blk, lambda link: inverse_root(dve, link, std[:, :], var[:, :], rstd[:, :]))
                for t in range(4):
                    dve_s.step(f"z{t}", dve.tensor_scalar(
                        z[slot][:, t, :], flat((blk + 1) * 4 + t), mean[:, t:t + 1], rstd[:, t:t + 1],
                        ALU.subtract, ALU.mult))

            dve_s.start(dve, 1)
            dve_s.skip(dve, [f"lo q{f}" for f in range(4)], -1)
            gather(-1)
            combine(-1, 0, 0)
            dve_s.skip(dve, [f"lo k{f}" for f in range(4)], -1)
            normalise(-1, 0)
            dve_s.skip(dve, ["y0", "y1"], -1)
            dve.wait_ge(w_ld, 64)

            def body(blk, k, i, last):
                def lower(side, s):
                    for f in range(4):
                        act_s.wait(dve, f"hi {s}{f}", blk)
                        dve_s.step(f"lo {s}{f}", dve.scalar_tensor_tensor(
                            out=parts[:, side, 1, f, :], in0=banks.bank(f"{s}{f}")[:, :],
                            scalar=scale_qk[side], in1=parts[:, side, 0, f, :], op0=ALU.mult,
                            op1=ALU.subtract))
                lower(0, "q")
                if last:
                    dve_s.skip(dve, gathered + combined + MOMENTS, blk)
                else:
                    gather(blk)
                    combine(blk, 1 - k, i + k)
                lower(1, "k")
                if last:
                    dve_s.skip(dve, ROOT + [f"z{t}" for t in range(4)], blk)
                else:
                    normalise(blk, 1 - k)
                act_s.wait(dve, "silu y", blk - 1)
                for m in range(2):
                    pe_s.wait(dve, f"y{m}", blk)
                    dve_s.step(f"y{m}", dve.tensor_tensor(
                        yt[:, 2 * m:2 * m + 2, :], banks.bank(f"y{m}")[:, :].rearrange("p (t d) -> p t d", t=2),
                        bias[:, :].unsqueeze(1).to_broadcast([P, 2, D]), ALU.add))
            blocks_ahead(dve, body)

        @block.tensor
        def _(pe):
            pe_s.start(pe)
            pe.wait_ge(w_ld, 64)

            def body(blk, k, i, last):
                for f in range(NF):
                    d = banks.take(pe, f"T{f}", blk, ("dve", "z3", 1))
                    for t in range(4):
                        mm = pe.transpose(d[:, t * P:(t + 1) * P], z[k][:, t, f * P:(f + 1) * P],
                                          C["identf"][:, :])
                    pe_s.step(f"T{f}", mm)
                for side, s in enumerate("qk"):
                    for f in range(4):
                        d = banks.take(pe, f"{s}{f}", blk, ("act", "T1", 0))
                        for n in range(NF):
                            mm = pe.matmul(d[:, :], w[:, side, n, f * P:(f + 1) * P], xT[:, n, :],
                                           start=n == 0, stop=n == NF - 1)
                        pe_s.step(f"{s}{f}", mm)
                for t in range(4):
                    d = banks.take(pe, f"v{t}", blk)
                    for n in range(NF):
                        mm = pe.matmul(d[:, :], xT[:, n, t * P:(t + 1) * P], w[:, 2, n, :],
                                       start=n == 0, stop=n == NF - 1)
                    pe_s.step(f"v{t}", mm)
                for m in range(2):
                    d = banks.take(pe, f"y{m}", blk)
                    for t in range(2):
                        for n in range(NF):
                            mm = pe.matmul(d[:, t * D:(t + 1) * D],
                                           xT[:, n, (2 * m + t) * P:(2 * m + t + 1) * P],
                                           C["w_ffn"][:, n, :], start=n == 0, stop=n == NF - 1)
                    pe_s.step(f"y{m}", mm)
            blocks_ahead(pe, body)


def finish(nc, W, att, sums, inverse, x_all, g_all, out):
    jobs = [(f"x{t}", "dve", f"mul{t}") for t in range(4)]
    dve_names = [f"{s}{t}" for t in range(4) for s in ("mul", "add")]
    with Ctx(nc, "fi") as c:
        w = c.sb("w", [P, 4, D], F32)
        o = [c.sb(f"o{k}", [P, 4, D], F32) for k in range(2)]
        w_ld = c.sem("w_ld")
        stored = [c.sem(f"stored{k}") for k in range(2)]
        pe_s = Steps(c.sem("pe"), [j[0] for j in jobs], credit=NB // B)
        dve_s = Steps(c.sem("dve"), dve_names)
        banks = Banks(c, jobs, {"dve": dve_s}, ring=4)
        attended = Attended(c, att, sums, inverse, 32, pe_s, "x3")
        block = c.block()

        @block.sync
        def _(sp):
            sp.dma_start(w[:, :, :], W["Wo"].rearrange("(g p) n -> p g n", p=P)).then_inc(w_ld, 16)

            attended.load(sp)

        @block.gpsimd
        def _(pool):
            attended.divide(pool)

        @block.scalar
        def _(act):
            def body(blk, k, i):
                dve_s.wait(act, "add3", blk)
                act.dma_start(out.rearrange("b (n p) d -> p (b n) d", p=P)[:, bass.ds(blk * 4, 4), :],
                              o[k][:, :, :]).then_inc(stored[k], 16)
            blocks(act, body)
            for k in range(2):
                act.wait_ge(stored[k], 1 + 16 * NB // 2)

        @block.vector
        def _(dve):
            attended.invert(dve)
            dve_s.start(dve)
            for k in range(2):
                dve.nop().then_inc(stored[k], 1)

            def body(blk, k, i):
                dve.wait_ge(stored[k], i * 16 + 1)
                for t in range(4):
                    n = bass.ds(blk * 4 + t, 1)
                    flat = lambda a: a.rearrange("p a d -> p (a d)")
                    pe_s.wait(dve, f"x{t}", blk)
                    dve_s.step(f"mul{t}", dve.tensor_tensor(o[k][:, t, :], flat(g_all[:, n, :]),
                                                            banks.bank(f"x{t}")[:, 0:D], ALU.mult))
                    dve_s.wait(dve, f"mul{t}", blk)
                    dve_s.step(f"add{t}", dve.tensor_tensor(o[k][:, t, :], o[k][:, t, :],
                                                            flat(x_all[:, n, :]), ALU.add))
            blocks(dve, body)

        @block.tensor
        def _(pe):
            pe_s.start(pe)
            pe.wait_ge(w_ld, 16)

            def body(blk, k, i):
                attended.wait(pe, blk)
                for t in range(4):
                    d = banks.take(pe, f"x{t}", blk)
                    for g in range(4):
                        mm = pe.matmul(d[:, 0:D], attended.a[k][:, g, t * P:(t + 1) * P], w[:, g, :],
                                       start=g == 0, stop=g == 3)
                    pe_s.step(f"x{t}", mm)
            blocks(pe, body, NB // B)


def build(nc, W, x, out):
    dram = lambda name, shape, dt: nc.dram_tensor(name, shape, dt, kind="Internal").ap()
    exp_in = dram("exp_in", [E * CAP, D], F32)
    exp_out = dram("exp_out", [E * CAP, D], F32)
    s_out = dram("s_out", [NT, P, D], F32)
    att = [dram(f"att{n}", [GROUPS, P, T], F32) for n in range(2)]
    sums = [att[0].rearrange("g (h r) t -> g h r t", r=32)[:, :, 16, :], dram("sums1", [GROUPS, HG, T], F32)]
    all_sums = [a.rearrange("g h t -> (g h) t") for a in sums]
    inverse = [dram(f"inverse{n}", [GROUPS * HG, T], F32) for n in range(2)]
    v = [dram(f"v{n}", [B, 4, P, NKC, P], F32) for n in range(2)]
    qk = [[[dram(f"{s}{part}{n}", [GROUPS, HG, hd, T], F16) for part in ("hi", "lo")] for s in "qk"]
          for n, hd in ((0, 16), (1, 32))]

    def attention(c, n, hd, scores):
        softmax_attention(nc, f"at{n}", hd, c, *qk[n][0], *qk[n][1], v[n].rearrange("b g p c n -> (b g) p c n"),
                          scores[n][:, 2:3], att[n], sums[n])

    with Ctx(nc, "all") as c:
        C = constants(nc, c, W["shift_rows"])
        x_all = c.sb("x_all", [P, NT, D], F32)
        score = [c.sb(f"score{n}", [P, 3], F32) for n in range(2)]
        mean = c.sb("mean", [P, NT], F32)
        rstd = c.sb("rstd", [P, NT], F32)
        stats = c.sb("stats", [P, NT, 6], F32)
        gate = c.sb("gate", [P, 2, NT], F32)
        gather_at = c.sb("gather_at", [P, 2, NT], U32)
        zeros = c.sb("zeros", [P, D], F32)
        zero_fill = c.sem("zero_fill")
        scales = lambda n: [score[n][:, 0:1], score[n][:, 1:2]]

        with Ctx(nc, "lin") as lin:
            qf_all = lin.sb("qf_all", [P, NF, B * T], F32)
            kv_sum = lin.sb("kv_sum", [P, B * NF, P + 8], F32)
            with Ctx(nc, "first") as first:
                F, load_next = first_operands(nc, first, x, W, x_all)
                prepare(nc, C, W, score, zeros, exp_in, zero_fill, load_next)
                project_first(nc, C, F, x_all, qf_all, kv_sum, scales(0), qk[0], v[0])
            attention(C, 0, 16, score)
            after_attention(nc, W, att[0], all_sums[0], inverse[0], x_all, stats)
            row_statistics(nc, "rs1", stats, mean, rstd)
            z_all = lin.sb("z_all", [P, NT, D], F32)
            logits = lin.sb("logits", [P, NT, E], F32)
            scatter_at = lin.sb("scatter_at", [P, 2, NT], U32)
            sent = lin.sem("sent")
            gate_logits(nc, C, W, x_all, mean, rstd, z_all, logits)
            route(nc, C, W, logits, scatter_at, gather_at, gate)
            X, load_weights = expert_operands(lin, W)
            linear_out(nc, C, W, qf_all, kv_sum, s_out,
                       lambda pool: scatter_rows(pool, z_all, scatter_at, exp_in, zero_fill, sent),
                       lambda sp: [load_weights(sp, e, e) for e in range(2)])
            experts(nc, C, W, X, load_weights, exp_in, exp_out, qf_all)
        with Ctx(nc, "g") as last:
            g_all = last.sb("g_all", [P, NT, D], F32)
            combine_and_project(nc, C, W, x, s_out, exp_out, gather_at, gate, x_all, scales(1),
                                qk[1], v[1], g_all)
            attention(C, 1, 32, score)
            finish(nc, W, att[1], all_sums[1], inverse[1], x_all, g_all, out)


_NAMES = {"L0_attn_x": "x", "L0_attn_W_qkv": "W_qkv", "L0_attn_W_out": "W_out", "L0_ffn_ln1_g": "ln1_g",
          "L0_ffn_ln1_b": "ln1_b", "L0_ffn_Wqkv": "ffn_Wqkv", "L0_ffn_Wproj": "Wproj",
          "L0_ffn_ln2_g": "ln2_g", "L0_ffn_ln2_b": "ln2_b", "L0_ffn_Wgate": "Wgate", "L0_ffn_W1": "W1",
          "L0_ffn_b1": "b1", "L0_ffn_W2": "W2", "L0_ffn_b2": "b2", "L1_attn_Wq": "Wq",
          "L1_attn_Wk": "Wk", "L1_attn_Wv": "Wv", "L1_attn_Wo": "Wo", "L1_ffn_kernel": "kernel",
          "L1_ffn_bias": "bias", "L1_ffn_a": "a", "L1_ffn_b": "b"}


def tables():
    import numpy as np
    t = np.arange(2048, dtype=np.float32)
    power = np.arange(0, 16, 2, dtype=np.float32) / np.float32(16)
    ang = {b: (t[:, None] * (np.float32(1) / np.float32(b) ** power)[None, :]).astype(np.float32)
           for b in (500000.0, 10000.0)}
    rows = lambda a: np.ascontiguousarray(np.tile(a, (1, 16)).T).astype(np.float32)
    tiles = lambda a: np.ascontiguousarray(a.reshape(16, 128, 8).transpose(1, 0, 2))
    rotate = np.zeros((128, 128), np.float32)
    for m in range(128):
        rotate[m + 8 if m % 16 < 8 else m - 8, m] = -1.0 if m % 16 < 8 else 1.0
    lin, soft = ang[500000.0], ang[10000.0]
    heads = np.zeros((128, 136), np.float32)
    for r in range(128):
        heads[r, r // 16 * 16:r // 16 * 16 + 16] = 1.0
        heads[r, 128 + r // 16] = 1.0
    iota8 = np.tile(np.stack([8 - np.arange(8), np.arange(8)]).astype(np.float32)[None], (128, 1, 1))
    shift_rows = np.zeros((2 * HG, HG, T), np.float16)
    for h in range(HG):
        shift_rows[2 * h:2 * h + 2, h] = MSHIFT
    return {"heads": heads, "iota8": iota8, "shift_rows": shift_rows,
            "cos_q": rows(np.cos(lin)) * np.float32(0.25), "sin_q": rows(np.sin(lin)) * np.float32(0.25),
            "cos_f": rows(np.cos(soft)), "sin_f": rows(np.sin(soft)),
            "cos_k": tiles(np.cos(lin)), "sin_k": tiles(np.sin(lin)), "rotate": rotate}


def kernel(**inputs):
    import numpy as _np
    import concourse.bacc as _bacc
    from concourse.bass_utils import run_bass_kernel_spmd as _run

    nc = _bacc.Bacc("TRN2", target_bir_lowering=False, num_devices=1)
    given = {short: _np.ascontiguousarray(inputs[name]) for name, short in _NAMES.items()}
    given.update({name: _np.ascontiguousarray(a) for name, a in tables().items()})
    arrays, W = {}, {}
    for name, a in given.items():
        arrays[f"in_{name}"] = a
        W[name] = nc.dram_tensor(f"in_{name}", a.shape, mybir.dt.from_np(a.dtype), kind="ExternalInput").ap()
    out = nc.dram_tensor("out_0", (B, T, D), F32, kind="ExternalOutput").ap()
    build(nc, W, W["x"], out)
    r = _run(nc, [arrays], core_ids=[0])
    return r.results[0]["out_0"]
```
